# Optimizing a Trainium2 kernel written in Bass

```python
import numpy as np
import jax
import jax.numpy as jnp

def _softmax(x, axis=-1):
    return jax.nn.softmax(x, axis=axis)

def _gelu(x):
    return jax.nn.gelu(x, approximate=True)

def _silu(x):
    return jax.nn.silu(x)

def _sigmoid(x):
    return jax.nn.sigmoid(x)

def _layernorm(x, axis=-1, eps=1e-05):
    m = jnp.mean(x, axis=axis, keepdims=True)
    v = jnp.var(x, axis=axis, keepdims=True)
    return (x - m) / jnp.sqrt(v + eps)

def _scatter_add(tgt, idx, src, axis=0):
    return tgt.at[idx].add(src)

def _segment_sum(src, seg, n):
    return jax.ops.segment_sum(src, seg, n)
kernel_name = 'mk_perceiver_d2_seqx_r4_c86b9d'

def setup_inputs(seed: int=0):
    np.random.seed(seed)
    _w = jnp.asarray

    def _rec_inputs():
        import jax
        import jax.numpy as jnp
        _rk = jax.random.key(seed)
        x = 7.22e-05 + 1 * jax.random.normal(jax.random.fold_in(_rk, 1), (32, 64, 256), jnp.float32)
        _lenS = 64 - jax.random.randint(jax.random.fold_in(_rk, 7), (32,), 0, max(1, 64 // 4) + 1, jnp.int32)
        _lenS2 = 256 - jax.random.randint(jax.random.fold_in(_rk, 8), (32,), 0, max(1, 256 // 4) + 1, jnp.int32)
        _ctx_768P = jax.random.normal(jax.random.fold_in(_rk, 11), (32, 16, 192), jnp.float32)
        _ctx_768c = jax.random.dirichlet(jax.random.fold_in(_rk, 511), 0.3 * jnp.ones((16,), jnp.float32), (32, 256))
        _ctx_768t = jnp.einsum('bsk,bkd->bsd', _ctx_768c, _ctx_768P)
        _ctx_768t = _ctx_768t * jax.lax.rsqrt(jnp.mean(jnp.square(_ctx_768t)) + 1e-12) * 0.953939
        ctx_768 = -0.000191848 + 0.999787 * (_ctx_768t + 0.3 * jax.random.normal(jax.random.fold_in(_rk, 611), (32, 256, 192), jnp.float32))
        _validS = jnp.arange(64)[None, :] < _lenS[:, None]
        _validS2 = jnp.arange(256)[None, :] < _lenS2[:, None]
        _causal = jnp.tril(jnp.ones((64, 64), dtype=bool))
        mask_BxS2_bk0 = jnp.logical_not(jnp.broadcast_to(_validS2[:, :], (32, 256)))
        return (x, ctx_768, mask_BxS2_bk0)
    x, ctx_768, mask_BxS2_bk0 = _rec_inputs()

    def _L0_xattn_setup():
        import jax, jax.numpy as jnp
        import numpy as np
        HEADS = 8
        DIM_HEAD = 64
        QUERY_DIM = 256
        CONTEXT_DIM = 192
        INNER = HEADS * DIM_HEAD
        key = jax.random.key(seed)
        ks = jax.random.split(key, 8)
        b, n, j = (4, 512, 512)
        x = jax.random.normal(ks[0], (b, n, QUERY_DIM), dtype=jnp.float32)
        context = jax.random.normal(ks[1], (b, j, CONTEXT_DIM), dtype=jnp.float32)
        mask = jax.random.randint(ks[2], (b, j), 0, 2).astype(jnp.bool_)
        W_q = jax.random.normal(ks[3], (QUERY_DIM, INNER), dtype=jnp.float32) / np.sqrt(QUERY_DIM)
        W_k = jax.random.normal(ks[4], (CONTEXT_DIM, INNER), dtype=jnp.float32) / np.sqrt(CONTEXT_DIM)
        W_v = jax.random.normal(ks[5], (CONTEXT_DIM, INNER), dtype=jnp.float32) / np.sqrt(CONTEXT_DIM)
        W_o = jax.random.normal(ks[6], (INNER, QUERY_DIM), dtype=jnp.float32) / np.sqrt(INNER)
        b_o = jax.random.normal(ks[7], (QUERY_DIM,), dtype=jnp.float32) * 0.01
        return {'x': x, 'context': context, 'mask': mask, 'W_q': W_q, 'W_k': W_k, 'W_v': W_v, 'W_o': W_o, 'b_o': b_o}
    _L0_xattn_all = _L0_xattn_setup()
    _L0_xattn_in = {k: v for k, v in _L0_xattn_all.items() if k in ('W_q', 'W_k', 'W_v', 'W_o', 'b_o')}
    del _L0_xattn_all

    def _L0_attn_setup():
        import jax, jax.numpy as jnp
        import numpy as np
        DIM = 256
        NH = 16
        HD = DIM // NH
        DROPE = 16
        MAXSEQ = 512
        LAT = 64
        BATCH = 2
        SEQ = 512

        def _rope_freqs(max_seq, head_dim):
            inv = 1.0 / 10000.0 ** (jnp.arange(0, head_dim, 2, dtype=jnp.float32) / head_dim)
            ang = jnp.arange(max_seq, dtype=jnp.float32)[:, None] * inv[None, :]
            return (jnp.cos(ang), jnp.sin(ang))

        def _apply_decoupled_rope(x, cosf, sinf, d_rope):
            b, d1, d2, hd = x.shape
            half = d_rope // 2
            xr = x[..., :d_rope].astype(jnp.float32).reshape(b, d1, d2, half, 2)
            xa, xb = (xr[..., 0], xr[..., 1])
            c = cosf[:d1, :half][None, :, None, :]
            s = sinf[:d1, :half][None, :, None, :]
            rot = jnp.stack([xa * c - xb * s, xa * s + xb * c], axis=-1)
            rot = rot.reshape(b, d1, d2, d_rope)
            return jnp.concatenate([rot, x[..., d_rope:]], axis=-1)
        key = jax.random.key(seed)
        ks = jax.random.split(key, 8)

        def w(k, o, i):
            return jax.random.normal(k, (o, i), jnp.float32) / np.sqrt(i).astype(np.float32)
        return {'x': jax.random.normal(ks[0], (BATCH, SEQ, DIM), jnp.float32), 'wq': w(ks[1], NH * HD, DIM), 'wk_a': w(ks[2], LAT, DIM), 'wk_b': w(ks[3], NH * HD, LAT), 'wv_a': w(ks[4], LAT, DIM), 'wv_b': w(ks[5], NH * HD, LAT), 'wo': w(ks[6], DIM, NH * HD)}
    _L0_attn_all = _L0_attn_setup()
    _L0_attn_in = {k: v for k, v in _L0_attn_all.items() if k in ('wq', 'wk_a', 'wk_b', 'wv_a', 'wv_b', 'wo')}
    del _L0_attn_all

    def _L0_ffn_setup():
        import jax, jax.numpy as jnp
        import numpy as np
        LN_EPS = 0.001
        EPS = 1e-05
        QB = 128.0

        def ste_round(x):
            return x + jax.lax.stop_gradient(jnp.round(x) - x)
        key = jax.random.key(seed)
        k1, k2 = jax.random.split(key)
        x = jax.random.normal(k1, (4, 2048, 256), dtype=jnp.float32)
        weight = jax.random.normal(k2, (256, 256), dtype=jnp.float32) * 0.02
        ln_gamma = jnp.ones((256,), dtype=jnp.float32)
        ln_beta = jnp.zeros((256,), dtype=jnp.float32)
        return {'x': x, 'weight': weight, 'ln_gamma': ln_gamma, 'ln_beta': ln_beta}
    _L0_ffn_all = _L0_ffn_setup()
    _L0_ffn_in = {k: v for k, v in _L0_ffn_all.items() if k in ('weight', 'ln_gamma', 'ln_beta')}
    del _L0_ffn_all

    def _L1_xattn_setup():
        import jax, jax.numpy as jnp
        import numpy as np
        IN_DIM = 256
        CTX_DIM = 192
        NUM_HEADS = 16
        HEAD_DIM = IN_DIM // NUM_HEADS
        SCALE = 1.0 / float(np.sqrt(HEAD_DIM))
        key = jax.random.key(seed)
        ks = jax.random.split(key, 10)
        B, NQ, NKV = (8, 256, 128)
        s_in = 1.0 / float(np.sqrt(IN_DIM))
        s_ctx = 1.0 / float(np.sqrt(CTX_DIM))
        return {'x': jax.random.normal(ks[0], (B, NQ, IN_DIM), dtype=jnp.float32), 'context': jax.random.normal(ks[1], (B, NKV, CTX_DIM), dtype=jnp.float32), 'Wq': jax.random.normal(ks[2], (IN_DIM, IN_DIM), dtype=jnp.float32) * s_in, 'bq': jax.random.normal(ks[3], (IN_DIM,), dtype=jnp.float32) * 0.01, 'Wk': jax.random.normal(ks[4], (IN_DIM, CTX_DIM), dtype=jnp.float32) * s_ctx, 'bk': jax.random.normal(ks[5], (IN_DIM,), dtype=jnp.float32) * 0.01, 'Wv': jax.random.normal(ks[6], (IN_DIM, CTX_DIM), dtype=jnp.float32) * s_ctx, 'bv': jax.random.normal(ks[7], (IN_DIM,), dtype=jnp.float32) * 0.01, 'Wo': jax.random.normal(ks[8], (IN_DIM, IN_DIM), dtype=jnp.float32) * s_in, 'bo': jax.random.normal(ks[9], (IN_DIM,), dtype=jnp.float32) * 0.01}
    _L1_xattn_all = _L1_xattn_setup()
    _L1_xattn_in = {k: v for k, v in _L1_xattn_all.items() if k in ('Wq', 'bq', 'Wk', 'bk', 'Wv', 'bv', 'Wo', 'bo')}
    del _L1_xattn_all

    def _L1_attn_setup():
        import jax, jax.numpy as jnp
        import numpy as np
        DIM = 256
        QK = 128
        HID = 512
        B, N = (4, 512)
        EPS = 1e-05
        key = jax.random.key(seed)
        ks = jax.random.split(key, 8)
        std = 0.02
        return {'x': jax.random.normal(ks[0], (B, N, DIM), jnp.float32), 'ln_scale': jnp.ones((DIM,), jnp.float32), 'ln_bias': jnp.zeros((DIM,), jnp.float32), 'W_hidden': jax.random.normal(ks[1], (DIM, 2 * HID), jnp.float32) * std, 'b_hidden': jnp.zeros((2 * HID,), jnp.float32), 'W_qk': jax.random.normal(ks[2], (DIM, QK), jnp.float32) * std, 'b_qk': jnp.zeros((QK,), jnp.float32), 'os_weight': jax.random.normal(ks[3], (2, QK), jnp.float32) * std, 'os_bias': jnp.zeros((2, QK), jnp.float32), 'W_out': jax.random.normal(ks[4], (HID, DIM), jnp.float32) * std, 'b_out': jnp.zeros((DIM,), jnp.float32)}
    _L1_attn_all = _L1_attn_setup()
    _L1_attn_in = {k: v for k, v in _L1_attn_all.items() if k in ('ln_scale', 'ln_bias', 'W_hidden', 'b_hidden', 'W_qk', 'b_qk', 'os_weight', 'os_bias', 'W_out', 'b_out')}
    del _L1_attn_all

    def _L1_ffn_setup():
        import jax, jax.numpy as jnp
        import numpy as np
        NUM_EXPERTS = 160
        TOP_K = 8
        ROUTED_SCALE = 2.5
        HIDDEN = 256
        INTER = 128
        key = jax.random.key(seed)
        ks = jax.random.split(key, 7)
        B, S = (1, 512)
        return {'hidden_states': jax.random.normal(ks[0], (B, S, HIDDEN), dtype=jnp.float32), 'router_w': jax.random.normal(ks[1], (NUM_EXPERTS, HIDDEN), dtype=jnp.float32) * 0.02, 'expert_bias': jnp.zeros((NUM_EXPERTS,), dtype=jnp.float32), 'w_gate': jax.random.normal(ks[2], (NUM_EXPERTS, INTER, HIDDEN), dtype=jnp.float32) * 0.02, 'w_down': jax.random.normal(ks[3], (NUM_EXPERTS, HIDDEN, INTER), dtype=jnp.float32) * 0.02, 'w_gate_shared': jax.random.normal(ks[4], (INTER, HIDDEN), dtype=jnp.float32) * 0.02, 'w_down_shared': jax.random.normal(ks[5], (HIDDEN, INTER), dtype=jnp.float32) * 0.02}
    _L1_ffn_all = _L1_ffn_setup()
    _L1_ffn_in = {k: v for k, v in _L1_ffn_all.items() if k in ('router_w', 'expert_bias', 'w_gate', 'w_down', 'w_gate_shared', 'w_down_shared')}
    del _L1_ffn_all
    return {'x': x, 'ctx_768': ctx_768, 'mask_BxS2_bk0': mask_BxS2_bk0, 'L0_xattn_W_q': _L0_xattn_in['W_q'], 'L0_xattn_W_k': _L0_xattn_in['W_k'], 'L0_xattn_W_v': _L0_xattn_in['W_v'], 'L0_xattn_W_o': _L0_xattn_in['W_o'], 'L0_xattn_b_o': _L0_xattn_in['b_o'], 'L0_attn_wq': _L0_attn_in['wq'], 'L0_attn_wk_a': _L0_attn_in['wk_a'], 'L0_attn_wk_b': _L0_attn_in['wk_b'], 'L0_attn_wv_a': _L0_attn_in['wv_a'], 'L0_attn_wv_b': _L0_attn_in['wv_b'], 'L0_attn_wo': _L0_attn_in['wo'], 'L0_ffn_weight': _L0_ffn_in['weight'], 'L0_ffn_ln_gamma': _L0_ffn_in['ln_gamma'], 'L0_ffn_ln_beta': _L0_ffn_in['ln_beta'], 'L1_xattn_Wq': _L1_xattn_in['Wq'], 'L1_xattn_bq': _L1_xattn_in['bq'], 'L1_xattn_Wk': _L1_xattn_in['Wk'], 'L1_xattn_bk': _L1_xattn_in['bk'], 'L1_xattn_Wv': _L1_xattn_in['Wv'], 'L1_xattn_bv': _L1_xattn_in['bv'], 'L1_xattn_Wo': _L1_xattn_in['Wo'], 'L1_xattn_bo': _L1_xattn_in['bo'], 'L1_attn_ln_scale': _L1_attn_in['ln_scale'], 'L1_attn_ln_bias': _L1_attn_in['ln_bias'], 'L1_attn_W_hidden': _L1_attn_in['W_hidden'], 'L1_attn_b_hidden': _L1_attn_in['b_hidden'], 'L1_attn_W_qk': _L1_attn_in['W_qk'], 'L1_attn_b_qk': _L1_attn_in['b_qk'], 'L1_attn_os_weight': _L1_attn_in['os_weight'], 'L1_attn_os_bias': _L1_attn_in['os_bias'], 'L1_attn_W_out': _L1_attn_in['W_out'], 'L1_attn_b_out': _L1_attn_in['b_out'], 'L1_ffn_router_w': _L1_ffn_in['router_w'], 'L1_ffn_expert_bias': _L1_ffn_in['expert_bias'], 'L1_ffn_w_gate': _L1_ffn_in['w_gate'], 'L1_ffn_w_down': _L1_ffn_in['w_down'], 'L1_ffn_w_gate_shared': _L1_ffn_in['w_gate_shared'], 'L1_ffn_w_down_shared': _L1_ffn_in['w_down_shared']}

def reference(x, ctx_768, mask_BxS2_bk0, L0_xattn_W_q, L0_xattn_W_k, L0_xattn_W_v, L0_xattn_W_o, L0_xattn_b_o, L0_attn_wq, L0_attn_wk_a, L0_attn_wk_b, L0_attn_wv_a, L0_attn_wv_b, L0_attn_wo, L0_ffn_weight, L0_ffn_ln_gamma, L0_ffn_ln_beta, L1_xattn_Wq, L1_xattn_bq, L1_xattn_Wk, L1_xattn_bk, L1_xattn_Wv, L1_xattn_bv, L1_xattn_Wo, L1_xattn_bo, L1_attn_ln_scale, L1_attn_ln_bias, L1_attn_W_hidden, L1_attn_b_hidden, L1_attn_W_qk, L1_attn_b_qk, L1_attn_os_weight, L1_attn_os_bias, L1_attn_W_out, L1_attn_b_out, L1_ffn_router_w, L1_ffn_expert_bias, L1_ffn_w_gate, L1_ffn_w_down, L1_ffn_w_gate_shared, L1_ffn_w_down_shared):
    import jax
    import jax.numpy as jnp

    def _L0_xattn_ref(x, context, mask, W_q, W_k, W_v, W_o, b_o):
        import jax, jax.numpy as jnp
        import numpy as np
        HEADS = 8
        DIM_HEAD = 64
        QUERY_DIM = 256
        CONTEXT_DIM = 192
        INNER = HEADS * DIM_HEAD
        b, n, _ = x.shape
        j = context.shape[1]
        scale = DIM_HEAD ** (-0.5)
        q = (x @ W_q).reshape(b, n, HEADS, DIM_HEAD)
        k = (context @ W_k).reshape(b, j, HEADS, DIM_HEAD)
        v = (context @ W_v).reshape(b, j, HEADS, DIM_HEAD)
        sim = jnp.einsum('bihd,bjhd->bhij', q, k) * scale
        max_neg = -jnp.finfo(sim.dtype).max
        sim = jnp.where(mask[:, None, None, :], sim, max_neg)
        attn = jax.nn.softmax(sim, axis=-1)
        out = jnp.einsum('bhij,bjhd->bihd', attn, v).reshape(b, n, INNER)
        return out @ W_o + b_o

    def _L0_attn_ref(x, wq, wk_a, wk_b, wv_a, wv_b, wo):
        import jax, jax.numpy as jnp
        import numpy as np
        DIM = 256
        NH = 16
        HD = DIM // NH
        DROPE = 16
        MAXSEQ = 512
        LAT = 64
        BATCH = 2
        SEQ = 512

        def _rope_freqs(max_seq, head_dim):
            inv = 1.0 / 10000.0 ** (jnp.arange(0, head_dim, 2, dtype=jnp.float32) / head_dim)
            ang = jnp.arange(max_seq, dtype=jnp.float32)[:, None] * inv[None, :]
            return (jnp.cos(ang), jnp.sin(ang))

        def _apply_decoupled_rope(x, cosf, sinf, d_rope):
            b, d1, d2, hd = x.shape
            half = d_rope // 2
            xr = x[..., :d_rope].astype(jnp.float32).reshape(b, d1, d2, half, 2)
            xa, xb = (xr[..., 0], xr[..., 1])
            c = cosf[:d1, :half][None, :, None, :]
            s = sinf[:d1, :half][None, :, None, :]
            rot = jnp.stack([xa * c - xb * s, xa * s + xb * c], axis=-1)
            rot = rot.reshape(b, d1, d2, d_rope)
            return jnp.concatenate([rot, x[..., d_rope:]], axis=-1)
        b, s, _ = x.shape
        q = (x @ wq.T).reshape(b, s, NH, HD).transpose(0, 2, 1, 3)
        k = (x @ wk_a.T @ wk_b.T).reshape(b, s, NH, HD).transpose(0, 2, 1, 3)
        v = (x @ wv_a.T @ wv_b.T).reshape(b, s, NH, HD).transpose(0, 2, 1, 3)
        cosf, sinf = _rope_freqs(MAXSEQ, HD)
        q = _apply_decoupled_rope(q, cosf, sinf, DROPE)
        k = _apply_decoupled_rope(k, cosf, sinf, DROPE)
        scores = jnp.einsum('bhqd,bhkd->bhqk', q, k) / np.float32(np.sqrt(HD))
        attn = jax.nn.softmax(scores, axis=-1)
        out = jnp.einsum('bhqk,bhkd->bhqd', attn, v)
        out = out.transpose(0, 2, 1, 3).reshape(b, s, NH * HD)
        return out @ wo.T

    def _L0_ffn_ref(x, weight, ln_gamma, ln_beta):
        import jax, jax.numpy as jnp
        import numpy as np
        LN_EPS = 0.001
        EPS = 1e-05
        QB = 128.0

        def ste_round(x):
            return x + jax.lax.stop_gradient(jnp.round(x) - x)
        mu = jnp.mean(x, axis=-1, keepdims=True)
        var = jnp.var(x, axis=-1, keepdims=True)
        xn = (x - mu) * jax.lax.rsqrt(var + LN_EPS) * ln_gamma + ln_beta
        beta = jnp.mean(jnp.abs(weight))
        w_q = jnp.clip(ste_round(weight / (beta + EPS)), -1.0, 1.0)
        gamma = jnp.max(jnp.abs(xn))
        xq = jnp.clip(xn * QB / gamma, -QB + EPS, QB - EPS)
        y = jnp.einsum('bsd,du->bsu', xq, w_q)
        return y * (gamma * beta / QB)

    def _L1_xattn_ref(x, context, Wq, bq, Wk, bk, Wv, bv, Wo, bo):
        import jax, jax.numpy as jnp
        import numpy as np
        IN_DIM = 256
        CTX_DIM = 192
        NUM_HEADS = 16
        HEAD_DIM = IN_DIM // NUM_HEADS
        SCALE = 1.0 / float(np.sqrt(HEAD_DIM))
        q = x @ Wq.T + bq
        k = context @ Wk.T + bk
        v = context @ Wv.T + bv
        B, NQ, _ = q.shape
        NKV = k.shape[1]
        q = q.reshape(B, NQ, NUM_HEADS, HEAD_DIM)
        k = k.reshape(B, NKV, NUM_HEADS, HEAD_DIM)
        v = v.reshape(B, NKV, NUM_HEADS, HEAD_DIM)
        attn = jnp.einsum('bihd,bjhd->bhij', q, k) * SCALE
        attn = jax.nn.softmax(attn, axis=-1)
        out = jnp.einsum('bhij,bjhd->bihd', attn, v)
        out = out.reshape(B, NQ, IN_DIM)
        return out @ Wo.T + bo

    def _L1_attn_ref(x, ln_scale, ln_bias, W_hidden, b_hidden, W_qk, b_qk, os_weight, os_bias, W_out, b_out):
        import jax, jax.numpy as jnp
        import numpy as np
        DIM = 256
        QK = 128
        HID = 512
        B, N = (4, 512)
        EPS = 1e-05
        n = x.shape[1]
        mu = jnp.mean(x, axis=-1, keepdims=True)
        var = jnp.mean(jnp.square(x - mu), axis=-1, keepdims=True)
        xn = (x - mu) / jnp.sqrt(var + EPS) * ln_scale + ln_bias
        hid = jax.nn.silu(xn @ W_hidden + b_hidden)
        v, gate = (hid[..., :HID], hid[..., HID:])
        qk = jax.nn.silu(xn @ W_qk + b_qk)
        qk2 = qk[..., None, :] * os_weight + os_bias
        q, k = (qk2[..., 0, :], qk2[..., 1, :])
        sim = jnp.einsum('bid,bjd->bij', q, k) / n
        attn = jnp.square(jax.nn.relu(sim))
        out = jnp.einsum('bij,bjd->bid', attn, v)
        out = out * gate
        return out @ W_out + b_out

    def _L1_ffn_ref(hidden_states, router_w, expert_bias, w_gate, w_down, w_gate_shared, w_down_shared):
        import jax, jax.numpy as jnp
        import numpy as np
        NUM_EXPERTS = 160
        TOP_K = 8
        ROUTED_SCALE = 2.5
        HIDDEN = 256
        INTER = 128
        B, S, H = hidden_states.shape
        x = hidden_states.reshape(-1, H)
        T = x.shape[0]
        logits = x @ router_w.T + expert_bias[None, :]
        probs = jax.nn.sigmoid(logits)
        top_w, top_idx = jax.lax.top_k(probs, TOP_K)
        top_w = top_w / (jnp.sum(top_w, axis=-1, keepdims=True) + 1e-09)
        top_w = top_w * ROUTED_SCALE
        combine = jnp.zeros((T, NUM_EXPERTS), dtype=x.dtype)
        combine = combine.at[jnp.arange(T)[:, None], top_idx].set(top_w)
        h1 = jax.nn.silu(jnp.einsum('th,eih->eti', x, w_gate))
        h1w = h1 * combine.T[:, :, None]
        routed = jnp.einsum('eti,ehi->th', h1w, w_down)
        shared = jax.nn.silu(x @ w_gate_shared.T) @ w_down_shared.T
        return (routed + shared).reshape(B, S, H)
    x = x + _L0_xattn_ref(_layernorm(x, axis=-1), ctx_768, mask_BxS2_bk0, L0_xattn_W_q, L0_xattn_W_k, L0_xattn_W_v, L0_xattn_W_o, L0_xattn_b_o)
    x = x + _L0_attn_ref(_layernorm(x, axis=-1), L0_attn_wq, L0_attn_wk_a, L0_attn_wk_b, L0_attn_wv_a, L0_attn_wv_b, L0_attn_wo)
    x = x + _L0_ffn_ref(_layernorm(x, axis=-1), L0_ffn_weight, L0_ffn_ln_gamma, L0_ffn_ln_beta)
    x = x + _L1_xattn_ref(_layernorm(x, axis=-1), ctx_768, L1_xattn_Wq, L1_xattn_bq, L1_xattn_Wk, L1_xattn_bk, L1_xattn_Wv, L1_xattn_bv, L1_xattn_Wo, L1_xattn_bo)
    x = x + _L1_attn_ref(_layernorm(x, axis=-1), L1_attn_ln_scale, L1_attn_ln_bias, L1_attn_W_hidden, L1_attn_b_hidden, L1_attn_W_qk, L1_attn_b_qk, L1_attn_os_weight, L1_attn_os_bias, L1_attn_W_out, L1_attn_b_out)
    x = x + _L1_ffn_ref(_layernorm(x, axis=-1), L1_ffn_router_w, L1_ffn_expert_bias, L1_ffn_w_gate, L1_ffn_w_down, L1_ffn_w_gate_shared, L1_ffn_w_down_shared)
    return x

_drawn_inputs = setup_inputs


def setup_inputs(seed=0):
    import zlib

    import numpy as np

    out = dict(_drawn_inputs(seed))
    spreads = {'L0_ffn_ln_gamma': (1.0, 0.2),
     'L0_ffn_ln_beta': (0.0, 0.52),
     'L1_attn_ln_scale': (1.0, 0.6),
     'L1_attn_ln_bias': (0.0, 0.8),
     'L1_attn_b_hidden': (0.0, 0.8),
     'L1_attn_b_qk': (0.0, 0.8),
     'L1_attn_os_bias': (0.0, 0.8),
     'L1_attn_b_out': (0.0, 0.8),
     'L1_ffn_expert_bias': (0.0, 2.0)}
    factors = {'L0_xattn_b_o': 5.362,
     'L1_xattn_bq': 25.818,
     'L1_xattn_bk': 64.0,
     'L1_xattn_bv': 7.776,
     'L1_xattn_bo': 7.344,
     'L1_attn_W_hidden': 8.0,
     'L1_attn_W_qk': 8.0,
     'L1_attn_os_weight': 8.0,
     'L1_attn_W_out': 8.0,
     'L1_ffn_router_w': 8.0,
     'L1_ffn_w_gate': 8.0,
     'L1_ffn_w_down': 8.0,
     'L1_ffn_w_gate_shared': 8.0,
     'L1_ffn_w_down_shared': 8.0}
    for name, (base, spread) in spreads.items():
        noise = np.random.default_rng([zlib.crc32(name.encode()), seed]).standard_normal(out[name].shape)
        drawn = base * np.exp(spread * noise) if base else spread * noise
        out[name] = jnp.asarray(drawn.astype(out[name].dtype))
    for name, factor in factors.items():
        out[name] = (out[name] * factor).astype(out[name].dtype)
    return out
```

```python
from contextlib import ExitStack
from math import sqrt

import numpy as np
import concourse.bass as bass
from concourse import mybir

F32 = mybir.dt.float32
I32 = mybir.dt.int32
U32 = mybir.dt.uint32
U8 = mybir.dt.uint8
ALU = mybir.AluOpType
ACT = mybir.ActivationFunctionType
AX = mybir.AxisListType

P = 128
BATCHES, SEQ, DIM = 32, 64, 256
CTX, CDIM = 256, 192
TILES = BATCHES * SEQ // P
CW = CDIM // 2
H0, D0 = 8, 64
H1, D1 = 16, 16
TOKENS = BATCHES * SEQ
EXPERTS, TOPK, INTER = 160, 8, 128
BLOCKS = -(-((TOKENS * TOPK + EXPERTS * (P - 1)) // P) // 4) * 4
REGION = TOKENS // P
ROWS = (EXPERTS * REGION + BLOCKS) * P
NOBODY = 1 << 20
NEG = -3.4028234663852886e38


class Stage:

    def __init__(self, nc, sem, name, plan):
        self.nc, self.name, self.plan = nc, name, plan
        self.engines = {"pe": nc.tensor, "dve": nc.vector, "act": nc.scalar, "pool": nc.gpsimd}
        self.sem = {e: sem(f"{name}_{e}") for e in self.engines}
        self.per, self.at = plan.get(name, ({e: 0 for e in self.engines}, {}))
        self.n = {}
        for e, eng in self.engines.items():
            if self.per[e]:
                eng.sem_inc(self.sem[e], self.per[e])

    def begin(self, idx):
        self.idx, self.n, self.seen = idx, {e: 0 for e in self.engines}, {}

    def end(self):
        self.plan[self.name] = (dict(self.n), dict(self.seen))

    def done(self, e, ins, event):
        self.n[e] += 1
        assert event not in self.seen, event
        self.seen[event] = (e, self.n[e])
        ins.then_inc(self.sem[e], 1)

    def wait(self, eng, event, back=0, idx=None):
        e, k = self.at.get(event, ("pe", 1))
        idx = self.idx if idx is None else idx
        eng.wait_ge(self.sem[e], (idx + (1 - back)) * self.per[e] + k)


class Chain:

    def __init__(self, nc, ctx, eng, name):
        self.eng, self.sem, self.n = eng, ctx.enter_context(nc.semaphore(name)), 0

    def link(self, ins):
        self.n += 1
        ins.then_inc(self.sem, 1)
        self.eng.wait_ge(self.sem, self.n)

    def reset(self):
        if self.n:
            self.eng.sem_clear(self.sem)
        self.n = 0


def constants():
    ident = np.eye(P, dtype=np.float32)
    head = (np.arange(P)[:, None] // D1 == np.arange(8)[None, :]).astype(np.float32)
    inv = 1.0 / 10000.0 ** (np.arange(0, D1, 2, dtype=np.float32) / D1)
    ang = np.arange(H1, dtype=np.float32)[:, None] * inv[None, :].astype(np.float32)
    rope = np.stack([np.cos(ang), np.sin(ang)]).astype(np.float32).reshape(1, 2 * P)
    return {
        "c_ident": ident, "c_head": head, "c_rope": rope,
        "c_tri": np.triu(np.ones((P, P), np.float32), 1),
        "c_ones": np.ones((P, P), np.float32),
        "c_base": (np.arange(EXPERTS, dtype=np.float32) * TOKENS + 1)[None, :],
        "c_steps": (np.arange(3)[None, :] * P + np.arange(P)[:, None]).astype(np.float32),
        "c_tokens": (np.arange(TILES)[None, :] * P + np.arange(P)[:, None]).astype(np.uint32),
    }


def bc(ap, axis, n):
    shape = list(ap.shape)
    shape[axis] = n
    return ap.broadcast_to(shape)


def phase2(nc, a, plan, routes, sem, bank, X, XN, ident, head, small, idle, dchain, amax, pool_waits, carrier, upto):
    slots, wts, shift, todo_row, slots_d, xf_d, todo_d = routes
    pe, dve, act, pool, sp = nc.tensor, nc.vector, nc.scalar, nc.gpsimd, nc.sync
    ph = ExitStack()
    with ph:
        def sb(name, shape, dt=F32):
            return ph.enter_context(nc.sbuf_tensor(name, shape, dt))

        s_const = sem("s_const2")
        n_const = 0

        def const(dst, src):
            nonlocal n_const
            sp.dma_start(dst, src).then_inc(s_const, 16)
            n_const += 1

        def weights(name, rows, cols, p=P):
            w = sb(name, [p, rows // p, cols])
            const(w[:, :, :], a[name].rearrange("(c p) n -> p c n", p=p))
            return w

        def spread(name, n):
            w = sb(name, [P, n])
            const(w[:, :], bc(a[name].rearrange("(a n) -> a n", a=1), 0, P))
            return w

        def column(name, n):
            w = sb(name, [P, n])
            const(w[:, :], a[name])
            return w

        wf = weights("wf", DIM, DIM)
        wqd, wod = weights("wqd", DIM, DIM), weights("wod", DIM, DIM)
        wkd, wvd = weights("wkd", CDIM, DIM, CW), weights("wvd", CDIM, DIM, CW)
        bqd, bkd = column("bqd", 2), column("bkd", 2)
        bvd, bod = spread("bvd", DIM), spread("bod", DIM)
        lns, lnb = spread("lns", DIM), spread("lnb", DIM)
        wh, bh = weights("wh", DIM, 1024), spread("bh", 1024)
        wqk, bqk = weights("wqk", DIM, P), column("bqk", 1)
        osw, osb = column("osw", 2), column("osb", 2)
        wout, bout = weights("wout", 512, DIM), spread("bout", DIM)
        wgs, wds = weights("wgs", DIM, P), weights("wds", P, DIM)
        wr, be = weights("wr", DIM, EXPERTS), spread("be", EXPERTS)
        tri, ones = weights("c_tri", P, P), weights("c_ones", P, P)
        base = sb("base", [P, EXPERTS])
        const(base[:, :], bc(a["c_base"], 0, P))
        tokens = sb("tokens", [P, TILES], U32)
        const(tokens[:, :], a["c_tokens"])

        tern = sb("tern", [P, 2, DIM])
        tmp = sb("tmp", [P, 2, DIM])
        sc = sb("sc", [P, 8])
        s_set = sem("s_set2")

        cT = sb("cT2", [CW, 2, 512])
        s_c = sem("s_c2")
        xq = sb("xq", [P, DIM])
        xqT = sb("xqT", [P, 2, P])
        x3 = sb("x3", [P, DIM])
        stC = sb("stC", [P, 16])
        xnC = sb("xnC", [P, DIM])
        xbC = sb("xbC", [P, DIM])
        xT = sb("xTC", [P, 2, P])
        qT = sb("qTC", [P, 2, P])
        qx = sb("qxC", [P, 2, 2, 8, 64])
        kT = sb("kTC", [P, 2, 512])
        vv = sb("vvC", [P, 4, DIM])
        ex = sb("ex", [P, 8, 512])
        nm = sb("nmC", [P, 8, 2])
        sums = sb("sumsC", [P, 8, 2])
        rec = sb("recC", [P, 8, 2])
        pT = sb("pTC", [P, 8, 512])
        oD = sb("oD", [P, 8, 2, D1])
        oT = sb("oTC", [P, 2, P])
        x4 = sb("x4", [P, DIM])

        x4r = sb("x4r", [P, DIM])
        xbE = sb("xbE", [P, DIM])
        stE = sb("stE", [P, 16])
        xnE = sb("xnE", [P, 2, DIM])
        xTE = sb("xTE", [P, 2, P])
        th = sb("th", [P, 1024])
        uu = sb("uu", [P, 1024])
        hid = sb("hid", [P, 1024])
        qk = sb("qk", [P, 4, P])
        qk2 = sb("qk2", [P, P])
        rel = sb("rel", [P, P])
        att = sb("att", [P, P])
        og = sb("og", [P, 512])
        ogT = sb("ogT", [P, 4, P])
        x5 = sb("x5", [P, DIM])
        xf = sb("xf", [P, DIM])
        xfT = sb("xfT", [P, 2, P])
        ths = sb("ths", [P, P])
        hs = sb("hs", [P, P])
        lg = sb("lg", [P, EXPERTS])
        ez = sb("ez", [P, EXPERTS])
        pr = sb("pr", [P, EXPERTS])
        sel = sb("sel", [P, EXPERTS])
        comb = sb("comb", [P, EXPERTS])
        before = sb("before", [P, EXPERTS])
        junk = sb("junk", [P, EXPERTS])
        top = sb("top", [P, 4, 8])
        slot_id = sb("slot_id", [P, 8], U32)
        tok_id = sb("tok_id", [P, 1], U32)
        ones_e = sb("ones_e", [P, EXPERTS])
        mark = sb("mark", [P, ROWS // P], U32)
        s_mark, s_xf, s_sc = sem("s_mark"), sem("s_xf"), sem("s_sc")

        pool.memset(qx[:, :, :, :, :], 0.0).then_inc(s_set, 1)
        pool.memset(rel[:, :], 0.0).then_inc(s_set, 1)
        pool.memset(before[:, :], 0.0).then_inc(s_set, 1)
        dve.memset(ones_e[:, :], 1.0).then_inc(s_set, 1)
        pool.memset(mark[:, :], NOBODY).then_inc(s_set, 1)
        for e in (pe, dve, act, pool, sp):
            e.wait_ge(s_const, 16 * n_const)
            e.wait_ge(s_set, 5)
        sp.dma_start(slots_d.rearrange("(p n) o -> p (n o)", p=P), mark[:, :]).then_inc(s_mark, 16)
        pool.wait_ge(s_mark, 16)
        dve.tensor_reduce(sc[:, 0:1], wf[:, :, :], AX.XY, ALU.add, apply_absolute_value=True).then_inc(s_set, 1)
        pool.wait_ge(s_set, 6)
        radd, rmax = bass.bass_isa.ReduceOp.add, bass.bass_isa.ReduceOp.max
        pool.partition_all_reduce(sc[:, 1:2], sc[:, 0:1], P, radd).then_inc(s_set, 1)
        pool.partition_all_reduce(sc[:, 2:3], amax[:, 0:1], P, rmax).then_inc(s_set, 1)
        dve.wait_ge(s_set, 8)
        link = dchain.link
        link(dve.tensor_scalar(sc[:, 1:2], sc[:, 1:2], 1.0 / (DIM * DIM), None, ALU.mult))
        link(dve.tensor_scalar(sc[:, 5:6], sc[:, 1:2], 1e-5, None, ALU.add))
        link(dve.reciprocal(sc[:, 6:7], sc[:, 5:6]))
        link(dve.tensor_scalar(tmp[:, :, :], wf[:, :, :], sc[:, 6:7], None, ALU.mult))
        link(dve.tensor_scalar(tern[:, :, :], tmp[:, :, :], 0.5, None, ALU.is_gt))
        link(dve.tensor_scalar(tmp[:, :, :], tmp[:, :, :], -0.5, None, ALU.is_lt))
        link(dve.tensor_tensor(tern[:, :, :], tern[:, :, :], tmp[:, :, :], ALU.subtract))
        link(dve.reciprocal(sc[:, 3:4], sc[:, 2:3]))
        link(dve.tensor_scalar(sc[:, 3:4], sc[:, 3:4], 128.0, None, ALU.mult))
        link(dve.tensor_scalar(sc[:, 4:5], sc[:, 2:3], sc[:, 1:2], 1.0 / 128, ALU.mult, ALU.mult))
        link(dve.tensor_scalar(bqd[:, :], bqd[:, :], 0.25, None, ALU.mult))
        dve.tensor_scalar(bqk[:, :], bqk[:, :], 0.5, None, ALU.mult).then_inc(s_set, 1)
        for e in (pe, dve, act, pool):
            e.wait_ge(s_set, 9)
        dchain.reset()

        C, E = Stage(nc, sem, "C", plan), Stage(nc, sem, "E", plan)

        def moments(S, st, x, tag):
            link(dve.bn_stats(st[:, 0:6], x))
            link(dve.bn_aggr(st[:, 6:8], st[:, 0:6]))
            S.done("dve", dve.tensor_scalar(st[:, 8:9], st[:, 7:8], 1e-5, None, ALU.add), f"var{tag}")
            S.wait(pool, f"var{tag}")
            S.done("pool", pool.tensor_tensor(st[:, 9:10], st[:, 8:9], small[:, 0:1], ALU.pow), f"rstd{tag}")
            S.wait(dve, f"rstd{tag}")

        def halves(b):
            return b[:, 0:2 * P].rearrange("p (c n) -> p c n", c=2)

        def stage_c(i):
            C.begin(i)
            C.wait(sp, "v1", 1)
            sp.dma_start(cT[:, :, :], a["ctx"][bass.ds(i, 1)].rearrange("a p c n -> (a p) c n")).then_inc(s_c, 16)
            lim = float(np.float32(128.0 - 1e-5))
            C.wait(dve, "xqT", 1)
            link(dve.tensor_scalar(xq[:, :], XN[:, bass.ds(i, 1), :].rearrange("p a n -> p (a n)"), sc[:, 3:4], lim, ALU.mult, ALU.min))
            C.done("dve", dve.tensor_scalar(xq[:, :], xq[:, :], -lim, None, ALU.max), "xq")
            C.wait(pe, "xq")
            C.wait(pe, "oTe", 1)
            for c in range(2):
                last = pe.transpose(bank[4][:, c * P:(c + 1) * P], xq[:, c * P:(c + 1) * P], ident[:, :])
            C.done("pe", last, "xqT")
            C.wait(act, "xqT")
            C.wait(act, "yc", 1)
            C.done("act", act.copy(xqT[:, :, :], halves(bank[4])), "xqTe")
            C.wait(pe, "xqTe")
            C.wait(pe, "x4", 1)
            for c in range(2):
                last = pe.matmul(bank[5][:, 0:DIM], xqT[:, c, :], tern[:, c, :], start=(c == 0), stop=(c == 1))
            C.done("pe", last, "yc")
            C.wait(dve, "yc")
            C.wait(dve, "xb", 1)
            C.done("dve", dve.scalar_tensor_tensor(out=x3[:, :], in0=bank[5][:, 0:DIM], scalar=sc[:, 4:5],
                                                   in1=X[:, bass.ds(i, 1), :].rearrange("p a n -> p (a n)"),
                                                   op0=ALU.mult, op1=ALU.add), "x3")
            C.wait(dve, "x3")
            moments(C, stC, x3[:, :], "")
            C.wait(dve, "xnT", 1)
            C.done("dve", dve.tensor_scalar(xnC[:, :], x3[:, :], stC[:, 6:7], stC[:, 9:10], ALU.subtract, ALU.mult), "xn")
            C.wait(pool, "x4", 1)
            C.wait(pool, "xn")
            C.done("pool", pool.tensor_tensor(xbC[:, :], x3[:, :], bod[:, :], ALU.add), "xb")
            yield
            pe.wait_ge(s_c, (i + 1) * 16)
            for m in range(2):
                C.wait(pe, "o1" if m == 0 else "v1e", 1)
                for c in range(2):
                    last = pe.matmul(bank[m][:, :], wkd[:, c, m * P:(m + 1) * P], cT[:, c, :], start=(c == 0), stop=(c == 1))
                C.done("pe", last, f"k{m}")
                C.wait(act, f"k{m}")
                C.wait(act, "s7", 1)
                C.done("act", act.activation(kT[:, m, :], bank[m][:, :], ACT.Identity, bias=bkd[:, m:m + 1]), f"k{m}e")
            yield
            C.wait(pe, "xn")
            C.wait(pe, "xqTe")
            for c in range(2):
                last = pe.transpose(bank[4][:, c * P:(c + 1) * P], xnC[:, c * P:(c + 1) * P], ident[:, :])
            C.done("pe", last, "xnT")
            C.wait(act, "xnT")
            C.wait(act, "q", 1)
            C.done("act", act.copy(xT[:, :, :], halves(bank[4])), "xT")
            for m in range(2):
                C.wait(pe, f"k{m}e")
                for t2 in range(2):
                    q = 2 * m + t2
                    for c in range(2):
                        last = pe.matmul(bank[m][:, t2 * DIM:(t2 + 1) * DIM], cT[:, c, q * P:(q + 1) * P], wvd[:, c, :],
                                         start=(c == 0), stop=(c == 1))
                C.done("pe", last, f"v{m}")
                C.wait(dve, f"v{m}")
                C.wait(dve, "pv1", 1)
                C.done("dve", dve.tensor_tensor(vv[:, 2 * m:2 * m + 2, :], bank[m][:, :].rearrange("p (c n) -> p c n", c=2),
                                                bc(bvd[:, :].rearrange("p (o n) -> p o n", o=1), 1, 2), ALU.add), f"v{m}e")
            yield
            C.wait(pe, "xT")
            C.wait(pe, "x3")
            for m in range(2):
                for c in range(2):
                    last = pe.matmul(bank[5][:, m * P:(m + 1) * P], wqd[:, c, m * P:(m + 1) * P], xT[:, c, :],
                                     start=(c == 0), stop=(c == 1))
            C.done("pe", last, "q")
            C.wait(act, "q")
            C.wait(act, "qx", 1)
            for m in range(2):
                last = act.activation(qT[:, m, :], bank[5][:, m * P:(m + 1) * P], ACT.Identity, bias=bqd[:, m:m + 1], scale=0.25)
            C.done("act", last, "qe")
            C.wait(dve, "qe")
            C.wait(dve, "s7", 1)
            hm = head[:, :].rearrange("p (a h o) -> p a h o", a=1, o=1)
            for m in range(2):
                last = dve.tensor_tensor(qx[:, m, :, :, :], bc(qT[:, m, :].rearrange("p (b o t) -> p b o t", b=2, o=1), 2, 8),
                                         bc(bc(hm, 1, 2), 3, 64), ALU.mult)
            C.done("dve", last, "qx")
            yield
            for u in range(8):
                m, hp = divmod(u, 4)
                bk = bank[2 + u % 2]
                if u == 0:
                    C.wait(pe, "qx")
                if hp == 0:
                    C.wait(pe, f"k{m}e")
                C.wait(pe, f"e{(u - 2) % 8}", 0 if u >= 2 else 1)
                for b in range(2):
                    last = pe.matmul(bk[:, 256 * b:256 * b + 256], qx[:, m, b, 2 * hp:2 * hp + 2, :].rearrange("p h t -> p (h t)"),
                                     kT[:, m, 256 * b:256 * b + 256], start=True, stop=True)
                C.done("pe", last, f"s{u}")
                C.wait(dve, f"s{u}")
                C.wait(dve, f"e{u}", 1)
                C.done("dve", dve.tensor_reduce(nm[:, u, :], bk[:, :].rearrange("p (b n) -> p b n", b=2), AX.X, ALU.max, negate=True), f"m{u}")
                C.wait(act, f"m{u}")
                if u == 0:
                    C.wait(act, "rec", 1)
                C.wait(act, f"pT{u}", 1)
                for b in range(2):
                    last = act.activation(ex[:, u, 256 * b:256 * b + 256], bk[:, 256 * b:256 * b + 256], ACT.Exp,
                                          bias=nm[:, u, b:b + 1], accum_out=sums[:, u, b:b + 1])
                C.done("act", last, f"e{u}")
                if u == 3:
                    yield
            yield
            for u in range(8):
                bk = bank[4 + u % 2]
                C.wait(pe, f"e{u}")
                C.wait(pe, {0: "xT", 1: "qe"}.get(u, f"pT{u - 2}e"))
                for q in range(4):
                    last = pe.transpose(bk[:, q * P:(q + 1) * P], ex[:, u, q * P:(q + 1) * P], ident[:, :])
                C.done("pe", last, f"pT{u}")
                eng, en = (act, "act") if u % 2 else (dve, "dve")
                C.wait(eng, f"pT{u}")
                if u < 2:
                    C.wait(eng, "pv1", 1)
                copy = act.copy if u % 2 else dve.tensor_copy
                C.done(en, copy(pT[:, u, :], bk[:, :]), f"pT{u}e")
            C.wait(dve, "e7")
            C.wait(dve, "o1", 1)
            C.done("dve", dve.reciprocal(rec[:, :, :], sums[:, :, :]), "rec")
            yield
            for b in range(2):
                C.wait(pe, f"v{b}e")
                C.wait(pe, "pT7e")
                C.wait(pe, "pT6e")
                for u in range(8):
                    for kc in range(2):
                        q = 2 * b + kc
                        last = pe.matmul(bank[b][:, 32 * u:32 * u + 32], pT[:, u, q * P:(q + 1) * P], vv[:, q, 32 * u:32 * u + 32],
                                         start=(kc == 0), stop=(kc == 1))
                C.done("pe", last, f"pv{b}")
                C.wait(dve, f"pv{b}")
                if b == 0:
                    C.wait(dve, "rec")
                    C.wait(dve, "oT", 1)
                for h2 in range(2):
                    r = slice(64 * h2, 64 * h2 + 64)
                    src = bank[b][r, 0:DIM].rearrange("p (u n) -> p u n", u=8)[:, :, D1 * h2:D1 * h2 + D1]
                    last = dve.tensor_tensor(oD[64 * b:64 * b + 64, :, h2, :], src, bc(rec[r, :, b:b + 1], 2, D1), ALU.mult)
                C.done("dve", last, f"o{b}")
            yield
            C.wait(pe, "o1")
            C.wait(pe, "pT6e")
            for c in range(2):
                last = pe.transpose(bank[4][:, c * P:(c + 1) * P], oD[:, 4 * c:4 * c + 4, :, :].rearrange("p u a n -> p (u a n)"), ident[:, :])
            C.done("pe", last, "oT")
            C.wait(act, "oT")
            C.wait(act, "yp", 1)
            C.done("act", act.copy(oT[:, :, :], halves(bank[4])), "oTe")
            C.wait(pe, "oTe")
            C.wait(pe, "pT7e")
            for c in range(2):
                last = pe.matmul(bank[5][:, 0:DIM], oT[:, c, :], wod[:, c, :], start=(c == 0), stop=(c == 1))
            C.done("pe", last, "yp")
            C.wait(dve, "yp")
            C.wait(dve, "xb")
            E.wait(dve, "x4r", idx=i - 1)
            C.done("dve", dve.tensor_tensor(x4[:, :], bank[5][:, 0:DIM], xbC[:, :], ALU.add), "x4")
            C.end()

        def stage_e(j):
            E.begin(j)
            C.wait(dve, "x4", idx=j)
            moments(E, stE, x4[:, :], "a")
            link(dve.tensor_scalar(stE[:, 10:11], stE[:, 7:8], stE[:, 9:10], stE[:, 9:10], ALU.mult, ALU.mult))
            E.done("dve", dve.tensor_scalar(stE[:, 11:12], stE[:, 10:11], 1e-5, None, ALU.add), "var2")
            E.wait(pool, "var2")
            E.done("pool", pool.tensor_tensor(stE[:, 12:13], stE[:, 11:12], small[:, 0:1], ALU.pow), "rstd2")
            E.wait(dve, "rstd2")
            E.wait(dve, "xnT", 1)
            E.done("dve", dve.tensor_scalar(xnE[:, 0, :], x4[:, :], stE[:, 6:7], stE[:, 9:10], ALU.subtract, ALU.mult), "xc")
            C.wait(act, "x4", idx=j)
            E.wait(act, "xbE", 1)
            E.done("act", act.copy(x4r[:, :], x4[:, :]), "x4r0")
            E.wait(dve, "xc")
            link(dve.scalar_tensor_tensor(out=xnE[:, 1, :], in0=xnE[:, 0, :], scalar=stE[:, 12:13], in1=lns[:, :], op0=ALU.mult, op1=ALU.mult))
            E.wait(dve, "x4r0")
            E.done("dve", dve.tensor_tensor(xnE[:, 0, :], xnE[:, 1, :], lnb[:, :], ALU.add), "x4r")
            E.wait(pool, "x5", 1)
            E.wait(pool, "x4r0")
            E.done("pool", pool.tensor_tensor(xbE[:, :], x4r[:, :], bout[:, :], ALU.add), "xbE")
            E.wait(pe, "x4r")
            E.wait(pe, "before", 1)
            for c in range(2):
                last = pe.transpose(bank[6][:, c * P:(c + 1) * P], xnE[:, 0, c * P:(c + 1) * P], ident[:, :])
            E.done("pe", last, "xnT")
            E.wait(act, "xnT")
            E.wait(act, "h1", 1)
            E.done("act", act.copy(xTE[:, :, :], halves(bank[6])), "xT")
            yield
            E.wait(pe, "xT")
            E.wait(pe, "x6", 1)
            for c in range(2):
                last = pe.matmul(bank[7][:, 0:P], wqk[:, c, :], xTE[:, c, :], start=(c == 0), stop=(c == 1))
            E.done("pe", last, "qk")
            E.wait(act, "qk")
            E.wait(act, "qke", 1)
            act.activation(qk[:, 1, :], bank[7][:, 0:P], ACT.Identity, bias=bqk[:, 0:1], scale=0.5)
            E.done("act", act.activation(qk[:, 0, :], bank[7][:, 0:P], ACT.Tanh, bias=bqk[:, 0:1], scale=0.5), "qku")
            E.wait(dve, "qku")
            E.wait(dve, "sim", 1)
            link(dve.scalar_tensor_tensor(out=qk2[:, :], in0=qk[:, 0, :], scalar=1.0, in1=qk[:, 1, :], op0=ALU.add, op1=ALU.mult))
            dve.tensor_scalar(qk[:, 2, :], qk2[:, :], osw[:, 0:1], osb[:, 0:1], ALU.mult, ALU.add)
            E.done("dve", dve.tensor_scalar(qk[:, 3, :], qk2[:, :], osw[:, 1:2], osb[:, 1:2], ALU.mult, ALU.add), "qke")
            for g in range(2):
                bk = bank[6 + g]
                E.wait(pe, "xT" if g == 0 else "qku")
                for c in range(2):
                    last = pe.matmul(bk[:, :], xTE[:, c, :], wh[:, c, 512 * g:512 * g + 512], start=(c == 0), stop=(c == 1))
                E.done("pe", last, f"h{g}")
                hs_ = slice(512 * g, 512 * g + 512)
                E.wait(dve, f"h{g}")
                E.wait(dve, f"hid{g}", 1)
                E.done("dve", dve.tensor_tensor(uu[:, hs_], bk[:, :], bh[:, hs_], ALU.add), f"u{g}")
                E.wait(act, f"u{g}")
                E.done("act", act.activation(th[:, hs_], uu[:, hs_], ACT.Tanh, scale=0.5), f"th{g}")
                E.wait(dve, f"th{g}")
                if g == 0:
                    E.wait(dve, "av", 1)
                else:
                    E.wait(dve, "og", 1)
                E.done("dve", dve.scalar_tensor_tensor(out=hid[:, hs_], in0=th[:, hs_], scalar=1.0, in1=uu[:, hs_], op0=ALU.add, op1=ALU.mult), f"hid{g}")
            yield
            E.wait(pe, "qke")
            E.wait(pe, "u0")
            E.done("pe", pe.matmul(bank[6][:, 0:P], qk[:, 3, :], qk[:, 2, :], start=True, stop=True), "sim")
            E.wait(dve, "sim")
            for b in range(2):
                r = slice(64 * b, 64 * b + 64)
                last = dve.tensor_scalar(rel[r, r], bank[6][r, r], 1.0 / SEQ, 0.0, ALU.mult, ALU.max)
            E.done("dve", last, "rel")
            E.wait(dve, "rel")
            E.wait(dve, "av", 1)
            E.done("dve", dve.tensor_tensor(att[:, :], rel[:, :], rel[:, :], ALU.mult), "att")
            E.wait(pe, "att")
            E.wait(pe, "hid0")
            E.wait(pe, "u1")
            E.done("pe", pe.matmul(bank[7][:, :], att[:, :], hid[:, 0:512], start=True, stop=True), "av")
            E.wait(dve, "av")
            E.wait(dve, "hid1")
            E.wait(dve, "ogT", 1)
            E.done("dve", dve.scalar_tensor_tensor(out=og[:, :], in0=bank[7][:, :], scalar=0.25, in1=hid[:, 512:1024], op0=ALU.mult, op1=ALU.mult), "og")
            yield
            E.wait(pe, "og")
            E.wait(pe, "rel")
            for c in range(4):
                last = pe.transpose(bank[6][:, c * P:(c + 1) * P], og[:, c * P:(c + 1) * P], ident[:, :])
            E.done("pe", last, "ogT")
            E.wait(act, "ogT")
            E.wait(act, "yo", 1)
            E.done("act", act.copy(ogT[:, :, :], bank[6][:, :].rearrange("p (c n) -> p c n", c=4)), "ogTe")
            E.wait(pe, "ogTe")
            for c in range(4):
                last = pe.matmul(bank[7][:, 0:DIM], ogT[:, c, :], wout[:, c, :], start=(c == 0), stop=(c == 3))
            E.done("pe", last, "yo")
            E.wait(dve, "yo")
            E.wait(dve, "xbE")
            E.wait(dve, "x6", 1)
            E.done("dve", dve.tensor_tensor(x5[:, :], bank[7][:, 0:DIM], xbE[:, :], ALU.add), "x5")
            E.wait(dve, "x5")
            moments(E, stE, x5[:, :], "f")
            E.wait(dve, "xfT", 1)
            dve.wait_ge(s_xf, j * 16)
            E.done("dve", dve.tensor_scalar(xf[:, :], x5[:, :], stE[:, 6:7], stE[:, 9:10], ALU.subtract, ALU.mult), "xf")
            yield
            E.wait(pe, "xf")
            E.wait(pe, "ogTe")
            for c in range(2):
                last = pe.transpose(bank[6][:, c * P:(c + 1) * P], xf[:, c * P:(c + 1) * P], ident[:, :])
            E.done("pe", last, "xfT")
            E.wait(act, "xfT")
            E.wait(act, "sh", 1)
            E.done("act", act.copy(xfT[:, :, :], halves(bank[6])), "xfTe")
            E.wait(pe, "xfTe")
            E.wait(pe, "x5")
            for c in range(2):
                last = pe.matmul(bank[7][:, 0:P], wgs[:, c, :], xfT[:, c, :], start=(c == 0), stop=(c == 1))
            E.done("pe", last, "sh")
            E.wait(act, "sh")
            E.wait(act, "hs", 1)
            E.done("act", act.activation(ths[:, :], bank[7][:, 0:P], ACT.Tanh, scale=0.5), "ths")
            E.wait(dve, "ths")
            E.wait(dve, "ys", 1)
            E.done("dve", dve.scalar_tensor_tensor(out=hs[:, :], in0=ths[:, :], scalar=1.0, in1=bank[7][:, 0:P], op0=ALU.add, op1=ALU.mult), "hs")
            E.wait(pe, "hs")
            E.done("pe", pe.matmul(bank[7][:, 0:DIM], hs[:, :], wds[:, 0, :], start=True, stop=True), "ys")
            E.wait(dve, "ys")
            E.done("dve", dve.scalar_tensor_tensor(out=X[:, bass.ds(j, 1), :].rearrange("p a n -> p (a n)"), in0=bank[7][:, 0:DIM],
                                                   scalar=0.5, in1=x5[:, :], op0=ALU.mult, op1=ALU.add), "x6")
            E.wait(sp, "xf")
            sp.dma_start(xf_d[bass.ds(j, 1)].rearrange("a p n -> (a p) n"), xf[:, :]).then_inc(s_xf, 16)
            yield
            E.wait(pe, "x6")
            for c in range(2):
                last = pe.matmul(bank[7][:, 0:EXPERTS], xfT[:, c, :], wr[:, c, :], start=(c == 0), stop=(c == 1))
            E.done("pe", last, "lg")
            E.wait(dve, "lg")
            E.done("dve", dve.tensor_tensor(lg[:, :], bank[7][:, 0:EXPERTS], be[:, :], ALU.add), "lge")
            E.wait(act, "lge")
            E.done("act", act.activation(ez[:, :], lg[:, :], ACT.Exp, scale=-1.0), "ez")
            E.wait(dve, "ez")
            link(dve.tensor_scalar(ez[:, :], ez[:, :], 1.0, None, ALU.add))
            link(dve.reciprocal(pr[:, :], ez[:, :]))
            link(dve.max(top[:, 0, :], pr[:, :]))
            link(dve.match_replace(out=ez[:, :], in_to_replace=top[:, 0, :], in_values=pr[:, :], imm_value=-1.0))
            E.wait(dve, "before", 1)
            E.done("dve", dve.tensor_scalar(sel[:, :], ez[:, :], 0.0, None, ALU.is_lt), "sel")
            link(dve.tensor_reduce(top[:, 3, 0:1], top[:, 0, :], AX.X, ALU.add))
            link(dve.tensor_scalar(top[:, 3, 0:1], top[:, 3, 0:1], 1e-9, None, ALU.add))
            link(dve.reciprocal(top[:, 3, 1:2], top[:, 3, 0:1]))
            link(dve.tensor_scalar(top[:, 3, 1:2], top[:, 3, 1:2], 2.5, None, ALU.mult))
            E.wait(dve, "sel")
            link(dve.scalar_tensor_tensor(out=comb[:, :], in0=pr[:, :], scalar=top[:, 3, 1:2], in1=sel[:, :], op0=ALU.mult, op1=ALU.mult))
            E.wait(pe, "sel")
            E.wait(pe, "xfTe")
            E.wait(pe, "before", 1)
            pe.matmul(bank[6][:, 0:EXPERTS], tri[:, 0, :], sel[:, :], start=True, stop=False)
            E.done("pe", pe.matmul(bank[6][:, 0:EXPERTS], ones[:, 0, :], before[:, :], start=False, stop=True), "rank")
            E.wait(dve, "rank")
            link(dve.tensor_tensor(lg[:, :], bank[6][:, 0:EXPERTS], base[:, :], ALU.add))
            E.done("dve", dve.tensor_tensor(before[:, :], before[:, :], sel[:, :], ALU.add), "before")
            link(dve.tensor_tensor(lg[:, :], lg[:, :], sel[:, :], ALU.mult))
            link(dve.max(top[:, 1, :], lg[:, :]))
            for k in range(TOPK):
                link(dve.scalar_tensor_tensor(out=junk[:, :], in0=lg[:, :], scalar=top[:, 1, k:k + 1], in1=comb[:, :],
                                              op0=ALU.is_equal, op1=ALU.mult, accum_out=top[:, 2, k:k + 1]))
            dve.wait_ge(s_sc, j * 16 * TOPK)
            dve.tensor_scalar(slot_id[:, :], top[:, 1, :], 1.0, None, ALU.subtract).then_inc(dchain.sem, 1)
            dchain.n += 1
            E.done("dve", dve.tensor_copy(tok_id[:, :], tokens[:, bass.ds(j, 1)]), "tok")
            dve.wait_ge(dchain.sem, dchain.n)
            E.done("dve", dve.tensor_copy(slots[:, bass.ds(j, 1), :].rearrange("p a n -> p (a n)"), lg[:, :]), "ids")
            E.done("dve", dve.tensor_copy(wts[:, bass.ds(j, 1), :].rearrange("p a n -> p (a n)"), top[:, 2, :]), "wts")
            E.wait(dve, "wts")
            E.wait(pool, "ids")
            pool_waits.link(pool.tensor_tensor(carrier[:, 1:2], carrier[:, 0:1], carrier[:, 0:1], ALU.add))
            for k in range(TOPK):
                pool.indirect_dma_start(out=slots_d, out_offset=bass.IndirectOffsetOnAxis(ap=slot_id[:, k:k + 1], axis=0),
                                        in_=tok_id[:, 0:1], in_offset=None).then_inc(s_sc, 16)
            E.end()

        def step(s, do_c, do_e):
            gc = stage_c(s) if do_c else iter(())
            ge = stage_e(s - 1) if do_e else iter(())
            for which in "ECCECCECECECECEC":
                next(ge if which == "E" else gc, None)
            for g in (gc, ge):
                for _ in g:
                    pass
            dchain.reset()
            pool_waits.reset()

        step(0, True, False)
        with nc.Fori(1, TILES, 1) as s:
            step(s, True, True)
        step(TILES, False, True)
        E.wait(pe, "before", idx=TILES - 1)
        s_pl = sem("s_plan")
        pe.matmul(bank[0][:, 0:EXPERTS], ones[:, 0, :], before[:, :], start=True, stop=True).then_inc(s_pl, 1)
        dve.wait_ge(s_pl, 1)
        blocks = sb("blocks", [P, EXPERTS], I32)
        bf = sb("bf", [P, EXPERTS])
        ends = sb("ends", [P, EXPERTS])
        steps = sb("steps", [P, 3])
        done = sb("done", [P, 3, EXPERTS])
        st = sb("st", [P, 3, 4])
        todo = sb("todo", [P, 3, 2], U32)
        sp.dma_start(steps[:, :], a["c_steps"]).then_inc(s_mark, 16)
        link(dve.tensor_scalar(blocks[:, :], bank[0][:, 0:EXPERTS], P - 1.0, None, ALU.add))
        link(dve.tensor_scalar(blocks[:, :], blocks[:, :], 7, None, ALU.logical_shift_right))
        link(dve.tensor_copy(bf[:, :], blocks[:, :]))
        link(dve.tensor_tensor_scan(ends[:, :], ones_e[:, :], bf[:, :], 0.0, ALU.mult, ALU.add))
        link(dve.tensor_tensor(bf[:, :], ends[:, :], bf[:, :], ALU.subtract))
        link(dve.scalar_tensor_tensor(out=bf[:, :], in0=bf[:, :], scalar=float(P), in1=base[:, :], op0=ALU.mult, op1=ALU.subtract))
        link(dve.tensor_scalar(shift[:, :], bf[:, :], 1.0, None, ALU.add))
        dve.wait_ge(s_mark, 32)
        for g in range(3):
            link(dve.tensor_scalar(done[:, g, :], ends[:, :], steps[:, g:g + 1], None, ALU.is_le))
            link(dve.tensor_reduce(st[:, g, 0:1], done[:, g, :], AX.X, ALU.add))
            link(dve.tensor_tensor(done[:, g, :], done[:, g, :], ends[:, :], ALU.mult))
            link(dve.tensor_reduce(st[:, g, 1:2], done[:, g, :], AX.X, ALU.max))
            link(dve.tensor_tensor(st[:, g, 2:3], steps[:, g:g + 1], st[:, g, 1:2], ALU.subtract))
            link(dve.scalar_tensor_tensor(out=todo[:, g, 0:1], in0=st[:, g, 0:1], scalar=float(REGION), in1=st[:, g, 2:3], op0=ALU.mult, op1=ALU.add))
            link(dve.tensor_scalar(todo[:, g, 1:2], st[:, g, 0:1], EXPERTS - 1.0, None, ALU.min))
        dve.memset(idle[:, 0:1], 0.0).then_inc(s_pl, 1)
        dchain.reset()
        sp.wait_ge(s_pl, 2)
        sp.dma_start(todo_d.rearrange("(g p) n -> p g n", p=P), todo[:, :, :]).then_inc(s_mark, 16)
        sp.wait_ge(s_mark, 48)
        sp.dma_start(todo_row[:, :], todo_d.rearrange("(o t) n -> o (t n)", o=1)).then_inc(s_mark, 16)
        sp.wait_ge(s_mark, 64)
        sp.wait_ge(s_xf, 16 * TILES)
        sp.wait_ge(s_sc, 16 * TOPK * TILES)
        E.wait(sp, "x6", idx=TILES - 1)
        E.wait(sp, "wts", idx=TILES - 1)
    nc.all_engine_barrier()


def experts(nc, a, plan, sem, bank, ident, todo_row, slots_d, xf_d, y_d, pool_waits, carrier):
    pe, dve, act, pool, sp = nc.tensor, nc.vector, nc.scalar, nc.gpsimd, nc.sync
    DEEP = 4
    ph = ExitStack()
    with ph:
        def ring(name, shape, dt=F32):
            return [ph.enter_context(nc.sbuf_tensor(f"{name}{z}", shape, dt)) for z in range(DEEP)]

        who = ring("who", [P, 1], U32)
        w = ring("w", [P, DIM + DIM])
        xg = ring("xg", [P, DIM])
        xgT = ring("xgT", [P, 2, P])
        h = ring("h", [P, P])
        y = ring("y", [P, DIM])
        s_who = [sem(f"s_who{z}") for z in range(DEEP)]
        s_w = [sem(f"s_w{z}") for z in range(DEEP)]
        s_g = [sem(f"s_g{z}") for z in range(DEEP)]
        s_y = [sem(f"s_y{z}") for z in range(DEEP)]
        s_z = sem("s_zero")
        for z in range(DEEP):
            dve.memset(xg[z][:, :], 0.0).then_inc(s_z, 1)
        pool.wait_ge(s_z, DEEP)
        last_token = pool.to_reg(TOKENS - 1)
        M = Stage(nc, sem, "M", plan)
        rows = xf_d.rearrange("t p n -> (t p) n")
        blocks_of = slots_d.rearrange("(q p) o -> q p o", p=P)
        y_blocks = y_d.rearrange("(q p) n -> q p n", p=P)

        with nc.Fori(0, BLOCKS // DEEP, 1) as s:
            M.begin(s)
            for z in range(DEEP):
                at = (s * DEEP + z) * 2
                q = sp.value_load(todo_row[0:1, bass.ds(at, 1)])
                e = sp.value_load(todo_row[0:1, bass.ds(at + 1, 1)])
                sp.wait_ge(s_g[z], s * 16)
                sp.dma_start(who[z][:, :], blocks_of[bass.ds(q, 1)].rearrange("a p o -> (a p) o")).then_inc(s_who[z], 16)
                M.wait(sp, f"y{z}", 1)
                sp.dma_start(w[z][:, :], a["wexp"][bass.ds(e, 1)].rearrange("a p n -> (a p) n")).then_inc(s_w[z], 16)
                M.wait(pool, f"xT{z}", 1)
                pool.wait_ge(s_who[z], (s + 1) * 16)
                pool_waits.link(pool.tensor_tensor(carrier[:, 1:2], carrier[:, 0:1], carrier[:, 0:1], ALU.add))
                pool.indirect_dma_start(out=xg[z][:, :], out_offset=None, in_=rows,
                                        in_offset=bass.IndirectOffsetOnAxis(ap=who[z][:, 0:1], axis=0),
                                        bounds_check=last_token, oob_is_err=False).then_inc(s_g[z], 16)

            def turn(z):
                bk = bank[2 * z]
                pe.wait_ge(s_g[z], (s + 1) * 16)
                M.wait(pe, f"ye{z}", 1)
                for c in range(2):
                    last = pe.transpose(bk[:, c * P:(c + 1) * P], xg[z][:, c * P:(c + 1) * P], ident[:, :])
                M.done("pe", last, f"xT{z}")
                M.wait(dve, f"xT{z}")
                M.wait(dve, f"h{z}", 1)
                M.done("dve", dve.tensor_copy(xgT[z][:, :, :], bk[:, 0:2 * P].rearrange("p (c n) -> p c n", c=2)), f"xTe{z}")

            def up(z):
                bk = bank[2 * z + 1]
                pe.wait_ge(s_w[z], (s + 1) * 16)
                M.wait(pe, f"xTe{z}")
                M.wait(pe, f"silu{z}", 1)
                for c in range(2):
                    last = pe.matmul(bk[:, 0:P], w[z][:, c * P:(c + 1) * P], xgT[z][:, c, :], start=(c == 0), stop=(c == 1))
                M.done("pe", last, f"h{z}")
                M.wait(act, f"h{z}")
                M.wait(act, f"y{z}", 1)
                M.done("act", act.activation(h[z][:, :], bk[:, 0:P], ACT.Silu), f"silu{z}")

            def down(z):
                bk = bank[2 * z]
                M.wait(pe, f"silu{z}")
                M.done("pe", pe.matmul(bk[:, 0:DIM], h[z][:, :], w[z][:, DIM:2 * DIM], start=True, stop=True), f"y{z}")
                M.wait(dve, f"y{z}")
                dve.wait_ge(s_y[z], s * 16)
                M.done("dve", dve.tensor_copy(y[z][:, :], bk[:, 0:DIM]), f"ye{z}")
                M.wait(act, f"ye{z}")
                act.dma_start(y_blocks[bass.ds(s * DEEP + z, 1)].rearrange("a p n -> (a p) n"), y[z][:, :]).then_inc(s_y[z], 16)

            turn(0)
            turn(1)
            up(0)
            turn(2)
            up(1)
            down(0)
            turn(3)
            up(2)
            down(1)
            up(3)
            down(2)
            down(3)
            M.end()
            pool_waits.reset()
        for z in range(DEEP):
            sp.wait_ge(s_y[z], 16 * (BLOCKS // DEEP))
    nc.all_engine_barrier()


def combine(nc, plan, sem, X, slots, shift, wts, y_d, out, dchain, pool_waits, carrier):
    dve, pool, sp = nc.vector, nc.gpsimd, nc.sync
    ph = ExitStack()
    with ph:
        def pair(name, shape, dt=F32):
            return [ph.enter_context(nc.sbuf_tensor(f"{name}{z}", shape, dt)) for z in range(2)]

        ids, wt = pair("ids", [P, TOPK], U32), pair("wt", [P, TOPK])
        g, acc = pair("g", [P, TOPK, DIM]), pair("acc", [P, 2, DIM])
        moved = ph.enter_context(nc.sbuf_tensor("moved", [P, 2, EXPERTS], F32))
        top = ph.enter_context(nc.sbuf_tensor("top_rows", [P, 8], F32))
        s_row = [[sem(f"s_row{z}{k}") for k in range(TOPK)] for z in range(2)]
        s_o = [sem(f"s_o{z}") for z in range(2)]
        T = Stage(nc, sem, "T", plan)
        with nc.Fori(0, TILES // 2, 1) as s:
            T.begin(s)
            for z in range(2):
                i = s * 2 + z
                mine = slots[:, bass.ds(i, 1), :].rearrange("p a n -> p (a n)")
                dchain.link(dve.tensor_tensor(moved[:, 0, :], mine, shift[:, :], ALU.add))
                dchain.link(dve.scalar_tensor_tensor(out=moved[:, 1, :], in0=mine, scalar=0.0, in1=moved[:, 0, :], op0=ALU.is_gt, op1=ALU.mult))
                dchain.link(dve.max(top[:, :], moved[:, 1, :]))
                dve.wait_ge(s_row[z][TOPK - 1], s * 16)
                T.done("dve", dve.tensor_scalar(ids[z][:, :], top[:, :], 1.0, None, ALU.subtract), f"ids{z}")
                T.wait(pool, f"ids{z}")
                T.wait(pool, f"acc{z}", 1)
                pool_waits.link(pool.tensor_tensor(carrier[:, 1:2], carrier[:, 0:1], carrier[:, 0:1], ALU.add))
                for k in range(TOPK):
                    pool.indirect_dma_start(out=g[z][:, k, :], out_offset=None, in_=y_d,
                                            in_offset=bass.IndirectOffsetOnAxis(ap=ids[z][:, k:k + 1], axis=0)).then_inc(s_row[z][k], 16)
            for z in range(2):
                i = s * 2 + z
                T.wait(dve, f"acc{z}", 1)
                T.done("dve", dve.tensor_copy(wt[z][:, :], wts[:, bass.ds(i, 1), :].rearrange("p a n -> p (a n)")), f"wt{z}")
                T.wait(dve, f"wt{z}")
                dve.wait_ge(s_o[z], s * 16)
                for k in range(TOPK):
                    dve.wait_ge(s_row[z][k], (s + 1) * 16)
                    prev = X[:, bass.ds(i, 1), :].rearrange("p a n -> p (a n)") if k == 0 else acc[z][:, (k - 1) % 2, :]
                    ins = dve.scalar_tensor_tensor(out=acc[z][:, k % 2, :], in0=g[z][:, k, :], scalar=wt[z][:, k:k + 1], in1=prev,
                                                   op0=ALU.mult, op1=ALU.add)
                    if k < TOPK - 1:
                        dchain.link(ins)
                T.done("dve", ins, f"acc{z}")
                T.wait(sp, f"acc{z}")
                sp.dma_start(out.rearrange("(t p) n -> t p n", p=P)[bass.ds(i, 1)].rearrange("a p n -> (a p) n"),
                             acc[z][:, (TOPK - 1) % 2, :]).then_inc(s_o[z], 16)
            T.end()
            dchain.reset()
            pool_waits.reset()
        for z in range(2):
            sp.wait_ge(s_o[z], 16 * (TILES // 2))


def program(nc, a, out, plan, upto=9):
    ctx = ExitStack()
    with ctx:
        pe, dve, act, pool, sp = nc.tensor, nc.vector, nc.scalar, nc.gpsimd, nc.sync

        def sb(name, shape, dt=F32):
            return ctx.enter_context(nc.sbuf_tensor(name, shape, dt))

        bank = [ctx.enter_context(nc.psum_tensor(f"bank{k}", [P, 512], F32)) for k in range(8)]

        def sem(name):
            return ctx.enter_context(nc.semaphore(name))

        X = sb("X", [P, TILES, DIM])
        XN = sb("XN", [P, TILES, DIM])
        amax = sb("amax", [P, 2])
        ident = sb("ident", [P, P])
        head = sb("head", [P, 8])
        small = sb("small", [P, 16])
        idle = sb("idle", [1, 1])
        s_const, s_w0, s_setup = sem("s_const"), sem("s_rope"), sem("s_setup")
        dchain = Chain(nc, ctx, dve, "dve_chain")
        pool_waits = Chain(nc, ctx, pool, "pool_waits")
        carrier = sb("carrier", [1, 2])

        n_const = 0

        def const(dst, src):
            nonlocal n_const
            sp.dma_start(dst, src).then_inc(s_const, 16)
            n_const += 1

        const(ident[:, :], a["c_ident"])
        const(head[:, :], a["c_head"])

        ph1 = ExitStack()
        with ph1:
            def sb1(name, shape, dt=F32):
                return ph1.enter_context(nc.sbuf_tensor(name, shape, dt))

            wq0 = sb1("wq0", [P, 2, 512])
            wk0 = sb1("wk0", [CW, 2, 512])
            wv0 = sb1("wv0", [CW, 2, 512])
            wo0 = sb1("wo0", [P, 4, DIM])
            bo0 = sb1("bo0", [P, DIM])
            const(wq0[:, :, :], a["wq0"].rearrange("(c p) n -> p c n", p=P))
            const(wk0[:, :, :], a["wk0"].rearrange("(c p) n -> p c n", p=CW))
            const(wv0[:, :, :], a["wv0"].rearrange("(c p) n -> p c n", p=CW))
            const(wo0[:, :, :], a["wo0"].rearrange("(c p) n -> p c n", p=P))
            const(bo0[:, :], bc(a["bo0"].rearrange("(a n) -> a n", a=1), 0, P))
            wqs = sb1("wqs", [P, 2, DIM])
            wla = sb1("wla", [P, 2, P])
            wlb = sb1("wlb", [P, DIM])
            wos = sb1("wos", [P, 2, DIM])
            gam = sb1("gam", [P, DIM])
            bet = sb1("bet", [P, DIM])
            rope = sb1("rope", [P, 2 * P])
            wraw = sb1("wraw", [P, 3, DIM])
            const(wraw[:, 0:2, :], a["wqs"].rearrange("(c p) n -> p c n", p=P))
            const(wraw[0:64, 2, :], a["wkb"])
            const(wlb[64:128, :], a["wvb"])
            const(wla[:, :, 0:64], a["wka"].rearrange("(c p) n -> p c n", p=P))
            const(wla[:, :, 64:128], a["wva"].rearrange("(c p) n -> p c n", p=P))
            const(wos[:, :, :], a["wos"].rearrange("(c p) n -> p c n", p=P))
            const(gam[:, :], bc(a["gam"].rearrange("(a n) -> a n", a=1), 0, P))
            const(bet[:, :], bc(a["bet"].rearrange("(a n) -> a n", a=1), 0, P))
            const(rope[:, :], bc(a["c_rope"], 0, P))

            xin = sb1("xin", [P, DIM])
            cT = sb1("cT", [CW, 2, 512])
            mk = sb1("mk", [P, 512], U8)
            s_x, s_c, s_m = sem("s_x"), sem("s_c"), sem("s_m")
            stA = sb1("stA", [P, 16])
            xnA = sb1("xnA", [P, DIM])
            xb = sb1("xb", [P, DIM])
            xT = sb1("xT", [P, 2, P])
            qx = sb1("qx", [P, 2, 4, P])
            kT = sb1("kT", [P, 4, 512])
            vv = sb1("vv", [P, 4, 512])
            mb = sb1("mb", [P, 512])
            sm = sb1("sm", [P, 4, 512])
            nm = sb1("nm", [P, 8])
            sums = sb1("sums", [P, 8])
            rec = sb1("rec", [P, 8])
            pT = sb1("pT", [P, 4, 512])
            oA = sb1("oA", [P, 4, 2, 64])
            oT = sb1("oT", [P, 4, P])
            xB = sb1("xB", [P, DIM])

            xr = sb1("xr", [P, DIM])
            stB = sb1("stB", [P, 16])
            xnB = sb1("xnB", [P, DIM])
            xTB = sb1("xTB", [P, 2, P])
            lat = sb1("lat", [P, P])
            qTB = sb1("qTB", [P, 2, P])
            kx = sb1("kx", [P, 2, 8, P])
            vB = sb1("vB", [P, DIM])
            negm = sb1("negm", [P, H1])
            sB = sb1("sB", [P, H1])
            recB = sb1("recB", [P, H1])
            pB = sb1("pB", [P, H1, P])
            pTB = sb1("pTB", [P, H1, P])
            oB = sb1("oB", [P, DIM])
            oTB = sb1("oTB", [P, 2, P])
            x2 = sb1("x2", [P, DIM])
            t3 = sb1("t3", [P, 2, DIM])

            pool.memset(small[:, 0:1], -0.5).then_inc(s_setup, 1)
            pool.memset(carrier[:, :], 0.0).then_inc(s_setup, 1)
            pool.memset(qx[:, :, :, :], 0.0).then_inc(s_setup, 1)
            pool.memset(pB[:, :, :], 0.0).then_inc(s_setup, 1)
            pool.memset(amax[:, :], 0.0).then_inc(s_setup, 1)
            for e in (pe, dve, act, pool):
                e.wait_ge(s_const, 16 * n_const)
                e.wait_ge(s_setup, 5)

            cos, sin = rope[:, 0:P], rope[:, P:2 * P]
            for c, (dst, src, np_) in enumerate([(wqs[:, 0, :], wraw[:, 0, :], P), (wqs[:, 1, :], wraw[:, 1, :], P),
                                                 (wlb[0:64, :], wraw[0:64, 2, :], 64)]):
                s4 = src.rearrange("p (n t) -> p t n", t=2)
                d4 = dst.rearrange("p (n t) -> p t n", t=2)
                tmp = t3[0:np_, 0, 0:P]
                tmp2 = t3[0:np_, 0, P:2 * P]
                dchain.link(dve.tensor_tensor(tmp, s4[:, 1, :], sin[0:np_], ALU.mult))
                dchain.link(dve.tensor_tensor(tmp2, s4[:, 0, :], cos[0:np_], ALU.mult))
                dchain.link(dve.tensor_tensor(d4[:, 0, :], tmp2, tmp, ALU.subtract))
                dchain.link(dve.tensor_tensor(tmp, s4[:, 0, :], sin[0:np_], ALU.mult))
                dchain.link(dve.tensor_tensor(tmp2, s4[:, 1, :], cos[0:np_], ALU.mult))
                last = dve.tensor_tensor(d4[:, 1, :], tmp2, tmp, ALU.add)
                if c < 2:
                    dchain.link(last)
            last.then_inc(s_w0, 1)
            for e in (pe, dve):
                e.wait_ge(s_w0, 1)
            dchain.reset()

            A, B = Stage(nc, sem, "A", plan), Stage(nc, sem, "B", plan)

            def stage_a(i):
                A.begin(i)
                A.wait(sp, "xb", 1)
                sp.dma_start(xin[:, :], a["x"][bass.ds(i, 1)].rearrange("a p n -> (a p) n")).then_inc(s_x, 16)
                A.wait(sp, "v3", 1)
                sp.dma_start(cT[:, :, :], a["ctx"][bass.ds(i, 1)].rearrange("a p c n -> (a p) c n")).then_inc(s_c, 16)
                A.wait(act, "mb", 1)
                act.dma_start(mk[:, :], bc(a["mask"][bass.ds(i, 1)], 0, P)).then_inc(s_m, 16)
                dve.wait_ge(s_x, (i + 1) * 16)
                dchain.link(dve.bn_stats(stA[:, 0:6], xin[:, :]))
                dchain.link(dve.bn_aggr(stA[:, 6:8], stA[:, 0:6]))
                A.done("dve", dve.tensor_scalar(stA[:, 8:9], stA[:, 7:8], 1e-5, None, ALU.add), "var")
                A.wait(pool, "var")
                A.done("pool", pool.tensor_tensor(stA[:, 9:10], stA[:, 8:9], small[:, 0:1], ALU.pow), "rstd")
                A.wait(dve, "rstd")
                A.wait(dve, "xnT", 1)
                A.done("dve", dve.tensor_scalar(xnA[:, :], xin[:, :], stA[:, 6:7], stA[:, 9:10], ALU.subtract, ALU.mult), "xn")
                A.wait(pool, "y", 1)
                A.wait(pool, "xn")
                A.done("pool", pool.tensor_tensor(xb[:, :], xin[:, :], bo0[:, :], ALU.add), "xb")
                yield
                A.wait(pe, "xn")
                A.wait(pe, "oTe", 1)
                pe.transpose(bank[4][:, 0:P], xnA[:, 0:P], ident[:, :])
                A.done("pe", pe.transpose(bank[4][:, P:2 * P], xnA[:, P:2 * P], ident[:, :]), "xnT")
                A.wait(act, "xnT")
                A.wait(act, "q", 1)
                A.done("act", act.copy(xT[:, :, :], bank[4][:, 0:2 * P].rearrange("p (c n) -> p c n", c=2)), "xT")
                A.wait(pe, "xT")
                A.wait(pe, "y", 1)
                for m in range(4):
                    for c in range(2):
                        last = pe.matmul(bank[5][:, m * P:(m + 1) * P], wq0[:, c, m * P:(m + 1) * P], xT[:, c, :],
                                         start=(c == 0), stop=(c == 1))
                A.done("pe", last, "q")
                A.wait(act, "q")
                A.wait(act, "s3", 1)
                for h2 in range(2):
                    src = bank[5][64 * h2:64 * h2 + 64, :].rearrange("p (m b t) -> p b m t", m=4, b=2)
                    last = act.copy(qx[64 * h2:64 * h2 + 64, :, :, 64 * h2:64 * h2 + 64], src)
                A.done("act", last, "qx")
                yield
                pe.wait_ge(s_c, (i + 1) * 16)
                for m in range(4):
                    bk = bank[m % 2]
                    A.wait(pe, f"k{m - 2}e" if m >= 2 else f"o{m}", 0 if m >= 2 else 1)
                    for c in range(2):
                        last = pe.matmul(bk[:, :], wk0[:, c, m * P:(m + 1) * P], cT[:, c, :], start=(c == 0), stop=(c == 1))
                    A.done("pe", last, f"k{m}")
                    A.wait(act, f"k{m}")
                    if m == 0:
                        A.wait(act, "s3", 1)
                    A.done("act", act.copy(kT[:, m, :], bk[:, :]), f"k{m}e")
                yield
                dve.wait_ge(s_m, (i + 1) * 16)
                A.done("dve", dve.tensor_scalar(mb[:, :], mk[:, :], 1.0, -NEG, ALU.subtract, ALU.mult), "mb")
                A.wait(pe, "qx")
                for hp in range(4):
                    bk = bank[2 + hp % 2]
                    A.wait(pe, f"k{hp}e")
                    A.wait(pe, f"t{hp - 2}" if hp >= 2 else f"t{hp + 2}", 0 if hp >= 2 else 1)
                    for b in range(2):
                        last = pe.matmul(bk[:, 256 * b:256 * b + 256], qx[:, b, hp, :], kT[:, hp, 256 * b:256 * b + 256],
                                         start=True, stop=True)
                    A.done("pe", last, f"s{hp}")
                    A.wait(dve, f"s{hp}")
                    if hp == 0:
                        A.wait(dve, "mb")
                        A.wait(dve, "e3", 1)
                    A.wait(dve, f"pT{hp}", 1)
                    dchain.link(dve.memset(idle[:, 0:1], 0.0))
                    for b in range(2):
                        last = dve.tensor_tensor_reduce(sm[:, hp, 256 * b:256 * b + 256], bk[:, 256 * b:256 * b + 256],
                                                        mb[:, 256 * b:256 * b + 256], -0.125, -NEG, ALU.add, ALU.min,
                                                        nm[:, 2 * hp + b:2 * hp + b + 1])
                    A.done("dve", last, f"t{hp}")
                    A.wait(act, f"t{hp}")
                    if hp == 0:
                        A.wait(act, "rec", 1)
                    for b in range(2):
                        blk = sm[:, hp, 256 * b:256 * b + 256]
                        last = act.activation(blk, blk, ACT.Exp, bias=nm[:, 2 * hp + b:2 * hp + b + 1], scale=-1.0,
                                              accum_out=sums[:, 2 * hp + b:2 * hp + b + 1])
                    A.done("act", last, f"e{hp}")
                yield
                for c4 in range(4):
                    bk = bank[c4 % 2]
                    A.wait(pe, f"v{c4 - 2}e" if c4 >= 2 else f"k{c4 + 2}e")
                    for c in range(2):
                        last = pe.matmul(bk[:, :], cT[:, c, c4 * P:(c4 + 1) * P], wv0[:, c, :], start=(c == 0), stop=(c == 1))
                    A.done("pe", last, f"v{c4}")
                    A.wait(dve, f"v{c4}")
                    if c4 == 0:
                        A.wait(dve, "o1", 1) if False else A.wait(dve, "pv1", 1)
                    A.done("dve", dve.tensor_copy(vv[:, c4, :], bk[:, :]), f"v{c4}e")
                yield
                for hp in range(4):
                    bk = bank[4 + hp % 2]
                    A.wait(pe, f"e{hp}")
                    A.wait(pe, {0: "xT", 1: "qx", 2: "pT0e", 3: "pT1e"}[hp])
                    for q in range(4):
                        last = pe.transpose(bk[:, q * P:(q + 1) * P], sm[:, hp, q * P:(q + 1) * P], ident[:, :])
                    A.done("pe", last, f"pT{hp}")
                    eng, en = (act, "act") if hp % 2 else (dve, "dve")
                    A.wait(eng, f"pT{hp}")
                    if hp < 2:
                        A.wait(eng, "pv1", 1)
                    copy = act.copy if hp % 2 else dve.tensor_copy
                    A.done(en, copy(pT[:, hp, :], bk[:, :]), f"pT{hp}e")
                yield
                A.wait(dve, "e3")
                A.wait(dve, "o1", 1)
                A.done("dve", dve.reciprocal(rec[:, :], sums[:, :]), "rec")
                A.wait(pe, "pT3e")
                A.wait(pe, "pT2e")
                for b in range(2):
                    A.wait(pe, f"v{b + 2}e")
                    for hp in range(4):
                        for kc in range(2):
                            q = 2 * b + kc
                            last = pe.matmul(bank[b][:, hp * P:(hp + 1) * P], pT[:, hp, q * P:(q + 1) * P],
                                             vv[:, q, hp * P:(hp + 1) * P], start=(kc == 0), stop=(kc == 1))
                    A.done("pe", last, f"pv{b}")
                    A.wait(dve, f"pv{b}")
                    if b == 0:
                        A.wait(dve, "rec")
                        A.wait(dve, "oT", 1)
                    for h2 in range(2):
                        r = slice(64 * h2, 64 * h2 + 64)
                        src = bank[b][r, :].rearrange("p (m n) -> p m n", m=4)[:, :, 64 * h2:64 * h2 + 64]
                        w = bc(rec[r, b:8:2].rearrange("p (m o) -> p m o", o=1), 2, 64)
                        last = dve.tensor_tensor(oA[64 * b:64 * b + 64, :, h2, :], src, w, ALU.mult)
                    A.done("dve", last, f"o{b}")
                yield
                A.wait(pe, "o1")
                A.wait(pe, "pT2e")
                for m in range(4):
                    last = pe.transpose(bank[4][:, m * P:(m + 1) * P], oA[:, m, :, :].rearrange("p a n -> p (a n)"), ident[:, :])
                A.done("pe", last, "oT")
                A.wait(act, "oT")
                A.wait(act, "yp", 1)
                A.done("act", act.copy(oT[:, :, :], bank[4][:, :].rearrange("p (m n) -> p m n", m=4)), "oTe")
                A.wait(pe, "oTe")
                A.wait(pe, "pT3e")
                for m in range(4):
                    last = pe.matmul(bank[5][:, 0:DIM], oT[:, m, :], wo0[:, m, :], start=(m == 0), stop=(m == 3))
                A.done("pe", last, "yp")
                A.wait(dve, "yp")
                A.wait(dve, "xb")
                B.wait(dve, "xr", idx=i - 1)
                A.done("dve", dve.tensor_tensor(xB[:, :], bank[5][:, 0:DIM], xb[:, :], ALU.add), "y")
                A.end()

            def stage_b(j):
                B.begin(j)
                A.wait(dve, "y", idx=j)
                dchain.link(dve.bn_stats(stB[:, 0:6], xB[:, :]))
                dchain.link(dve.bn_aggr(stB[:, 6:8], stB[:, 0:6]))
                B.done("dve", dve.tensor_scalar(stB[:, 8:9], stB[:, 7:8], 1e-5, None, ALU.add), "var")
                B.wait(pool, "var")
                B.done("pool", pool.tensor_tensor(stB[:, 9:10], stB[:, 8:9], small[:, 0:1], ALU.pow), "rstd")
                A.wait(act, "y", idx=j)
                B.wait(act, "x2", 1)
                B.done("act", act.copy(xr[:, :], xB[:, :]), "xr")
                B.wait(dve, "rstd")
                B.wait(dve, "xnT", 1)
                B.done("dve", dve.tensor_scalar(xnB[:, :], xB[:, :], stB[:, 6:7], stB[:, 9:10], ALU.subtract, ALU.mult), "xnB")
                B.wait(pe, "xnB")
                B.wait(pe, "x2", 1)
                pe.transpose(bank[6][:, 0:P], xnB[:, 0:P], ident[:, :])
                B.done("pe", pe.transpose(bank[6][:, P:2 * P], xnB[:, P:2 * P], ident[:, :]), "xnT")
                B.wait(act, "xnT")
                B.wait(act, "qk", 1)
                B.done("act", act.copy(xTB[:, :, :], bank[6][:, 0:2 * P].rearrange("p (c n) -> p c n", c=2)), "xT")
                yield
                B.wait(pe, "xT")
                B.wait(pe, "oTe", 1)
                for c in range(2):
                    last = pe.matmul(bank[7][:, 0:P], wla[:, c, :], xTB[:, c, :], start=(c == 0), stop=(c == 1))
                B.done("pe", last, "lat")
                B.wait(act, "lat")
                B.wait(act, "v", 1)
                B.done("act", act.copy(lat[:, :], bank[7][:, 0:P]), "late")
                for m in range(2):
                    for c in range(2):
                        pe.matmul(bank[6][:, m * P:(m + 1) * P], wqs[:, c, m * P:(m + 1) * P], xTB[:, c, :],
                                  start=(c == 0), stop=(c == 1))
                B.wait(pe, "late")
                for m in range(2):
                    last = pe.matmul(bank[6][:, 256 + m * P:256 + (m + 1) * P], wlb[0:64, m * P:(m + 1) * P], lat[0:64, :],
                                     start=True, stop=True)
                B.done("pe", last, "qk")
                last = pe.matmul(bank[7][:, 0:DIM], lat[64:128, :], wlb[64:128, :], start=True, stop=True)
                B.done("pe", last, "v")
                B.wait(act, "v")
                B.wait(act, "pv", 1)
                B.done("act", act.copy(vB[:, :], bank[7][:, 0:DIM]), "ve")
                B.wait(dve, "qk")
                B.wait(dve, "s3", 1)
                dve.tensor_copy(qTB[:, :, :], bank[6][:, 0:2 * P].rearrange("p (c n) -> p c n", c=2))
                for m in range(2):
                    src = bc(bank[6][:, 256 + m * P:256 + (m + 1) * P].rearrange("p (o n) -> p o n", o=1), 1, 8)
                    last = dve.tensor_tensor(kx[:, m, :, :], src, bc(head[:, :].rearrange("p (h o) -> p h o", o=1), 2, P), ALU.mult)
                B.done("dve", last, "kx")
                yield
                for c in range(4):
                    m, g = divmod(c, 2)
                    bk = bank[6 + c % 2]
                    B.wait(pe, {0: "kx", 1: "ve", 2: "d0", 3: "d1"}[c])
                    if c == 1:
                        B.wait(pe, "kx")
                    last = pe.matmul(bk[:, :], qTB[:, m, :], kx[:, m, 4 * g:4 * g + 4, :].rearrange("p h n -> p (h n)"),
                                     start=True, stop=True)
                    B.done("pe", last, f"s{c}")
                    B.wait(dve, f"s{c}")
                    hs = slice(4 * c, 4 * c + 4)
                    if c == 0:
                        B.wait(dve, "pT3", 1)
                    for b in range(2):
                        r = slice(64 * b, 64 * b + 64)
                        blk = bk[r, :].rearrange("p (h n) -> p h n", h=4)[:, :, 64 * b:64 * b + 64]
                        last = dve.tensor_reduce(negm[r, hs], blk, AX.X, ALU.max, negate=True)
                    dchain.link(last)
                    for b in range(2):
                        r = slice(64 * b, 64 * b + 64)
                        blk = bk[r, :].rearrange("p (h n) -> p h n", h=4)[:, :, 64 * b:64 * b + 64]
                        last = dve.tensor_tensor(pB[r, hs, 64 * b:64 * b + 64], blk,
                                                 bc(negm[r, hs].rearrange("p (h o) -> p h o", o=1), 2, 64), ALU.add)
                    B.done("dve", last, f"d{c}")
                    B.wait(act, f"d{c}")
                    for b in range(2):
                        r = slice(64 * b, 64 * b + 64)
                        blk = pB[r, hs, 64 * b:64 * b + 64]
                        last = act.activation(blk, blk, ACT.Exp, scale=0.25)
                    B.done("act", last, f"e{c}")
                yield
                for c in range(4):
                    hs = slice(4 * c, 4 * c + 4)
                    bk = bank[6 + c % 2]
                    B.wait(pe, f"e{c}")
                    B.wait(pe, {0: "d2", 1: "d3", 2: "pT0e", 3: "pT1e"}[c])
                    for h in range(4):
                        last = pe.transpose(bk[:, h * P:(h + 1) * P], pB[:, 4 * c + h, :], ident[:, :])
                    B.done("pe", last, f"pT{c}")
                    B.wait(act, f"pT{c}")
                    if c == 0:
                        B.wait(act, "pv", 1)
                    B.done("act", act.copy(pTB[:, hs, :], bk[:, :].rearrange("p (h n) -> p h n", h=4)), f"pT{c}e")
                    B.wait(dve, f"e{c}")
                    if c == 0:
                        B.wait(dve, "rec", 1)
                    for b in range(2):
                        r = slice(64 * b, 64 * b + 64)
                        last = dve.tensor_reduce(sB[r, hs], pB[r, hs, 64 * b:64 * b + 64], AX.X, ALU.add)
                B.done("dve", last, "sums")
                B.wait(dve, "sums")
                B.wait(dve, "oB", 1)
                B.done("dve", dve.reciprocal(recB[:, :], sB[:, :]), "rec")
                yield
                B.wait(pe, "pT3e")
                for h in range(H1):
                    last = pe.matmul(bank[6][:, h * D1:(h + 1) * D1], pTB[:, h, :], vB[:, h * D1:(h + 1) * D1], start=True, stop=True)
                B.done("pe", last, "pv")
                B.wait(dve, "pv")
                B.wait(dve, "rec")
                B.wait(dve, "oT", 1)
                B.done("dve", dve.tensor_tensor(oB[:, :].rearrange("p (h n) -> p h n", h=H1),
                                                bank[6][:, 0:DIM].rearrange("p (h n) -> p h n", h=H1),
                                                bc(recB[:, :].rearrange("p (h o) -> p h o", o=1), 2, D1), ALU.mult), "oB")
                yield
                B.wait(pe, "oB")
                B.wait(pe, "pT3e")
                for c in range(2):
                    last = pe.transpose(bank[7][:, c * P:(c + 1) * P], oB[:, c * P:(c + 1) * P], ident[:, :])
                B.done("pe", last, "oT")
                B.wait(act, "oT")
                B.wait(act, "yp", 1)
                B.done("act", act.copy(oTB[:, :, :], bank[7][:, 0:2 * P].rearrange("p (c n) -> p c n", c=2)), "oTe")
                B.wait(pe, "oTe")
                for c in range(2):
                    last = pe.matmul(bank[6][:, 0:DIM], oTB[:, c, :], wos[:, c, :], start=(c == 0), stop=(c == 1))
                B.done("pe", last, "yp")
                B.wait(dve, "yp")
                B.wait(dve, "xr")
                B.wait(dve, "keep", 1)
                B.done("dve", dve.tensor_tensor(x2[:, :], bank[6][:, 0:DIM], xr[:, :], ALU.add), "x2")
                B.wait(dve, "x2")
                dchain.link(dve.bn_stats(stB[:, 0:6], x2[:, :]))
                dchain.link(dve.bn_aggr(stB[:, 6:8], stB[:, 0:6]))
                B.done("dve", dve.tensor_scalar(stB[:, 8:9], stB[:, 7:8], 1e-5, None, ALU.add), "var2")
                B.wait(pool, "var2")
                B.done("pool", pool.tensor_tensor(stB[:, 9:10], stB[:, 8:9], small[:, 0:1], ALU.pow), "rstd2")
                B.wait(dve, "rstd2")
                dchain.link(dve.tensor_scalar(stB[:, 10:11], stB[:, 7:8], stB[:, 9:10], stB[:, 9:10], ALU.mult, ALU.mult))
                B.done("dve", dve.tensor_scalar(stB[:, 11:12], stB[:, 10:11], 1e-3, None, ALU.add), "var3")
                B.wait(pool, "var3")
                B.done("pool", pool.tensor_tensor(stB[:, 12:13], stB[:, 11:12], small[:, 0:1], ALU.pow), "rstd3")
                B.wait(dve, "rstd3")
                dchain.link(dve.tensor_scalar(t3[:, 0, :], x2[:, :], stB[:, 6:7], stB[:, 9:10], ALU.subtract, ALU.mult))
                dchain.link(dve.scalar_tensor_tensor(out=t3[:, 1, :], in0=t3[:, 0, :], scalar=stB[:, 12:13], in1=gam[:, :],
                                                     op0=ALU.mult, op1=ALU.mult))
                dchain.link(dve.tensor_tensor(t3[:, 0, :], t3[:, 1, :], bet[:, :], ALU.add))
                dchain.link(dve.tensor_reduce(amax[:, 1:2], t3[:, 0, :], AX.X, ALU.max, apply_absolute_value=True))
                dchain.link(dve.tensor_tensor(amax[:, 0:1], amax[:, 0:1], amax[:, 1:2], ALU.max))
                B.done("dve", dve.tensor_copy(XN[:, bass.ds(j, 1), :].rearrange("p a n -> p (a n)"), t3[:, 0, :]), "xn3")
                B.wait(act, "x2")
                B.done("act", act.copy(X[:, bass.ds(j, 1), :].rearrange("p a n -> p (a n)"), x2[:, :]), "keep")
                B.wait(dve, "xn3")
                B.end()

            def step(s, do_a, do_b):
                ga = stage_a(s) if do_a else iter(())
                gb = stage_b(s - 1) if do_b else iter(())
                for which in "BAABABABABABABABAB":
                    next(gb if which == "B" else ga, None)
                for g in (ga, gb):
                    for _ in g:
                        pass
                dchain.reset()

            step(0, True, False)
            with nc.Fori(1, TILES, 1) as s:
                step(s, True, True)
            step(TILES, False, True)
            B.wait(dve, "keep", idx=TILES - 1)
            B.wait(pool, "xn3", idx=TILES - 1)
            B.wait(pool, "keep", idx=TILES - 1)
        nc.all_engine_barrier()
        if upto >= 2:
            slots, wts, shift = sb("slots", [P, TILES, EXPERTS]), sb("wts", [P, TILES, TOPK]), sb("shift", [P, EXPERTS])
            todo_row = sb("todo_row", [1, 3 * P * 2], U32)
            slots_d = nc.dram_tensor("slots_d", (ROWS, 1), U32, kind="Internal").ap()
            xf_d = nc.dram_tensor("xf_d", (TILES, P, DIM), F32, kind="Internal").ap()
            todo_d = nc.dram_tensor("todo_d", (3 * P, 2), U32, kind="Internal").ap()
            y_d = nc.dram_tensor("y_d", (BLOCKS * P, DIM), F32, kind="Internal").ap()
            phase2(nc, a, plan, (slots, wts, shift, todo_row, slots_d, xf_d, todo_d), sem, bank, X, XN, ident, head, small, idle, dchain, amax, pool_waits, carrier, upto)

        if upto >= 3:
            experts(nc, a, plan, sem, bank, ident, todo_row, slots_d, xf_d, y_d, pool_waits, carrier)
            combine(nc, plan, sem, X, slots, shift, wts, y_d, out, dchain, pool_waits, carrier)
            return
        s_out = sem("s_out")
        sp.dma_start(out.rearrange("(t p) n -> p t n", p=P), X[:, :, :]).then_inc(s_out, 16)
        sp.wait_ge(s_out, 16)


def lay_out(i):
    c = np.ascontiguousarray
    t = lambda k: c(np.asarray(i[k]).T)
    ctx = np.asarray(i["ctx_768"]).reshape(TILES, 512, 2, CW)
    d = {
        "x": np.asarray(i["x"]).reshape(TILES, P, DIM),
        "ctx": c(ctx.transpose(0, 3, 2, 1)),
        "mask": np.asarray(i["mask_BxS2_bk0"]).reshape(TILES, 512),
        "wq0": np.asarray(i["L0_xattn_W_q"]), "wk0": np.asarray(i["L0_xattn_W_k"]), "wv0": np.asarray(i["L0_xattn_W_v"]),
        "wo0": np.asarray(i["L0_xattn_W_o"]), "bo0": np.asarray(i["L0_xattn_b_o"]),
        "wqs": t("L0_attn_wq"), "wka": t("L0_attn_wk_a"), "wkb": t("L0_attn_wk_b"), "wva": t("L0_attn_wv_a"),
        "wvb": t("L0_attn_wv_b"), "wos": t("L0_attn_wo"),
        "gam": np.asarray(i["L0_ffn_ln_gamma"]), "bet": np.asarray(i["L0_ffn_ln_beta"]),
    }
    for k, v in {"wf": "L0_ffn_weight", "bqd": "L1_xattn_bq", "bkd": "L1_xattn_bk", "bvd": "L1_xattn_bv", "bod": "L1_xattn_bo",
                 "lns": "L1_attn_ln_scale", "lnb": "L1_attn_ln_bias", "wh": "L1_attn_W_hidden", "bh": "L1_attn_b_hidden",
                 "wqk": "L1_attn_W_qk", "bqk": "L1_attn_b_qk", "wout": "L1_attn_W_out", "bout": "L1_attn_b_out"}.items():
        d[k] = np.asarray(i[v])
    for k, v in {"wqd": "L1_xattn_Wq", "wkd": "L1_xattn_Wk", "wvd": "L1_xattn_Wv", "wod": "L1_xattn_Wo",
                 "wgs": "L1_ffn_w_gate_shared", "wds": "L1_ffn_w_down_shared"}.items():
        d[k] = t(v)
    d["osw"], d["osb"] = np.asarray(i["L1_attn_os_weight"]), np.asarray(i["L1_attn_os_bias"])
    for k in ("bqd", "bkd", "bqk", "osw", "osb"):
        d[k] = c(d[k].reshape(-1, P).T)
    d["wr"], d["be"] = t("L1_ffn_router_w"), np.asarray(i["L1_ffn_expert_bias"])
    gate = np.asarray(i["L1_ffn_w_gate"]).reshape(EXPERTS, INTER, 2, P).transpose(0, 3, 2, 1).reshape(EXPERTS, P, 2 * INTER)
    down = np.asarray(i["L1_ffn_w_down"]).transpose(0, 2, 1)
    d["wexp"] = np.concatenate([gate, down], axis=2)
    d.update(constants())
    return d


def kernel(**inputs):
    import concourse.bacc as bacc
    from concourse.bass_utils import run_bass_kernel_spmd

    arrays = lay_out(inputs)
    plan = {}
    for _ in range(2):
        nc = bacc.Bacc("TRN2", target_bir_lowering=False, num_devices=1)
        a = {n: nc.dram_tensor(f"in_{n}", v.shape, mybir.dt.from_np(v.dtype), kind="ExternalInput").ap() for n, v in arrays.items()}
        out = nc.dram_tensor("out", (TOKENS, DIM), F32, kind="ExternalOutput").ap()
        program(nc, a, out, plan)
    r = run_bass_kernel_spmd(nc, [{f"in_{n}": v for n, v in arrays.items()}], core_ids=[0])
    return r.results[0]["out"].reshape(BATCHES, SEQ, DIM)
```

```python
from contextlib import ExitStack
from math import sqrt

import numpy as np
import concourse.bass as bass
from concourse import mybir

F32 = mybir.dt.float32
I32 = mybir.dt.int32
U32 = mybir.dt.uint32
U8 = mybir.dt.uint8
ALU = mybir.AluOpType
ACT = mybir.ActivationFunctionType
AX = mybir.AxisListType

P = 128
BATCHES, SEQ, DIM = 32, 64, 256
CTX, CDIM = 256, 192
TILES = BATCHES * SEQ // P
CW = CDIM // 2
H0, D0 = 8, 64
H1, D1 = 16, 16
TOKENS = BATCHES * SEQ
EXPERTS, TOPK, INTER = 160, 8, 128
BLOCKS = -(-((TOKENS * TOPK + EXPERTS * (P - 1)) // P) // 4) * 4
REGION = TOKENS // P
ROWS = (EXPERTS * REGION + BLOCKS) * P
NOBODY = 1 << 20
NEG = -3.4028234663852886e38


class Stage:

    def __init__(self, nc, sem, name, plan):
        self.nc, self.name, self.plan = nc, name, plan
        self.engines = {"pe": nc.tensor, "dve": nc.vector, "act": nc.scalar, "pool": nc.gpsimd}
        self.sem = {e: sem(f"{name}_{e}") for e in self.engines}
        self.per, self.at = plan.get(name, ({e: 0 for e in self.engines}, {}))
        self.n = {}
        for e, eng in self.engines.items():
            if self.per[e]:
                eng.sem_inc(self.sem[e], self.per[e])

    def begin(self, idx):
        self.idx, self.n, self.seen = idx, {e: 0 for e in self.engines}, {}

    def end(self):
        self.plan[self.name] = (dict(self.n), dict(self.seen))

    def done(self, e, ins, event):
        self.n[e] += 1
        assert event not in self.seen, event
        self.seen[event] = (e, self.n[e])
        ins.then_inc(self.sem[e], 1)

    def wait(self, eng, event, back=0, idx=None):
        e, k = self.at.get(event, ("pe", 1))
        idx = self.idx if idx is None else idx
        eng.wait_ge(self.sem[e], (idx + (1 - back)) * self.per[e] + k)


class Steps:

    MARGIN = 8

    def __init__(self, nc, sem, name):
        self.engines = {"pe": nc.tensor, "dve": nc.vector, "act": nc.scalar}
        self.sem = {e: sem(f"{name}_{e}") for e in self.engines}
        for e, eng in self.engines.items():
            eng.sem_inc(self.sem[e], self.MARGIN)

    def done(self, e, ins):
        ins.then_inc(self.sem[e], 1)

    def wait(self, eng, e, b):
        eng.wait_ge(self.sem[e], b + 1 + self.MARGIN)


class Chain:

    def __init__(self, nc, ctx, eng, name):
        self.eng, self.sem, self.n = eng, ctx.enter_context(nc.semaphore(name)), 0

    def link(self, ins):
        self.n += 1
        ins.then_inc(self.sem, 1)
        self.eng.wait_ge(self.sem, self.n)

    def reset(self):
        if self.n:
            self.eng.sem_clear(self.sem)
        self.n = 0


def constants():
    ident = np.eye(P, dtype=np.float32)
    inv = 1.0 / 10000.0 ** (np.arange(0, D1, 2, dtype=np.float32) / D1)
    ang = np.arange(H1, dtype=np.float32)[:, None] * inv[None, :].astype(np.float32)
    rope = np.stack([np.cos(ang), np.sin(ang)]).astype(np.float32).reshape(1, 2 * P)
    return {
        "c_ident": ident, "c_head": (np.arange(P)[:, None] // D1 % 2 == np.arange(2)[None, :]).astype(np.float32), "c_rope": rope,
        "c_tri": np.triu(np.ones((P, P), np.float32), 1),
        "c_ones": np.ones((P, P), np.float32),
        "c_base": (np.arange(EXPERTS, dtype=np.float32) * TOKENS + 1)[None, :],
        "c_steps": (np.arange(3)[None, :] + 3 * np.arange(P)[:, None]).astype(np.float32),
        "c_tokens": (np.arange(TILES)[None, :] * P + np.arange(P)[:, None]).astype(np.uint32),
    }


def bc(ap, axis, n):
    shape = list(ap.shape)
    shape[axis] = n
    return ap.broadcast_to(shape)


def phase2(nc, a, plan, routes, sem, bank, X, XN, ident, head, small, idle, dchain, amax, pool_waits, carrier, upto):
    slots, wts, shift, who, todo_row, slots_d, xf_d, todo_d = routes
    pe, dve, act, pool, sp = nc.tensor, nc.vector, nc.scalar, nc.gpsimd, nc.sync
    ph = ExitStack()
    with ph:
        def sb(name, shape, dt=F32):
            return ph.enter_context(nc.sbuf_tensor(name, shape, dt))

        s_const = sem("s_const2")
        n_const = 0

        def const(dst, src):
            nonlocal n_const
            sp.dma_start(dst, src).then_inc(s_const, 16)
            n_const += 1

        def weights(name, rows, cols, p=P):
            w = sb(name, [p, rows // p, cols])
            const(w[:, :, :], a[name].rearrange("(c p) n -> p c n", p=p))
            return w

        def spread(name, n):
            w = sb(name, [P, n])
            const(w[:, :], bc(a[name].rearrange("(a n) -> a n", a=1), 0, P))
            return w

        def column(name, n):
            w = sb(name, [P, n])
            const(w[:, :], a[name])
            return w

        wf = weights("wf", DIM, DIM)
        wqd, wod = weights("wqd", DIM, DIM), weights("wod", DIM, DIM)
        wkd, wvd = weights("wkd", CDIM, DIM, CW), weights("wvd", CDIM, DIM, CW)
        bqd, bkd = column("bqd", 2), column("bkd", 2)
        bvd, bod = spread("bvd", DIM), spread("bod", DIM)
        lns, lnb = spread("lns", DIM), spread("lnb", DIM)
        wh, bh = weights("wh", DIM, 1024), spread("bh", 1024)
        wqk, bqk = weights("wqk", DIM, P), column("bqk", 1)
        osw, osb = column("osw", 2), column("osb", 2)
        wout, bout = weights("wout", 512, DIM), spread("bout", DIM)
        wgs, wds = weights("wgs", DIM, P), weights("wds", P, DIM)
        wr, be = weights("wr", DIM, EXPERTS), spread("be", EXPERTS)
        tri, ones = weights("c_tri", P, P), weights("c_ones", P, P)
        base = sb("base", [P, EXPERTS])
        const(base[:, :], bc(a["c_base"], 0, P))
        tokens = sb("tokens", [P, TILES], U32)
        const(tokens[:, :], a["c_tokens"])

        tern = sb("tern", [P, 2, DIM])
        tmp = sb("tmp", [P, 2, DIM])
        sc = sb("sc", [P, 8])
        s_set = sem("s_set2")

        cT = sb("cT2", [CW, 2, 512])
        s_c = sem("s_c2")
        xq = sb("xq", [P, DIM])
        xqT = sb("xqT", [P, 2, P])
        x3 = sb("x3", [P, DIM])
        stC = sb("stC", [P, 16])
        xnC = sb("xnC", [P, DIM])
        xbC = sb("xbC", [P, DIM])
        xT = sb("xTC", [P, 2, P])
        qT = sb("qTC", [P, 2, P])
        qx = sb("qxC", [P, 2, 2, 2, 64])
        kT = sb("kTC", [P, 2, 512])
        vv = sb("vvC", [P, 4, DIM])
        ex = sb("ex", [P, 8, 512])
        nm = sb("nmC", [P, 8, 2])
        pT = sb("pTC", [P, 8, 512])
        dn = sb("dn", [P, 4, DIM])
        oT = sb("oTC", [P, 2, P])
        x4 = sb("x4", [P, DIM])

        x4r = sb("x4r", [P, DIM])
        xbE = sb("xbE", [P, DIM])
        stE = sb("stE", [P, 16])
        xnE = sb("xnE", [P, 2, DIM])
        xTE = sb("xTE", [P, 2, P])
        th = sb("th", [P, 1024])
        uu = sb("uu", [P, 1024])
        hid = sb("hid", [P, 1024])
        qk = sb("qk", [P, 4, P])
        qk2 = sb("qk2", [P, P])
        rel = sb("rel", [P, P])
        att = sb("att", [P, P])
        og = sb("og", [P, 512])
        ogT = sb("ogT", [P, 4, P])
        x5 = sb("x5", [P, DIM])
        xf = sb("xf", [P, DIM])
        xfT = sb("xfT", [P, 2, P])
        ths = sb("ths", [P, P])
        hs = sb("hs", [P, P])
        lg = sb("lg", [P, EXPERTS])
        ez = sb("ez", [P, EXPERTS])
        pr = sb("pr", [P, EXPERTS])
        sel = sb("sel", [P, EXPERTS])
        comb = sb("comb", [P, EXPERTS])
        before = sb("before", [P, EXPERTS])
        junk = sb("junk", [P, TOPK, EXPERTS])
        top = sb("top", [P, 4, 8])
        slot_id = sb("slot_id", [P, 8], U32)
        tok_id = sb("tok_id", [P, 1], U32)
        ones_e = sb("ones_e", [P, EXPERTS])
        mark = sb("mark", [P, ROWS // P], U32)
        s_mark, s_xf, s_sc = sem("s_mark"), sem("s_xf"), sem("s_sc")

        pool.memset(idle[:, :], 0.0).then_inc(s_set, 1)
        pool.memset(rel[:, :], 0.0).then_inc(s_set, 1)
        pool.memset(before[:, :], 0.0).then_inc(s_set, 1)
        dve.memset(ones_e[:, :], 1.0).then_inc(s_set, 1)
        pool.memset(mark[:, :], NOBODY).then_inc(s_set, 1)
        for e in (pe, dve, act, pool, sp):
            e.wait_ge(s_const, 16 * n_const)
            e.wait_ge(s_set, 5)
        sp.dma_start(slots_d.rearrange("(p n) o -> p (n o)", p=P), mark[:, :]).then_inc(s_mark, 16)
        pool.wait_ge(s_mark, 16)
        dve.tensor_reduce(sc[:, 0:1], wf[:, :, :], AX.XY, ALU.add, apply_absolute_value=True).then_inc(s_set, 1)
        pool.wait_ge(s_set, 6)
        radd, rmax = bass.bass_isa.ReduceOp.add, bass.bass_isa.ReduceOp.max
        pool.partition_all_reduce(sc[:, 1:2], sc[:, 0:1], P, radd).then_inc(s_set, 1)
        pool.partition_all_reduce(sc[:, 2:3], amax[:, 0:1], P, rmax).then_inc(s_set, 1)
        dve.wait_ge(s_set, 8)
        link = dchain.link
        link(dve.tensor_scalar(sc[:, 1:2], sc[:, 1:2], 1.0 / (DIM * DIM), None, ALU.mult))
        link(dve.tensor_scalar(sc[:, 5:6], sc[:, 1:2], 1e-5, None, ALU.add))
        link(dve.reciprocal(sc[:, 6:7], sc[:, 5:6]))
        link(dve.tensor_scalar(tmp[:, :, :], wf[:, :, :], sc[:, 6:7], None, ALU.mult))
        link(dve.tensor_scalar(tern[:, :, :], tmp[:, :, :], 0.5, None, ALU.is_gt))
        link(dve.tensor_scalar(tmp[:, :, :], tmp[:, :, :], -0.5, None, ALU.is_lt))
        link(dve.tensor_tensor(tern[:, :, :], tern[:, :, :], tmp[:, :, :], ALU.subtract))
        link(dve.reciprocal(sc[:, 3:4], sc[:, 2:3]))
        link(dve.tensor_scalar(sc[:, 3:4], sc[:, 3:4], 128.0, None, ALU.mult))
        link(dve.tensor_scalar(sc[:, 4:5], sc[:, 2:3], sc[:, 1:2], 1.0 / 128, ALU.mult, ALU.mult))
        link(dve.tensor_scalar(bqd[:, :], bqd[:, :], 0.25, None, ALU.mult))
        dve.tensor_scalar(bqk[:, :], bqk[:, :], 0.5, None, ALU.mult).then_inc(s_set, 1)
        for e in (pe, dve, act, pool):
            e.wait_ge(s_set, 9)
        dchain.reset()

        C, E = Stage(nc, sem, "C", plan), Stage(nc, sem, "E", plan)

        def moments(S, st, x, tag):
            link(dve.bn_stats(st[:, 0:6], x))
            link(dve.bn_aggr(st[:, 6:8], st[:, 0:6]))
            S.done("dve", dve.tensor_scalar(st[:, 8:9], st[:, 7:8], 1e-5, None, ALU.add), f"var{tag}")
            S.wait(pool, f"var{tag}")
            S.done("pool", pool.tensor_tensor(st[:, 9:10], st[:, 8:9], small[:, 0:1], ALU.pow), f"rstd{tag}")
            S.wait(dve, f"rstd{tag}")

        def halves(b):
            return b[:, 0:2 * P].rearrange("p (c n) -> p c n", c=2)

        def stage_c(i):
            C.begin(i)
            C.wait(sp, "v1", 1)
            sp.dma_start(cT[:, :, :], a["ctx"][bass.ds(i, 1)].rearrange("a p c n -> (a p) c n")).then_inc(s_c, 16)
            pe.wait_ge(s_c, (i + 1) * 16)
            for m in range(2):
                C.wait(pe, "own", 1)
                for c in range(2):
                    last = pe.matmul(bank[m][:, :], wkd[:, c, m * P:(m + 1) * P], cT[:, c, :], start=(c == 0), stop=(c == 1))
                C.done("pe", last, f"k{m}")
                C.wait(act, f"k{m}")
                C.wait(act, "s7", 1)
                C.done("act", act.activation(kT[:, m, :], bank[m][:, :], ACT.Identity, bias=bkd[:, m:m + 1]), f"k{m}e")
            lim = float(np.float32(128.0 - 1e-5))
            C.wait(dve, "xqT", 1)
            link(dve.tensor_scalar(xq[:, :], XN[:, bass.ds(i, 1), :].rearrange("p a n -> p (a n)"), sc[:, 3:4], lim, ALU.mult, ALU.min))
            C.done("dve", dve.tensor_scalar(xq[:, :], xq[:, :], -lim, None, ALU.max), "xq")
            C.wait(pe, "xq")
            C.wait(pe, "pT6e", 1)
            for c in range(2):
                last = pe.transpose(bank[4][:, c * P:(c + 1) * P], xq[:, c * P:(c + 1) * P], ident[:, :])
            C.done("pe", last, "xqT")
            C.wait(act, "xqT")
            C.wait(act, "yc", 1)
            C.done("act", act.copy(xqT[:, :, :], halves(bank[4])), "xqTe")
            yield
            C.wait(pe, "xqTe")
            for c in range(2):
                last = pe.matmul(bank[4][:, DIM:512], xqT[:, c, :], tern[:, c, :], start=(c == 0), stop=(c == 1))
            C.done("pe", last, "yc")
            C.wait(dve, "yc")
            C.wait(dve, "xb", 1)
            C.done("dve", dve.scalar_tensor_tensor(out=x3[:, :], in0=bank[4][:, DIM:512], scalar=sc[:, 4:5],
                                                   in1=X[:, bass.ds(i, 1), :].rearrange("p a n -> p (a n)"),
                                                   op0=ALU.mult, op1=ALU.add), "x3")
            C.wait(dve, "x3")
            moments(C, stC, x3[:, :], "")
            C.wait(dve, "xnT", 1)
            C.done("dve", dve.tensor_scalar(xnC[:, :], x3[:, :], stC[:, 6:7], stC[:, 9:10], ALU.subtract, ALU.mult), "xn")
            E.wait(pool, "x4", idx=i - 1)
            C.wait(pool, "xn")
            C.done("pool", pool.tensor_tensor(xbC[:, :], x3[:, :], bod[:, :], ALU.add), "xb")
            yield
            for m in range(2):
                C.wait(pe, f"k{m}e")
                for t2 in range(2):
                    q = 2 * m + t2
                    for c in range(2):
                        last = pe.matmul(bank[m][:, t2 * DIM:(t2 + 1) * DIM], cT[:, c, q * P:(q + 1) * P], wvd[:, c, :],
                                         start=(c == 0), stop=(c == 1))
                C.done("pe", last, f"v{m}")
                C.wait(dve, f"v{m}")
                C.wait(dve, "pv", 1)
                C.done("dve", dve.tensor_tensor(vv[:, 2 * m:2 * m + 2, :], bank[m][:, :].rearrange("p (c n) -> p c n", c=2),
                                                bc(bvd[:, :].rearrange("p (o n) -> p o n", o=1), 1, 2), ALU.add), f"v{m}e")
            yield
            C.wait(pe, "xn")
            C.wait(pe, "xqTe")
            for c in range(2):
                last = pe.transpose(bank[4][:, c * P:(c + 1) * P], xnC[:, c * P:(c + 1) * P], ident[:, :])
            C.done("pe", last, "xnT")
            C.wait(act, "xnT")
            C.wait(act, "q", 1)
            C.done("act", act.copy(xT[:, :, :], halves(bank[4])), "xT")
            yield
            C.wait(pe, "xT")
            E.wait(pe, "x4", idx=i - 1)
            for m in range(2):
                for c in range(2):
                    last = pe.matmul(bank[5][:, m * P:(m + 1) * P], wqd[:, c, m * P:(m + 1) * P], xT[:, c, :],
                                     start=(c == 0), stop=(c == 1))
            C.done("pe", last, "q")
            C.wait(act, "q")
            C.wait(act, "qx", 1)
            for m in range(2):
                last = act.activation(qT[:, m, :], bank[5][:, m * P:(m + 1) * P], ACT.Identity, bias=bqd[:, m:m + 1], scale=0.25)
            C.done("act", last, "qe")
            C.wait(dve, "qe")
            C.wait(dve, "s7", 1)
            hm = head[:, :].rearrange("p (a h o) -> p a h o", a=1, o=1)
            for m in range(2):
                last = dve.tensor_tensor(qx[:, m, :, :, :], bc(qT[:, m, :].rearrange("p (b o t) -> p b o t", b=2, o=1), 2, 2),
                                         bc(bc(hm, 1, 2), 3, 64), ALU.mult)
            C.done("dve", last, "qx")
            yield
            for u in range(8):
                m, hp = divmod(u, 4)
                bk = bank[2 + u % 2]
                rows = slice(32 * hp, 32 * hp + 32)
                if u == 0:
                    C.wait(pe, "qx")
                if hp == 0:
                    C.wait(pe, f"k{m}e")
                C.wait(pe, f"e{(u - 2) % 8}", 0 if u >= 2 else 1)
                for b in range(2):
                    last = pe.matmul(bk[:, 256 * b:256 * b + 256], qx[rows, m, b, :, :].rearrange("p h t -> p (h t)"),
                                     kT[rows, m, 256 * b:256 * b + 256], start=True, stop=True)
                C.done("pe", last, f"s{u}")
                C.wait(dve, f"s{u}")
                C.wait(dve, f"e{u}", 1)
                C.done("dve", dve.tensor_reduce(nm[:, u, :], bk[:, :].rearrange("p (b n) -> p b n", b=2), AX.X, ALU.max, negate=True), f"m{u}")
                C.wait(act, f"m{u}")
                C.wait(act, f"pT{u}", 1)
                for b in range(2):
                    last = act.activation(ex[:, u, 256 * b:256 * b + 256], bk[:, 256 * b:256 * b + 256], ACT.Exp,
                                          bias=nm[:, u, b:b + 1])
                C.done("act", last, f"e{u}")
                if u % 2:
                    yield
            for u in range(8):
                bk = bank[4 + u % 2]
                C.wait(pe, f"e{u}")
                C.wait(pe, {0: "xT", 1: "qe"}.get(u, f"pT{u - 2}e"))
                for q in range(4):
                    last = pe.transpose(bk[:, q * P:(q + 1) * P], ex[:, u, q * P:(q + 1) * P], ident[:, :])
                C.done("pe", last, f"pT{u}")
                eng, en = (act, "act") if u % 2 else (dve, "dve")
                C.wait(eng, f"pT{u}")
                if u < 2:
                    C.wait(eng, "pv", 1)
                copy = act.copy if u % 2 else dve.tensor_copy
                C.done(en, copy(pT[:, u, :], bk[:, :]), f"pT{u}e")
                if u == 3:
                    yield
            yield
            C.wait(pe, "pT6e")
            C.wait(pe, "pT7e")
            C.wait(pe, "v1e")
            for t, part in ((1, "den"), (0, "pv")):
                C.wait(pe, f"v{t}e")
                for m in range(2):
                    for b in range(2):
                        for kc in range(2):
                            q = 2 * b + kc
                            for hp in range(4):
                                u = 4 * m + hp
                                rows = slice(32 * hp, 32 * hp + 32)
                                dst = bank[t][rows, :].rearrange("p (h m b q) -> p m b h q", h=2, m=2, b=2)[:, m, b, :, :]
                                src = vv[:, q, 32 * u:32 * u + 32] if t == 0 else ones[:, 0, 0:32]
                                last = pe.matmul(dst, src, pT[:, u, q * P:(q + 1) * P].rearrange("p (h q) -> p h q", h=2),
                                                 start=(kc == 0), stop=(kc == 1))
                C.done("pe", last, part)
            C.wait(dve, "den")
            C.wait(dve, "ot", 1)
            link(dve.tensor_scalar(dn[:, 0, :], bank[1][:, 0:DIM], head[:, 0:1], None, ALU.mult))
            link(dve.scalar_tensor_tensor(out=dn[:, 1, :], in0=bank[1][:, DIM:512], scalar=head[:, 1:2], in1=dn[:, 0, :], op0=ALU.mult, op1=ALU.add))
            dve.reciprocal(dn[:, 0, :], dn[:, 1, :])
            C.wait(dve, "pv")
            link(dve.tensor_scalar(dn[:, 2, :], bank[0][:, 0:DIM], head[:, 0:1], None, ALU.mult))
            C.done("dve", dve.scalar_tensor_tensor(out=dn[:, 3, :], in0=bank[0][:, DIM:512], scalar=head[:, 1:2], in1=dn[:, 2, :],
                                                   op0=ALU.mult, op1=ALU.add), "own")
            C.wait(dve, "own")
            E.wait(dve, "yp", idx=i - 1)
            C.done("dve", dve.tensor_tensor(oT[:, :, :].rearrange("p c n -> p (c n)"), dn[:, 3, :], dn[:, 0, :], ALU.mult), "ot")
            C.end()

        def stage_e(j):
            E.begin(j)
            C.wait(pe, "ot", idx=j)
            C.wait(pe, "pT7e", idx=j)
            for c in range(2):
                last = pe.matmul(bank[5][:, 0:DIM], oT[:, c, :], wod[:, c, :], start=(c == 0), stop=(c == 1))
            E.done("pe", last, "yp")
            E.wait(dve, "yp")
            C.wait(dve, "xb", idx=j)
            E.wait(dve, "x4r0", 1)
            E.done("dve", dve.tensor_tensor(x4[:, :], bank[5][:, 0:DIM], xbC[:, :], ALU.add), "x4")
            E.wait(dve, "x4")
            moments(E, stE, x4[:, :], "a")
            link(dve.tensor_scalar(stE[:, 10:11], stE[:, 7:8], stE[:, 9:10], stE[:, 9:10], ALU.mult, ALU.mult))
            E.done("dve", dve.tensor_scalar(stE[:, 11:12], stE[:, 10:11], 1e-5, None, ALU.add), "var2")
            E.wait(pool, "var2")
            E.done("pool", pool.tensor_tensor(stE[:, 12:13], stE[:, 11:12], small[:, 0:1], ALU.pow), "rstd2")
            E.wait(dve, "rstd2")
            E.wait(dve, "xnT", 1)
            E.done("dve", dve.tensor_scalar(xnE[:, 0, :], x4[:, :], stE[:, 6:7], stE[:, 9:10], ALU.subtract, ALU.mult), "xc")
            E.wait(act, "x4")
            E.wait(act, "xbE", 1)
            E.done("act", act.copy(x4r[:, :], x4[:, :]), "x4r0")
            E.wait(dve, "xc")
            link(dve.scalar_tensor_tensor(out=xnE[:, 1, :], in0=xnE[:, 0, :], scalar=stE[:, 12:13], in1=lns[:, :], op0=ALU.mult, op1=ALU.mult))
            E.wait(dve, "x4r0")
            E.done("dve", dve.tensor_tensor(xnE[:, 0, :], xnE[:, 1, :], lnb[:, :], ALU.add), "x4r")
            E.wait(pool, "x5", 1)
            E.wait(pool, "x4r0")
            E.done("pool", pool.tensor_tensor(xbE[:, :], x4r[:, :], bout[:, :], ALU.add), "xbE")
            yield
            E.wait(pe, "x4r")
            E.wait(pe, "before", 1)
            for c in range(2):
                last = pe.transpose(bank[6][:, c * P:(c + 1) * P], xnE[:, 0, c * P:(c + 1) * P], ident[:, :])
            E.done("pe", last, "xnT")
            E.wait(act, "xnT")
            E.wait(act, "h1", 1)
            E.done("act", act.copy(xTE[:, :, :], halves(bank[6])), "xT")
            yield
            E.wait(pe, "xT")
            E.wait(pe, "x6", 1)
            for c in range(2):
                last = pe.matmul(bank[7][:, 0:P], wqk[:, c, :], xTE[:, c, :], start=(c == 0), stop=(c == 1))
            E.done("pe", last, "qk")
            E.wait(act, "qk")
            E.wait(act, "qke", 1)
            act.activation(qk[:, 1, :], bank[7][:, 0:P], ACT.Identity, bias=bqk[:, 0:1], scale=0.5)
            E.done("act", act.activation(qk[:, 0, :], bank[7][:, 0:P], ACT.Tanh, bias=bqk[:, 0:1], scale=0.5), "qku")
            E.wait(dve, "qku")
            E.wait(dve, "sim", 1)
            link(dve.scalar_tensor_tensor(out=qk2[:, :], in0=qk[:, 0, :], scalar=1.0, in1=qk[:, 1, :], op0=ALU.add, op1=ALU.mult))
            dve.tensor_scalar(qk[:, 2, :], qk2[:, :], osw[:, 0:1], osb[:, 0:1], ALU.mult, ALU.add)
            E.done("dve", dve.tensor_scalar(qk[:, 3, :], qk2[:, :], osw[:, 1:2], osb[:, 1:2], ALU.mult, ALU.add), "qke")
            for g in range(2):
                bk = bank[6 + g]
                E.wait(pe, "xT" if g == 0 else "qku")
                for c in range(2):
                    last = pe.matmul(bk[:, :], xTE[:, c, :], wh[:, c, 512 * g:512 * g + 512], start=(c == 0), stop=(c == 1))
                E.done("pe", last, f"h{g}")
                hs_ = slice(512 * g, 512 * g + 512)
                E.wait(dve, f"h{g}")
                E.wait(dve, f"hid{g}", 1)
                E.done("dve", dve.tensor_tensor(uu[:, hs_], bk[:, :], bh[:, hs_], ALU.add), f"u{g}")
                E.wait(act, f"u{g}")
                E.done("act", act.activation(th[:, hs_], uu[:, hs_], ACT.Tanh, scale=0.5), f"th{g}")
                E.wait(dve, f"th{g}")
                if g == 0:
                    E.wait(dve, "av", 1)
                else:
                    E.wait(dve, "og", 1)
                E.done("dve", dve.scalar_tensor_tensor(out=hid[:, hs_], in0=th[:, hs_], scalar=1.0, in1=uu[:, hs_], op0=ALU.add, op1=ALU.mult), f"hid{g}")
            yield
            E.wait(pe, "qke")
            E.wait(pe, "u0")
            E.done("pe", pe.matmul(bank[6][:, 0:P], qk[:, 3, :], qk[:, 2, :], start=True, stop=True), "sim")
            E.wait(dve, "sim")
            for b in range(2):
                r = slice(64 * b, 64 * b + 64)
                last = dve.tensor_scalar(rel[r, r], bank[6][r, r], 1.0 / SEQ, 0.0, ALU.mult, ALU.max)
            E.done("dve", last, "rel")
            E.wait(dve, "rel")
            E.wait(dve, "av", 1)
            E.done("dve", dve.tensor_tensor(att[:, :], rel[:, :], rel[:, :], ALU.mult), "att")
            yield
            E.wait(pe, "att")
            E.wait(pe, "hid0")
            E.wait(pe, "u1")
            E.done("pe", pe.matmul(bank[7][:, :], att[:, :], hid[:, 0:512], start=True, stop=True), "av")
            E.wait(dve, "av")
            E.wait(dve, "hid1")
            E.wait(dve, "ogT", 1)
            E.done("dve", dve.scalar_tensor_tensor(out=og[:, :], in0=bank[7][:, :], scalar=0.25, in1=hid[:, 512:1024], op0=ALU.mult, op1=ALU.mult), "og")
            yield
            E.wait(pe, "og")
            E.wait(pe, "rel")
            for c in range(4):
                last = pe.transpose(bank[6][:, c * P:(c + 1) * P], og[:, c * P:(c + 1) * P], ident[:, :])
            E.done("pe", last, "ogT")
            E.wait(act, "ogT")
            E.wait(act, "yo", 1)
            E.done("act", act.copy(ogT[:, :, :], bank[6][:, :].rearrange("p (c n) -> p c n", c=4)), "ogTe")
            yield
            E.wait(pe, "ogTe")
            for c in range(4):
                last = pe.matmul(bank[7][:, 0:DIM], ogT[:, c, :], wout[:, c, :], start=(c == 0), stop=(c == 3))
            E.done("pe", last, "yo")
            E.wait(dve, "yo")
            E.wait(dve, "xbE")
            E.wait(dve, "x6", 1)
            E.done("dve", dve.tensor_tensor(x5[:, :], bank[7][:, 0:DIM], xbE[:, :], ALU.add), "x5")
            E.wait(dve, "x5")
            moments(E, stE, x5[:, :], "f")
            E.wait(dve, "xfT", 1)
            dve.wait_ge(s_xf, j * 16)
            E.done("dve", dve.tensor_scalar(xf[:, :], x5[:, :], stE[:, 6:7], stE[:, 9:10], ALU.subtract, ALU.mult), "xf")
            yield
            E.wait(pe, "xf")
            E.wait(pe, "ogTe")
            for c in range(2):
                last = pe.transpose(bank[6][:, c * P:(c + 1) * P], xf[:, c * P:(c + 1) * P], ident[:, :])
            E.done("pe", last, "xfT")
            E.wait(act, "xfT")
            E.wait(act, "sh", 1)
            E.done("act", act.copy(xfT[:, :, :], halves(bank[6])), "xfTe")
            yield
            E.wait(pe, "xfTe")
            E.wait(pe, "x5")
            for c in range(2):
                last = pe.matmul(bank[7][:, 0:P], wgs[:, c, :], xfT[:, c, :], start=(c == 0), stop=(c == 1))
            E.done("pe", last, "sh")
            E.wait(act, "sh")
            E.wait(act, "hs", 1)
            E.done("act", act.activation(ths[:, :], bank[7][:, 0:P], ACT.Tanh, scale=0.5), "ths")
            E.wait(dve, "ths")
            E.wait(dve, "ys", 1)
            E.done("dve", dve.scalar_tensor_tensor(out=hs[:, :], in0=ths[:, :], scalar=1.0, in1=bank[7][:, 0:P], op0=ALU.add, op1=ALU.mult), "hs")
            yield
            E.wait(pe, "hs")
            E.done("pe", pe.matmul(bank[7][:, 0:DIM], hs[:, :], wds[:, 0, :], start=True, stop=True), "ys")
            E.wait(dve, "ys")
            E.done("dve", dve.scalar_tensor_tensor(out=X[:, bass.ds(j, 1), :].rearrange("p a n -> p (a n)"), in0=bank[7][:, 0:DIM],
                                                   scalar=0.5, in1=x5[:, :], op0=ALU.mult, op1=ALU.add), "x6")
            E.wait(sp, "xf")
            sp.dma_start(xf_d[bass.ds(j, 1)].rearrange("a p n -> (a p) n"), xf[:, :]).then_inc(s_xf, 16)
            yield
            E.wait(pe, "x6")
            for c in range(2):
                last = pe.matmul(bank[7][:, 0:EXPERTS], xfT[:, c, :], wr[:, c, :], start=(c == 0), stop=(c == 1))
            E.done("pe", last, "lg")
            E.wait(dve, "lg")
            E.done("dve", dve.tensor_tensor(lg[:, :], bank[7][:, 0:EXPERTS], be[:, :], ALU.add), "lge")
            E.wait(act, "lge")
            E.done("act", act.activation(ez[:, :], lg[:, :], ACT.Exp, scale=-1.0), "ez")
            E.wait(dve, "ez")
            E.done("dve", dve.tensor_scalar(ez[:, :], ez[:, :], 1.0, None, ALU.add), "ez1")
            E.wait(dve, "ez1")
            link(dve.reciprocal(pr[:, :], ez[:, :]))
            link(dve.max(top[:, 0, :], pr[:, :]))
            link(dve.match_replace(out=ez[:, :], in_to_replace=top[:, 0, :], in_values=pr[:, :], imm_value=-1.0))
            E.wait(dve, "before", 1)
            E.done("dve", dve.tensor_scalar(sel[:, :], ez[:, :], 0.0, None, ALU.is_lt), "sel")
            link(dve.tensor_reduce(top[:, 3, 0:1], top[:, 0, :], AX.X, ALU.add))
            link(dve.tensor_scalar(top[:, 3, 0:1], top[:, 3, 0:1], 1e-9, None, ALU.add))
            link(dve.reciprocal(top[:, 3, 1:2], top[:, 3, 0:1]))
            link(dve.tensor_scalar(top[:, 3, 1:2], top[:, 3, 1:2], 2.5, None, ALU.mult))
            E.wait(dve, "sel")
            link(dve.scalar_tensor_tensor(out=comb[:, :], in0=pr[:, :], scalar=top[:, 3, 1:2], in1=sel[:, :], op0=ALU.mult, op1=ALU.mult))
            yield
            E.wait(pe, "sel")
            E.wait(pe, "xfTe")
            E.wait(pe, "before", 1)
            pe.matmul(bank[6][:, 0:EXPERTS], tri[:, 0, :], sel[:, :], start=True, stop=False)
            E.done("pe", pe.matmul(bank[6][:, 0:EXPERTS], ones[:, 0, :], before[:, :], start=False, stop=True), "rank")
            E.wait(dve, "rank")
            link(dve.tensor_tensor(lg[:, :], bank[6][:, 0:EXPERTS], base[:, :], ALU.add))
            E.done("dve", dve.tensor_tensor(before[:, :], before[:, :], sel[:, :], ALU.add), "before")
            link(dve.tensor_tensor(lg[:, :], lg[:, :], sel[:, :], ALU.mult))
            link(dve.max(top[:, 1, :], lg[:, :]))
            for k in range(TOPK):
                last = dve.scalar_tensor_tensor(out=junk[:, k, :], in0=lg[:, :], scalar=top[:, 1, k:k + 1], in1=comb[:, :],
                                                op0=ALU.is_equal, op1=ALU.mult, accum_out=top[:, 2, k:k + 1])
            link(last)
            dve.wait_ge(s_sc, j * 16 * TOPK)
            dve.tensor_scalar(slot_id[:, :], top[:, 1, :], 1.0, None, ALU.subtract).then_inc(dchain.sem, 1)
            dchain.n += 1
            E.done("dve", dve.tensor_copy(tok_id[:, :], tokens[:, bass.ds(j, 1)]), "tok")
            dve.wait_ge(dchain.sem, dchain.n)
            E.done("dve", dve.tensor_copy(slots[:, bass.ds(j, 1), :].rearrange("p a n -> p (a n)"), lg[:, :]), "ids")
            E.done("dve", dve.tensor_copy(wts[:, bass.ds(j, 1), :].rearrange("p a n -> p (a n)"), top[:, 2, :]), "wts")
            E.wait(dve, "wts")
            link(dve.memset(idle[:, 0:1], 0.0))
            E.wait(pool, "ids")
            pool_waits.link(pool.tensor_tensor(carrier[:, 1:2], carrier[:, 0:1], carrier[:, 0:1], ALU.add))
            for k in range(TOPK):
                pool.indirect_dma_start(out=slots_d, out_offset=bass.IndirectOffsetOnAxis(ap=slot_id[:, k:k + 1], axis=0),
                                        in_=tok_id[:, 0:1], in_offset=None).then_inc(s_sc, 16)
            E.end()

        def step(s, do_c, do_e):
            gc = stage_c(s) if do_c else iter(())
            ge = stage_e(s - 1) if do_e else iter(())
            for which in "CECCECECECECECECECECEECE":
                next(ge if which == "E" else gc, None)
            for g in (gc, ge):
                for _ in g:
                    pass
            dchain.reset()
            pool_waits.reset()

        step(0, True, False)
        with nc.Fori(1, TILES, 1) as s:
            step(s, True, True)
        step(TILES, False, True)
        E.wait(pe, "before", idx=TILES - 1)
        s_pl = sem("s_plan")
        pe.matmul(bank[0][:, 0:EXPERTS], ones[:, 0, :], before[:, :], start=True, stop=True).then_inc(s_pl, 1)
        dve.wait_ge(s_pl, 1)
        blocks = sb("blocks", [P, EXPERTS], I32)
        bf = sb("bf", [P, EXPERTS])
        ends = sb("ends", [P, EXPERTS])
        steps = sb("steps", [P, 3])
        done = sb("done", [P, 3, EXPERTS])
        st = sb("st", [P, 3, 4])
        blk = sb("blk", [P, 3], U32)
        expert = sb("expert", [P, 3], U32)
        taken = sb("taken", [P, 3, P], U32)
        takenf = sb("takenf", [P, 3, P])
        sp.dma_start(steps[:, :], a["c_steps"]).then_inc(s_mark, 16)
        link(dve.tensor_scalar(blocks[:, :], bank[0][:, 0:EXPERTS], P - 1.0, None, ALU.add))
        link(dve.tensor_scalar(blocks[:, :], blocks[:, :], 7, None, ALU.logical_shift_right))
        link(dve.tensor_copy(bf[:, :], blocks[:, :]))
        link(dve.tensor_tensor_scan(ends[:, :], ones_e[:, :], bf[:, :], 0.0, ALU.mult, ALU.add))
        link(dve.tensor_tensor(bf[:, :], ends[:, :], bf[:, :], ALU.subtract))
        link(dve.scalar_tensor_tensor(out=bf[:, :], in0=bf[:, :], scalar=float(P), in1=base[:, :], op0=ALU.mult, op1=ALU.subtract))
        link(dve.tensor_scalar(shift[:, :], bf[:, :], 1.0, None, ALU.add))
        dve.wait_ge(s_mark, 32)
        for g in range(3):
            link(dve.tensor_scalar(done[:, g, :], ends[:, :], steps[:, g:g + 1], None, ALU.is_le))
            link(dve.tensor_reduce(st[:, g, 0:1], done[:, g, :], AX.X, ALU.add))
            link(dve.tensor_tensor(done[:, g, :], done[:, g, :], ends[:, :], ALU.mult))
            link(dve.tensor_reduce(st[:, g, 1:2], done[:, g, :], AX.X, ALU.max))
            link(dve.tensor_tensor(st[:, g, 2:3], steps[:, g:g + 1], st[:, g, 1:2], ALU.subtract))
            link(dve.scalar_tensor_tensor(out=blk[:, g:g + 1], in0=st[:, g, 0:1], scalar=float(REGION), in1=st[:, g, 2:3], op0=ALU.mult, op1=ALU.add))
            link(dve.tensor_scalar(expert[:, g:g + 1], st[:, g, 0:1], EXPERTS - 1.0, None, ALU.min))
        dve.memset(idle[:, 0:1], 0.0).then_inc(s_pl, 1)
        dchain.reset()
        sp.wait_ge(s_pl, 2)
        sp.dma_start(todo_d.rearrange("(p g) n -> p (g n)", p=P), expert[:, :]).then_inc(s_mark, 16)
        sp.wait_ge(s_mark, 48)
        sp.dma_start(todo_row[:, :], todo_d.rearrange("(o t) n -> o (t n)", o=1)).then_inc(s_mark, 16)
        pool.wait_ge(s_pl, 2)
        pool.wait_ge(s_sc, 16 * TOPK * TILES)
        s_t = [sem(f"s_taken{g}") for g in range(3)]
        for g in range(3):
            pool.indirect_dma_start(out=taken[:, g, :], out_offset=None, in_=slots_d.rearrange("(q p) o -> q (p o)", p=P),
                                    in_offset=bass.IndirectOffsetOnAxis(ap=blk[:, g:g + 1], axis=0)).then_inc(s_t[g], 16)
        for g in range(3):
            dve.wait_ge(s_t[g], 16)
            dve.tensor_copy(takenf[:, g, :], taken[:, g, :]).then_inc(s_pl, 1)
            pe.wait_ge(s_pl, 3 + g)
            pe.transpose(bank[1][:, g * P:(g + 1) * P], takenf[:, g, :], ident[:, :]).then_inc(s_set, 1)
        dve.wait_ge(s_set, 12)
        dve.tensor_copy(who[:, :].rearrange("s (p g) -> s g p", g=3), bank[1][:, 0:3 * P].rearrange("s (g p) -> s g p", g=3)).then_inc(s_pl, 1)
        dve.wait_ge(s_pl, 6)
        sp.wait_ge(s_mark, 64)
        sp.wait_ge(s_xf, 16 * TILES)
        E.wait(sp, "x6", idx=TILES - 1)
        E.wait(sp, "wts", idx=TILES - 1)
    nc.all_engine_barrier()


def experts(nc, a, plan, sem, bank, ident, who, todo_row, xf_d, y_d, pool_waits, carrier):
    pe, dve, act, pool, sp = nc.tensor, nc.vector, nc.scalar, nc.gpsimd, nc.sync
    DEEP = 8
    UP, DOWN = 2, 4
    HALF = DEEP // 2
    ph = ExitStack()
    with ph:
        def ring(name, shape, dt=F32):
            return [ph.enter_context(nc.sbuf_tensor(f"{name}{z}", shape, dt)) for z in range(DEEP)]

        mine = [ph.enter_context(nc.sbuf_tensor(f"mine{f}", [P, HALF], U32)) for f in range(2)]
        w = ring("w", [P, DIM + DIM])
        xg = ring("xg", [P, DIM])
        xgT = ring("xgT", [P, 2, P])
        h = ring("h", [P, P])
        y = ring("y", [P, DIM])
        s_w = [sem(f"s_w{z}") for z in range(DEEP)]
        s_g = [sem(f"s_g{z}") for z in range(DEEP)]
        s_y = [sem(f"s_y{z}") for z in range(DEEP)]
        s_z = sem("s_zero")
        for z in range(DEEP):
            dve.memset(xg[z][:, :], 0.0).then_inc(s_z, 1)
        pool.wait_ge(s_z, DEEP)
        last_token = pool.to_reg(TOKENS - 1)
        rows = xf_d.rearrange("t p n -> (t p) n")
        y_blocks = y_d.rearrange("(q p) n -> q p n", p=P)
        T, U, D = (Steps(nc, sem, n) for n in ("T", "U", "D"))
        s_mine = [sem(f"s_mine{f}") for f in range(2)]

        def indices(s, f):
            for z in range(HALF * f, HALF * f + HALF):
                dve.wait_ge(s_g[z], s * 16)
            dve.tensor_copy(mine[f][:, :], who[:, bass.ds(s * DEEP + HALF * f, HALF)]).then_inc(s_mine[f], 1)

        def load(s, z):
            b = s * DEEP + z
            e = sp.value_load(todo_row[0:1, bass.ds(b, 1)])
            D.wait(sp, "pe", b - DEEP)
            sp.dma_start(w[z][:, :], a["wexp"][bass.ds(e, 1)].rearrange("a p n -> (a p) n")).then_inc(s_w[z], 16)
            if z % 2 == 0:
                T.wait(pool, "pe", b + 1 - DEEP)
                pool.wait_ge(s_mine[z // HALF], s + 1)
                pool_waits.link(pool.tensor_tensor(carrier[:, 1:2], carrier[:, 0:1], carrier[:, 0:1], ALU.add))
                for g in (z, z + 1):
                    pool.indirect_dma_start(out=xg[g][:, :], out_offset=None, in_=rows,
                                            in_offset=bass.IndirectOffsetOnAxis(ap=mine[g // HALF][:, g % HALF:g % HALF + 1], axis=0),
                                            bounds_check=last_token, oob_is_err=False).then_inc(s_g[g], 16)

        def turn(s, z):
            b, bk = s * DEEP + z, bank[z % 4]
            pe.wait_ge(s_g[z], (s + 1) * 16)
            T.wait(pe, "dve", b - 4)
            for c in range(2):
                last = pe.transpose(bk[:, c * P:(c + 1) * P], xg[z][:, c * P:(c + 1) * P], ident[:, :])
            T.done("pe", last)
            T.wait(dve, "pe", b)
            U.wait(dve, "pe", b - DEEP)
            T.done("dve", dve.tensor_copy(xgT[z][:, :, :], bk[:, 0:2 * P].rearrange("p (c n) -> p c n", c=2)))

        def up(s, z):
            b, bk = s * DEEP + z, bank[4 + z % 2]
            pe.wait_ge(s_w[z], (s + 1) * 16)
            T.wait(pe, "dve", b)
            U.wait(pe, "act", b - 2)
            for c in range(2):
                last = pe.matmul(bk[:, 0:P], w[z][:, c * P:(c + 1) * P], xgT[z][:, c, :], start=(c == 0), stop=(c == 1))
            U.done("pe", last)
            U.wait(act, "pe", b)
            D.wait(act, "pe", b - DEEP)
            U.done("act", act.activation(h[z][:, :], bk[:, 0:P], ACT.Silu))

        def down(s, z):
            b, bk = s * DEEP + z, bank[6 + z % 2]
            U.wait(pe, "act", b)
            D.wait(pe, "dve", b - 2)
            D.done("pe", pe.matmul(bk[:, 0:DIM], h[z][:, :], w[z][:, DIM:2 * DIM], start=True, stop=True))
            D.wait(dve, "pe", b)
            dve.wait_ge(s_y[z], s * 16)
            D.done("dve", dve.tensor_copy(y[z][:, :], bk[:, 0:DIM]))

        def store(s, z):
            b = s * DEEP + z
            D.wait(act, "dve", b)
            act.dma_start(y_blocks[bass.ds(b, 1)].rearrange("a p n -> (a p) n"), y[z][:, :]).then_inc(s_y[z], 16)

        def run(s, first=False, last=False):
            for z in range(DEEP):
                if not last:
                    if z == HALF:
                        indices(s + 1, 0)
                    if z == 0:
                        indices(s, 1)
                    load(s, z)
                for part, lag in ((down, DOWN), (up, UP)):
                    if z >= lag and not last:
                        part(s, z - lag)
                    elif z < lag and not first:
                        part(s - 1, z - lag + DEEP)
                if not last:
                    turn(s, z)
                if z >= DOWN and not last:
                    store(s, z - DOWN)
                elif z < DOWN and not first:
                    store(s - 1, z - DOWN + DEEP)
            pool_waits.reset()

        indices(0, 0)
        run(0, first=True)
        with nc.Fori(1, BLOCKS // DEEP, 1) as s:
            run(s)
        run(BLOCKS // DEEP, last=True)
        for z in range(DEEP):
            sp.wait_ge(s_y[z], 16 * (BLOCKS // DEEP))
    nc.all_engine_barrier()


def combine(nc, plan, sem, X, slots, shift, wts, y_d, out, dchain, pool_waits, carrier):
    dve, pool, sp = nc.vector, nc.gpsimd, nc.sync
    ph = ExitStack()
    with ph:
        def pair(name, shape, dt=F32):
            return [ph.enter_context(nc.sbuf_tensor(f"{name}{z}", shape, dt)) for z in range(2)]

        ids, wt = pair("ids", [P, TOPK], U32), pair("wt", [P, TOPK])
        g, acc = pair("g", [P, TOPK, DIM]), pair("acc", [P, 2, DIM])
        moved = ph.enter_context(nc.sbuf_tensor("moved", [P, 2, EXPERTS], F32))
        top = ph.enter_context(nc.sbuf_tensor("top_rows", [P, 8], F32))
        s_row = [[sem(f"s_row{z}{k}") for k in range(TOPK)] for z in range(2)]
        s_o = [sem(f"s_o{z}") for z in range(2)]
        T = Stage(nc, sem, "S", plan)
        with nc.Fori(0, TILES // 2, 1) as s:
            T.begin(s)
            for z in range(2):
                i = s * 2 + z
                mine = slots[:, bass.ds(i, 1), :].rearrange("p a n -> p (a n)")
                dchain.link(dve.tensor_tensor(moved[:, 0, :], mine, shift[:, :], ALU.add))
                dchain.link(dve.scalar_tensor_tensor(out=moved[:, 1, :], in0=mine, scalar=0.0, in1=moved[:, 0, :], op0=ALU.is_gt, op1=ALU.mult))
                dchain.link(dve.max(top[:, :], moved[:, 1, :]))
                dve.wait_ge(s_row[z][TOPK - 1], s * 16)
                T.done("dve", dve.tensor_scalar(ids[z][:, :], top[:, :], 1.0, None, ALU.subtract), f"ids{z}")
                T.wait(pool, f"ids{z}")
                T.wait(pool, f"acc{z}", 1)
                pool_waits.link(pool.tensor_tensor(carrier[:, 1:2], carrier[:, 0:1], carrier[:, 0:1], ALU.add))
                for k in range(TOPK):
                    pool.indirect_dma_start(out=g[z][:, k, :], out_offset=None, in_=y_d,
                                            in_offset=bass.IndirectOffsetOnAxis(ap=ids[z][:, k:k + 1], axis=0)).then_inc(s_row[z][k], 16)
            for z in range(2):
                i = s * 2 + z
                T.wait(dve, f"acc{z}", 1)
                T.done("dve", dve.tensor_copy(wt[z][:, :], wts[:, bass.ds(i, 1), :].rearrange("p a n -> p (a n)")), f"wt{z}")
                T.wait(dve, f"wt{z}")
                dve.wait_ge(s_o[z], s * 16)
                for k in range(TOPK):
                    dve.wait_ge(s_row[z][k], (s + 1) * 16)
                    prev = X[:, bass.ds(i, 1), :].rearrange("p a n -> p (a n)") if k == 0 else acc[z][:, (k - 1) % 2, :]
                    ins = dve.scalar_tensor_tensor(out=acc[z][:, k % 2, :], in0=g[z][:, k, :], scalar=wt[z][:, k:k + 1], in1=prev,
                                                   op0=ALU.mult, op1=ALU.add)
                    if k < TOPK - 1:
                        dchain.link(ins)
                T.done("dve", ins, f"acc{z}")
                T.wait(sp, f"acc{z}")
                sp.dma_start(out.rearrange("(t p) n -> t p n", p=P)[bass.ds(i, 1)].rearrange("a p n -> (a p) n"),
                             acc[z][:, (TOPK - 1) % 2, :]).then_inc(s_o[z], 16)
            T.end()
            dchain.reset()
            pool_waits.reset()
        for z in range(2):
            sp.wait_ge(s_o[z], 16 * (TILES // 2))


def program(nc, a, out, plan, upto=9):
    ctx = ExitStack()
    with ctx:
        pe, dve, act, pool, sp = nc.tensor, nc.vector, nc.scalar, nc.gpsimd, nc.sync

        def sb(name, shape, dt=F32):
            return ctx.enter_context(nc.sbuf_tensor(name, shape, dt))

        bank = [ctx.enter_context(nc.psum_tensor(f"bank{k}", [P, 512], F32)) for k in range(8)]

        def sem(name):
            return ctx.enter_context(nc.semaphore(name))

        X = sb("X", [P, TILES, DIM])
        XN = sb("XN", [P, TILES, DIM])
        amax = sb("amax", [P, 2])
        ident = sb("ident", [P, P])
        head = sb("head", [P, 2])
        small = sb("small", [P, 16])
        idle = sb("idle", [1, 1])
        s_const, s_w0, s_setup = sem("s_const"), sem("s_rope"), sem("s_setup")
        dchain = Chain(nc, ctx, dve, "dve_chain")
        pool_waits = Chain(nc, ctx, pool, "pool_waits")
        carrier = sb("carrier", [1, 2])

        n_const = 0

        def const(dst, src):
            nonlocal n_const
            sp.dma_start(dst, src).then_inc(s_const, 16)
            n_const += 1

        const(ident[:, :], a["c_ident"])
        const(head[:, :], a["c_head"])

        ph1 = ExitStack()
        with ph1:
            def sb1(name, shape, dt=F32):
                return ph1.enter_context(nc.sbuf_tensor(name, shape, dt))

            wq0 = sb1("wq0", [P, 2, 512])
            wk0 = sb1("wk0", [CW, 2, 512])
            wv0 = sb1("wv0", [CW, 2, 512])
            wo0 = sb1("wo0", [P, 4, DIM])
            bo0 = sb1("bo0", [P, DIM])
            const(wq0[:, :, :], a["wq0"].rearrange("(c p) n -> p c n", p=P))
            const(wk0[:, :, :], a["wk0"].rearrange("(c p) n -> p c n", p=CW))
            const(wv0[:, :, :], a["wv0"].rearrange("(c p) n -> p c n", p=CW))
            const(wo0[:, :, :], a["wo0"].rearrange("(c p) n -> p c n", p=P))
            const(bo0[:, :], bc(a["bo0"].rearrange("(a n) -> a n", a=1), 0, P))
            wqs = sb1("wqs", [P, 2, DIM])
            wla = sb1("wla", [P, 2, P])
            wlb = sb1("wlb", [P, DIM])
            wos = sb1("wos", [P, 2, DIM])
            gam = sb1("gam", [P, DIM])
            bet = sb1("bet", [P, DIM])
            rope = sb1("rope", [P, 2 * P])
            wraw = sb1("wraw", [P, 3, DIM])
            const(wraw[:, 0:2, :], a["wqs"].rearrange("(c p) n -> p c n", p=P))
            const(wraw[0:64, 2, :], a["wkb"])
            const(wlb[64:128, :], a["wvb"])
            const(wla[:, :, 0:64], a["wka"].rearrange("(c p) n -> p c n", p=P))
            const(wla[:, :, 64:128], a["wva"].rearrange("(c p) n -> p c n", p=P))
            const(wos[:, :, :], a["wos"].rearrange("(c p) n -> p c n", p=P))
            const(gam[:, :], bc(a["gam"].rearrange("(a n) -> a n", a=1), 0, P))
            const(bet[:, :], bc(a["bet"].rearrange("(a n) -> a n", a=1), 0, P))
            const(rope[:, :], bc(a["c_rope"], 0, P))

            xin = sb1("xin", [P, DIM])
            cT = sb1("cT", [CW, 2, 512])
            mk = sb1("mk", [P, 512], U8)
            s_x, s_c, s_m = sem("s_x"), sem("s_c"), sem("s_m")
            stA = sb1("stA", [P, 16])
            xnA = sb1("xnA", [P, DIM])
            xb = sb1("xb", [P, DIM])
            xT = sb1("xT", [P, 2, P])
            qx = sb1("qx", [P, 2, 4, P])
            kT = sb1("kT", [P, 4, 512])
            vv = sb1("vv", [P, 4, 512])
            mb = sb1("mb", [P, 512])
            sm = sb1("sm", [P, 4, 512])
            nm = sb1("nm", [P, 8])
            sums = sb1("sums", [P, 8])
            rec = sb1("rec", [P, 8])
            pT = sb1("pT", [P, 4, 512])
            oA = sb1("oA", [P, 4, 2, 64])
            oT = sb1("oT", [P, 4, P])
            xB = sb1("xB", [P, DIM])

            xr = sb1("xr", [P, DIM])
            stB = sb1("stB", [P, 16])
            xnB = sb1("xnB", [P, DIM])
            xTB = sb1("xTB", [P, 2, P])
            lat = sb1("lat", [P, P])
            qTB = sb1("qTB", [P, 2, P])
            kx = sb1("kx", [P, 2, 2, P])
            vB = sb1("vB", [P, DIM])
            negm = sb1("negm", [P, H1])
            pB = sb1("pB", [P, H1, P])
            pTB = sb1("pTB", [P, H1, P])
            dn = sb1("dn1", [P, 4, DIM])
            ones = sb1("ones1", [P, 32])
            oTB = sb1("oTB", [P, 2, P])
            x2 = sb1("x2", [P, DIM])
            t3 = sb1("t3", [P, 2, DIM])

            pool.memset(small[:, 0:1], -0.5).then_inc(s_setup, 1)
            pool.memset(carrier[:, :], 0.0).then_inc(s_setup, 1)
            pool.memset(qx[:, :, :, :], 0.0).then_inc(s_setup, 1)
            pool.memset(pB[:, :, :], 0.0).then_inc(s_setup, 1)
            pool.memset(amax[:, :], 0.0).then_inc(s_setup, 1)
            pool.memset(ones[:, :], 1.0).then_inc(s_setup, 1)
            for e in (pe, dve, act, pool):
                e.wait_ge(s_const, 16 * n_const)
                e.wait_ge(s_setup, 6)

            cos, sin = rope[:, 0:P], rope[:, P:2 * P]
            for c, (dst, src, np_) in enumerate([(wqs[:, 0, :], wraw[:, 0, :], P), (wqs[:, 1, :], wraw[:, 1, :], P),
                                                 (wlb[0:64, :], wraw[0:64, 2, :], 64)]):
                s4 = src.rearrange("p (n t) -> p t n", t=2)
                d4 = dst.rearrange("p (n t) -> p t n", t=2)
                tmp = t3[0:np_, 0, 0:P]
                tmp2 = t3[0:np_, 0, P:2 * P]
                dchain.link(dve.tensor_tensor(tmp, s4[:, 1, :], sin[0:np_], ALU.mult))
                dchain.link(dve.tensor_tensor(tmp2, s4[:, 0, :], cos[0:np_], ALU.mult))
                dchain.link(dve.tensor_tensor(d4[:, 0, :], tmp2, tmp, ALU.subtract))
                dchain.link(dve.tensor_tensor(tmp, s4[:, 0, :], sin[0:np_], ALU.mult))
                dchain.link(dve.tensor_tensor(tmp2, s4[:, 1, :], cos[0:np_], ALU.mult))
                last = dve.tensor_tensor(d4[:, 1, :], tmp2, tmp, ALU.add)
                if c < 2:
                    dchain.link(last)
            last.then_inc(s_w0, 1)
            for e in (pe, dve):
                e.wait_ge(s_w0, 1)
            dchain.reset()

            A, B = Stage(nc, sem, "A", plan), Stage(nc, sem, "B", plan)

            def stage_a(i):
                A.begin(i)
                A.wait(sp, "xb", 1)
                sp.dma_start(xin[:, :], a["x"][bass.ds(i, 1)].rearrange("a p n -> (a p) n")).then_inc(s_x, 16)
                A.wait(sp, "v3", 1)
                sp.dma_start(cT[:, :, :], a["ctx"][bass.ds(i, 1)].rearrange("a p c n -> (a p) c n")).then_inc(s_c, 16)
                A.wait(act, "mb", 1)
                act.dma_start(mk[:, :], bc(a["mask"][bass.ds(i, 1)], 0, P)).then_inc(s_m, 16)
                dve.wait_ge(s_x, (i + 1) * 16)
                dchain.link(dve.bn_stats(stA[:, 0:6], xin[:, :]))
                dchain.link(dve.bn_aggr(stA[:, 6:8], stA[:, 0:6]))
                A.done("dve", dve.tensor_scalar(stA[:, 8:9], stA[:, 7:8], 1e-5, None, ALU.add), "var")
                A.wait(pool, "var")
                A.done("pool", pool.tensor_tensor(stA[:, 9:10], stA[:, 8:9], small[:, 0:1], ALU.pow), "rstd")
                A.wait(dve, "rstd")
                A.wait(dve, "xnT", 1)
                A.done("dve", dve.tensor_scalar(xnA[:, :], xin[:, :], stA[:, 6:7], stA[:, 9:10], ALU.subtract, ALU.mult), "xn")
                A.wait(pool, "y", 1)
                A.wait(pool, "xn")
                A.done("pool", pool.tensor_tensor(xb[:, :], xin[:, :], bo0[:, :], ALU.add), "xb")
                yield
                A.wait(pe, "xn")
                A.wait(pe, "oTe", 1)
                pe.transpose(bank[4][:, 0:P], xnA[:, 0:P], ident[:, :])
                A.done("pe", pe.transpose(bank[4][:, P:2 * P], xnA[:, P:2 * P], ident[:, :]), "xnT")
                A.wait(act, "xnT")
                A.wait(act, "q", 1)
                A.done("act", act.copy(xT[:, :, :], bank[4][:, 0:2 * P].rearrange("p (c n) -> p c n", c=2)), "xT")
                A.wait(pe, "xT")
                A.wait(pe, "y", 1)
                for m in range(4):
                    for c in range(2):
                        last = pe.matmul(bank[5][:, m * P:(m + 1) * P], wq0[:, c, m * P:(m + 1) * P], xT[:, c, :],
                                         start=(c == 0), stop=(c == 1))
                A.done("pe", last, "q")
                A.wait(act, "q")
                A.wait(act, "s3", 1)
                for h2 in range(2):
                    src = bank[5][64 * h2:64 * h2 + 64, :].rearrange("p (m b t) -> p b m t", m=4, b=2)
                    last = act.copy(qx[64 * h2:64 * h2 + 64, :, :, 64 * h2:64 * h2 + 64], src)
                A.done("act", last, "qx")
                yield
                pe.wait_ge(s_c, (i + 1) * 16)
                for m in range(4):
                    bk = bank[m % 2]
                    A.wait(pe, f"k{m - 2}e" if m >= 2 else f"o{m}", 0 if m >= 2 else 1)
                    for c in range(2):
                        last = pe.matmul(bk[:, :], wk0[:, c, m * P:(m + 1) * P], cT[:, c, :], start=(c == 0), stop=(c == 1))
                    A.done("pe", last, f"k{m}")
                    A.wait(act, f"k{m}")
                    if m == 0:
                        A.wait(act, "s3", 1)
                    A.done("act", act.copy(kT[:, m, :], bk[:, :]), f"k{m}e")
                yield
                dve.wait_ge(s_m, (i + 1) * 16)
                A.done("dve", dve.tensor_scalar(mb[:, :], mk[:, :], 1.0, -NEG, ALU.subtract, ALU.mult), "mb")
                A.wait(pe, "qx")
                for hp in range(4):
                    bk = bank[2 + hp % 2]
                    A.wait(pe, f"k{hp}e")
                    A.wait(pe, f"t{hp - 2}" if hp >= 2 else f"t{hp + 2}", 0 if hp >= 2 else 1)
                    for b in range(2):
                        last = pe.matmul(bk[:, 256 * b:256 * b + 256], qx[:, b, hp, :], kT[:, hp, 256 * b:256 * b + 256],
                                         start=True, stop=True)
                    A.done("pe", last, f"s{hp}")
                    A.wait(dve, f"s{hp}")
                    if hp == 0:
                        A.wait(dve, "mb")
                        A.wait(dve, "e3", 1)
                    A.wait(dve, f"pT{hp}", 1)
                    dchain.link(dve.memset(idle[:, 0:1], 0.0))
                    for b in range(2):
                        last = dve.tensor_tensor_reduce(sm[:, hp, 256 * b:256 * b + 256], bk[:, 256 * b:256 * b + 256],
                                                        mb[:, 256 * b:256 * b + 256], -0.125, -NEG, ALU.add, ALU.min,
                                                        nm[:, 2 * hp + b:2 * hp + b + 1])
                    A.done("dve", last, f"t{hp}")
                    A.wait(act, f"t{hp}")
                    if hp == 0:
                        A.wait(act, "rec", 1)
                    for b in range(2):
                        blk = sm[:, hp, 256 * b:256 * b + 256]
                        last = act.activation(blk, blk, ACT.Exp, bias=nm[:, 2 * hp + b:2 * hp + b + 1], scale=-1.0,
                                              accum_out=sums[:, 2 * hp + b:2 * hp + b + 1])
                    A.done("act", last, f"e{hp}")
                yield
                for c4 in range(4):
                    bk = bank[c4 % 2]
                    A.wait(pe, f"v{c4 - 2}e" if c4 >= 2 else f"k{c4 + 2}e")
                    for c in range(2):
                        last = pe.matmul(bk[:, :], cT[:, c, c4 * P:(c4 + 1) * P], wv0[:, c, :], start=(c == 0), stop=(c == 1))
                    A.done("pe", last, f"v{c4}")
                    A.wait(dve, f"v{c4}")
                    if c4 == 0:
                        A.wait(dve, "o1", 1) if False else A.wait(dve, "pv1", 1)
                    A.done("dve", dve.tensor_copy(vv[:, c4, :], bk[:, :]), f"v{c4}e")
                yield
                for hp in range(4):
                    bk = bank[4 + hp % 2]
                    A.wait(pe, f"e{hp}")
                    A.wait(pe, {0: "xT", 1: "qx", 2: "pT0e", 3: "pT1e"}[hp])
                    for q in range(4):
                        last = pe.transpose(bk[:, q * P:(q + 1) * P], sm[:, hp, q * P:(q + 1) * P], ident[:, :])
                    A.done("pe", last, f"pT{hp}")
                    eng, en = (act, "act") if hp % 2 else (dve, "dve")
                    A.wait(eng, f"pT{hp}")
                    if hp < 2:
                        A.wait(eng, "pv1", 1)
                    copy = act.copy if hp % 2 else dve.tensor_copy
                    A.done(en, copy(pT[:, hp, :], bk[:, :]), f"pT{hp}e")
                yield
                A.wait(dve, "e3")
                A.wait(dve, "o1", 1)
                A.done("dve", dve.reciprocal(rec[:, :], sums[:, :]), "rec")
                A.wait(pe, "pT3e")
                A.wait(pe, "pT2e")
                for b in range(2):
                    A.wait(pe, f"v{b + 2}e")
                    for hp in range(4):
                        for kc in range(2):
                            q = 2 * b + kc
                            last = pe.matmul(bank[b][:, hp * P:(hp + 1) * P], pT[:, hp, q * P:(q + 1) * P],
                                             vv[:, q, hp * P:(hp + 1) * P], start=(kc == 0), stop=(kc == 1))
                    A.done("pe", last, f"pv{b}")
                    A.wait(dve, f"pv{b}")
                    if b == 0:
                        A.wait(dve, "rec")
                        A.wait(dve, "oT", 1)
                    for h2 in range(2):
                        r = slice(64 * h2, 64 * h2 + 64)
                        src = bank[b][r, :].rearrange("p (m n) -> p m n", m=4)[:, :, 64 * h2:64 * h2 + 64]
                        w = bc(rec[r, b:8:2].rearrange("p (m o) -> p m o", o=1), 2, 64)
                        last = dve.tensor_tensor(oA[64 * b:64 * b + 64, :, h2, :], src, w, ALU.mult)
                    A.done("dve", last, f"o{b}")
                yield
                A.wait(pe, "o1")
                A.wait(pe, "pT2e")
                for m in range(4):
                    last = pe.transpose(bank[4][:, m * P:(m + 1) * P], oA[:, m, :, :].rearrange("p a n -> p (a n)"), ident[:, :])
                A.done("pe", last, "oT")
                A.wait(act, "oT")
                A.wait(act, "yp", 1)
                A.done("act", act.copy(oT[:, :, :], bank[4][:, :].rearrange("p (m n) -> p m n", m=4)), "oTe")
                A.wait(pe, "oTe")
                A.wait(pe, "pT3e")
                for m in range(4):
                    last = pe.matmul(bank[5][:, 0:DIM], oT[:, m, :], wo0[:, m, :], start=(m == 0), stop=(m == 3))
                A.done("pe", last, "yp")
                A.wait(dve, "yp")
                A.wait(dve, "xb")
                B.wait(dve, "xr", idx=i - 1)
                A.done("dve", dve.tensor_tensor(xB[:, :], bank[5][:, 0:DIM], xb[:, :], ALU.add), "y")
                A.end()

            def stage_b(j):
                B.begin(j)
                A.wait(dve, "y", idx=j)
                dchain.link(dve.bn_stats(stB[:, 0:6], xB[:, :]))
                dchain.link(dve.bn_aggr(stB[:, 6:8], stB[:, 0:6]))
                B.done("dve", dve.tensor_scalar(stB[:, 8:9], stB[:, 7:8], 1e-5, None, ALU.add), "var")
                B.wait(pool, "var")
                B.done("pool", pool.tensor_tensor(stB[:, 9:10], stB[:, 8:9], small[:, 0:1], ALU.pow), "rstd")
                A.wait(act, "y", idx=j)
                B.wait(act, "x2", 1)
                B.done("act", act.copy(xr[:, :], xB[:, :]), "xr")
                B.wait(dve, "rstd")
                B.wait(dve, "xnT", 1)
                B.done("dve", dve.tensor_scalar(xnB[:, :], xB[:, :], stB[:, 6:7], stB[:, 9:10], ALU.subtract, ALU.mult), "xnB")
                B.wait(pe, "xnB")
                B.wait(pe, "x2", 1)
                pe.transpose(bank[6][:, 0:P], xnB[:, 0:P], ident[:, :])
                B.done("pe", pe.transpose(bank[6][:, P:2 * P], xnB[:, P:2 * P], ident[:, :]), "xnT")
                B.wait(act, "xnT")
                B.wait(act, "qk", 1)
                B.done("act", act.copy(xTB[:, :, :], bank[6][:, 0:2 * P].rearrange("p (c n) -> p c n", c=2)), "xT")
                yield
                B.wait(pe, "xT")
                B.wait(pe, "own", 1)
                for c in range(2):
                    last = pe.matmul(bank[7][:, 0:P], wla[:, c, :], xTB[:, c, :], start=(c == 0), stop=(c == 1))
                B.done("pe", last, "lat")
                B.wait(act, "lat")
                B.wait(act, "v", 1)
                B.done("act", act.copy(lat[:, :], bank[7][:, 0:P]), "late")
                for m in range(2):
                    for c in range(2):
                        pe.matmul(bank[6][:, m * P:(m + 1) * P], wqs[:, c, m * P:(m + 1) * P], xTB[:, c, :],
                                  start=(c == 0), stop=(c == 1))
                B.wait(pe, "late")
                for m in range(2):
                    last = pe.matmul(bank[6][:, 256 + m * P:256 + (m + 1) * P], wlb[0:64, m * P:(m + 1) * P], lat[0:64, :],
                                     start=True, stop=True)
                B.done("pe", last, "qk")
                last = pe.matmul(bank[7][:, 0:DIM], lat[64:128, :], wlb[64:128, :], start=True, stop=True)
                B.done("pe", last, "v")
                B.wait(act, "v")
                B.wait(act, "pv", 1)
                B.done("act", act.copy(vB[:, :], bank[7][:, 0:DIM]), "ve")
                B.wait(dve, "qk")
                B.wait(dve, "s3", 1)
                dve.tensor_copy(qTB[:, :, :], bank[6][:, 0:2 * P].rearrange("p (c n) -> p c n", c=2))
                for m in range(2):
                    src = bc(bank[6][:, 256 + m * P:256 + (m + 1) * P].rearrange("p (o n) -> p o n", o=1), 1, 2)
                    last = dve.tensor_tensor(kx[:, m, :, :], src, bc(head[:, :].rearrange("p (h o) -> p h o", o=1), 2, P), ALU.mult)
                B.done("dve", last, "kx")
                yield
                for c in range(4):
                    bk = bank[6 + c % 2]
                    rows = slice(32 * c, 32 * c + 32)
                    B.wait(pe, {0: "kx", 1: "ve", 2: "d0", 3: "d1"}[c])
                    if c == 1:
                        B.wait(pe, "kx")
                    for m in range(2):
                        last = pe.matmul(bk[:, 256 * m:256 * m + 256], qTB[rows, m, :], kx[rows, m, :, :].rearrange("p h n -> p (h n)"),
                                         start=True, stop=True)
                    B.done("pe", last, f"s{c}")
                    B.wait(dve, f"s{c}")
                    hs = slice(4 * c, 4 * c + 4)
                    if c == 0:
                        B.wait(dve, "pT3", 1)
                    for b in range(2):
                        r = slice(64 * b, 64 * b + 64)
                        blk = bk[r, :].rearrange("p (h n) -> p h n", h=4)[:, :, 64 * b:64 * b + 64]
                        last = dve.tensor_reduce(negm[r, hs], blk, AX.X, ALU.max, negate=True)
                    dchain.link(last)
                    for b in range(2):
                        r = slice(64 * b, 64 * b + 64)
                        blk = bk[r, :].rearrange("p (h n) -> p h n", h=4)[:, :, 64 * b:64 * b + 64]
                        last = dve.tensor_tensor(pB[r, hs, 64 * b:64 * b + 64], blk,
                                                 bc(negm[r, hs].rearrange("p (h o) -> p h o", o=1), 2, 64), ALU.add)
                    B.done("dve", last, f"d{c}")
                    B.wait(act, f"d{c}")
                    for b in range(2):
                        r = slice(64 * b, 64 * b + 64)
                        blk = pB[r, hs, 64 * b:64 * b + 64]
                        last = act.activation(blk, blk, ACT.Exp, scale=0.25)
                    B.done("act", last, f"e{c}")
                yield
                for c in range(4):
                    hs = slice(4 * c, 4 * c + 4)
                    bk = bank[6 + c % 2]
                    B.wait(pe, f"e{c}")
                    B.wait(pe, {0: "d2", 1: "d3", 2: "pT0e", 3: "pT1e"}[c])
                    for h in range(4):
                        last = pe.transpose(bk[:, h * P:(h + 1) * P], pB[:, 4 * c + h, :], ident[:, :])
                    B.done("pe", last, f"pT{c}")
                    B.wait(act, f"pT{c}")
                    if c == 0:
                        B.wait(act, "pv", 1)
                    B.done("act", act.copy(pTB[:, hs, :], bk[:, :].rearrange("p (h n) -> p h n", h=4)), f"pT{c}e")
                yield
                B.wait(pe, "pT3e")
                B.wait(pe, "ve")
                for t, part in ((1, "den"), (0, "pv")):
                    for m in range(2):
                        for c in range(4):
                            rows = slice(32 * c, 32 * c + 32)
                            dst = bank[6 + t][rows, :].rearrange("p (h m n) -> p m h n", h=2, m=2)[:, m, :, :]
                            src = vB[:, P * m + 32 * c:P * m + 32 * c + 32] if t == 0 else ones[:, :]
                            last = pe.matmul(dst, src, pTB[:, 4 * c + 2 * m:4 * c + 2 * m + 2, :], start=True, stop=True)
                    B.done("pe", last, part)
                B.wait(dve, "den")
                B.wait(dve, "ot", 1)
                dchain.link(dve.tensor_scalar(dn[:, 0, :], bank[7][:, 0:DIM], head[:, 0:1], None, ALU.mult))
                dchain.link(dve.scalar_tensor_tensor(out=dn[:, 1, :], in0=bank[7][:, DIM:512], scalar=head[:, 1:2], in1=dn[:, 0, :],
                                                     op0=ALU.mult, op1=ALU.add))
                dve.reciprocal(dn[:, 0, :], dn[:, 1, :])
                B.wait(dve, "pv")
                dchain.link(dve.tensor_scalar(dn[:, 2, :], bank[6][:, 0:DIM], head[:, 0:1], None, ALU.mult))
                B.done("dve", dve.scalar_tensor_tensor(out=dn[:, 3, :], in0=bank[6][:, DIM:512], scalar=head[:, 1:2], in1=dn[:, 2, :],
                                                       op0=ALU.mult, op1=ALU.add), "own")
                B.wait(dve, "own")
                B.wait(dve, "yp", 1)
                B.done("dve", dve.tensor_tensor(oTB[:, :, :].rearrange("p c n -> p (c n)"), dn[:, 3, :], dn[:, 0, :], ALU.mult), "ot")
                yield
                B.wait(pe, "ot")
                for c in range(2):
                    last = pe.matmul(bank[6][:, 0:DIM], oTB[:, c, :], wos[:, c, :], start=(c == 0), stop=(c == 1))
                B.done("pe", last, "yp")
                B.wait(dve, "yp")
                B.wait(dve, "xr")
                B.wait(dve, "keep", 1)
                B.done("dve", dve.tensor_tensor(x2[:, :], bank[6][:, 0:DIM], xr[:, :], ALU.add), "x2")
                B.wait(dve, "x2")
                dchain.link(dve.bn_stats(stB[:, 0:6], x2[:, :]))
                dchain.link(dve.bn_aggr(stB[:, 6:8], stB[:, 0:6]))
                B.done("dve", dve.tensor_scalar(stB[:, 8:9], stB[:, 7:8], 1e-5, None, ALU.add), "var2")
                B.wait(pool, "var2")
                B.done("pool", pool.tensor_tensor(stB[:, 9:10], stB[:, 8:9], small[:, 0:1], ALU.pow), "rstd2")
                B.wait(dve, "rstd2")
                dchain.link(dve.tensor_scalar(stB[:, 10:11], stB[:, 7:8], stB[:, 9:10], stB[:, 9:10], ALU.mult, ALU.mult))
                B.done("dve", dve.tensor_scalar(stB[:, 11:12], stB[:, 10:11], 1e-3, None, ALU.add), "var3")
                B.wait(pool, "var3")
                B.done("pool", pool.tensor_tensor(stB[:, 12:13], stB[:, 11:12], small[:, 0:1], ALU.pow), "rstd3")
                B.wait(dve, "rstd3")
                dchain.link(dve.tensor_scalar(t3[:, 0, :], x2[:, :], stB[:, 6:7], stB[:, 9:10], ALU.subtract, ALU.mult))
                dchain.link(dve.scalar_tensor_tensor(out=t3[:, 1, :], in0=t3[:, 0, :], scalar=stB[:, 12:13], in1=gam[:, :],
                                                     op0=ALU.mult, op1=ALU.mult))
                dchain.link(dve.tensor_tensor(t3[:, 0, :], t3[:, 1, :], bet[:, :], ALU.add))
                dchain.link(dve.tensor_reduce(amax[:, 1:2], t3[:, 0, :], AX.X, ALU.max, apply_absolute_value=True))
                dchain.link(dve.tensor_tensor(amax[:, 0:1], amax[:, 0:1], amax[:, 1:2], ALU.max))
                B.done("dve", dve.tensor_copy(XN[:, bass.ds(j, 1), :].rearrange("p a n -> p (a n)"), t3[:, 0, :]), "xn3")
                B.wait(act, "x2")
                B.done("act", act.copy(X[:, bass.ds(j, 1), :].rearrange("p a n -> p (a n)"), x2[:, :]), "keep")
                B.wait(dve, "xn3")
                B.end()

            def step(s, do_a, do_b):
                ga = stage_a(s) if do_a else iter(())
                gb = stage_b(s - 1) if do_b else iter(())
                for which in "BAABABABABABABABAB":
                    next(gb if which == "B" else ga, None)
                for g in (ga, gb):
                    for _ in g:
                        pass
                dchain.reset()

            step(0, True, False)
            with nc.Fori(1, TILES, 1) as s:
                step(s, True, True)
            step(TILES, False, True)
            B.wait(dve, "keep", idx=TILES - 1)
            B.wait(pool, "xn3", idx=TILES - 1)
            B.wait(pool, "keep", idx=TILES - 1)
        nc.all_engine_barrier()
        if upto >= 2:
            slots, wts, shift = sb("slots", [P, TILES, EXPERTS]), sb("wts", [P, TILES, TOPK]), sb("shift", [P, EXPERTS])
            who = sb("who", [P, 3 * P], U32)
            todo_row = sb("todo_row", [1, 3 * P], U32)
            slots_d = nc.dram_tensor("slots_d", (ROWS, 1), U32, kind="Internal").ap()
            xf_d = nc.dram_tensor("xf_d", (TILES, P, DIM), F32, kind="Internal").ap()
            todo_d = nc.dram_tensor("todo_d", (3 * P, 1), U32, kind="Internal").ap()
            y_d = nc.dram_tensor("y_d", (BLOCKS * P, DIM), F32, kind="Internal").ap()
            phase2(nc, a, plan, (slots, wts, shift, who, todo_row, slots_d, xf_d, todo_d), sem, bank, X, XN, ident, head, small, idle, dchain, amax, pool_waits, carrier, upto)

        if upto >= 3:
            experts(nc, a, plan, sem, bank, ident, who, todo_row, xf_d, y_d, pool_waits, carrier)
            combine(nc, plan, sem, X, slots, shift, wts, y_d, out, dchain, pool_waits, carrier)
            return
        s_out = sem("s_out")
        sp.dma_start(out.rearrange("(t p) n -> p t n", p=P), X[:, :, :]).then_inc(s_out, 16)
        sp.wait_ge(s_out, 16)


def lay_out(i):
    c = np.ascontiguousarray
    t = lambda k: c(np.asarray(i[k]).T)
    ctx = np.asarray(i["ctx_768"]).reshape(TILES, 512, 2, CW)
    d = {
        "x": np.asarray(i["x"]).reshape(TILES, P, DIM),
        "ctx": c(ctx.transpose(0, 3, 2, 1)),
        "mask": np.asarray(i["mask_BxS2_bk0"]).reshape(TILES, 512),
        "wq0": np.asarray(i["L0_xattn_W_q"]), "wk0": np.asarray(i["L0_xattn_W_k"]), "wv0": np.asarray(i["L0_xattn_W_v"]),
        "wo0": np.asarray(i["L0_xattn_W_o"]), "bo0": np.asarray(i["L0_xattn_b_o"]),
        "wqs": t("L0_attn_wq"), "wka": t("L0_attn_wk_a"), "wkb": t("L0_attn_wk_b"), "wva": t("L0_attn_wv_a"),
        "wvb": t("L0_attn_wv_b"), "wos": t("L0_attn_wo"),
        "gam": np.asarray(i["L0_ffn_ln_gamma"]), "bet": np.asarray(i["L0_ffn_ln_beta"]),
    }
    for k, v in {"wf": "L0_ffn_weight", "bqd": "L1_xattn_bq", "bkd": "L1_xattn_bk", "bvd": "L1_xattn_bv", "bod": "L1_xattn_bo",
                 "lns": "L1_attn_ln_scale", "lnb": "L1_attn_ln_bias", "wh": "L1_attn_W_hidden", "bh": "L1_attn_b_hidden",
                 "wqk": "L1_attn_W_qk", "bqk": "L1_attn_b_qk", "wout": "L1_attn_W_out", "bout": "L1_attn_b_out"}.items():
        d[k] = np.asarray(i[v])
    for k, v in {"wqd": "L1_xattn_Wq", "wkd": "L1_xattn_Wk", "wvd": "L1_xattn_Wv", "wod": "L1_xattn_Wo",
                 "wgs": "L1_ffn_w_gate_shared", "wds": "L1_ffn_w_down_shared"}.items():
        d[k] = t(v)
    d["osw"], d["osb"] = np.asarray(i["L1_attn_os_weight"]), np.asarray(i["L1_attn_os_bias"])
    for k in ("bqd", "bkd", "bqk", "osw", "osb"):
        d[k] = c(d[k].reshape(-1, P).T)
    d["wr"], d["be"] = t("L1_ffn_router_w"), np.asarray(i["L1_ffn_expert_bias"])
    gate = np.asarray(i["L1_ffn_w_gate"]).reshape(EXPERTS, INTER, 2, P).transpose(0, 3, 2, 1).reshape(EXPERTS, P, 2 * INTER)
    down = np.asarray(i["L1_ffn_w_down"]).transpose(0, 2, 1)
    d["wexp"] = np.concatenate([gate, down], axis=2)
    d.update(constants())
    return d


def kernel(**inputs):
    import concourse.bacc as bacc
    from concourse.bass_utils import run_bass_kernel_spmd

    arrays = lay_out(inputs)
    plan = {}
    for _ in range(2):
        nc = bacc.Bacc("TRN2", target_bir_lowering=False, num_devices=1)
        a = {n: nc.dram_tensor(f"in_{n}", v.shape, mybir.dt.from_np(v.dtype), kind="ExternalInput").ap() for n, v in arrays.items()}
        out = nc.dram_tensor("out", (TOKENS, DIM), F32, kind="ExternalOutput").ap()
        program(nc, a, out, plan)
    r = run_bass_kernel_spmd(nc, [{f"in_{n}": v for n, v in arrays.items()}], core_ids=[0])
    return r.results[0]["out"].reshape(BATCHES, SEQ, DIM)
```

```python
from contextlib import ExitStack
from math import sqrt

import numpy as np
import concourse.bass as bass
from concourse import mybir

F32 = mybir.dt.float32
I32 = mybir.dt.int32
U32 = mybir.dt.uint32
U8 = mybir.dt.uint8
ALU = mybir.AluOpType
ACT = mybir.ActivationFunctionType
AX = mybir.AxisListType

P = 128
BATCHES, SEQ, DIM = 32, 64, 256
CTX, CDIM = 256, 192
TILES = BATCHES * SEQ // P
CW = CDIM // 2
H0, D0 = 8, 64
H1, D1 = 16, 16
TOKENS = BATCHES * SEQ
EXPERTS, TOPK, INTER = 160, 8, 128
BLOCKS = -(-((TOKENS * TOPK + EXPERTS * (P - 1)) // P) // 4) * 4
REGION = TOKENS // P
ROWS = (EXPERTS * REGION + BLOCKS) * P
NOBODY = 1 << 20
NEG = -3.4028234663852886e38


class Stage:

    def __init__(self, nc, sem, name, plan):
        self.nc, self.name, self.plan = nc, name, plan
        self.engines = {"pe": nc.tensor, "dve": nc.vector, "act": nc.scalar, "pool": nc.gpsimd}
        self.sem = {e: sem(f"{name}_{e}") for e in self.engines}
        self.per, self.at = plan.get(name, ({e: 0 for e in self.engines}, {}))
        for e, eng in self.engines.items():
            if self.per[e]:
                eng.sem_inc(self.sem[e], self.per[e])

    def begin(self, idx):
        self.idx, self.n, self.seen = idx, {e: 0 for e in self.engines}, {}

    def end(self):
        self.plan[self.name] = (dict(self.n), dict(self.seen))

    def done(self, e, ins, event):
        self.n[e] += 1
        assert event not in self.seen, event
        self.seen[event] = (e, self.n[e])
        ins.then_inc(self.sem[e], 1)

    def wait(self, eng, event, back=0, idx=None):
        e, k = self.at.get(event, ("pe", 1))
        idx = self.idx if idx is None else idx
        eng.wait_ge(self.sem[e], (idx + (1 - back)) * self.per[e] + k)


class Steps:

    MARGIN = 8

    def __init__(self, nc, sem, name):
        self.engines = {"pe": nc.tensor, "dve": nc.vector, "act": nc.scalar}
        self.sem = {e: sem(f"{name}_{e}") for e in self.engines}
        for e, eng in self.engines.items():
            eng.sem_inc(self.sem[e], self.MARGIN)

    def done(self, e, ins):
        ins.then_inc(self.sem[e], 1)

    def wait(self, eng, e, b):
        eng.wait_ge(self.sem[e], b + 1 + self.MARGIN)


class Chain:

    def __init__(self, nc, ctx, eng, name):
        self.eng, self.sem, self.n = eng, ctx.enter_context(nc.semaphore(name)), 0

    def link(self, ins):
        self.n += 1
        ins.then_inc(self.sem, 1)
        self.eng.wait_ge(self.sem, self.n)

    def reset(self):
        if self.n:
            self.eng.sem_clear(self.sem)
        self.n = 0


def constants():
    ident = np.eye(P, dtype=np.float32)
    inv = 1.0 / 10000.0 ** (np.arange(0, D1, 2, dtype=np.float32) / D1)
    ang = np.arange(H1, dtype=np.float32)[:, None] * inv[None, :].astype(np.float32)
    rope = np.stack([np.cos(ang), np.sin(ang)]).astype(np.float32).reshape(1, 2 * P)
    return {
        "c_ident": ident, "c_head": (np.arange(P)[:, None] // D1 % 2 == np.arange(2)[None, :]).astype(np.float32), "c_rope": rope,
        "c_tri": np.triu(np.ones((P, P), np.float32), 1),
        "c_ones": np.ones((P, P), np.float32),
        "c_base": (np.arange(EXPERTS, dtype=np.float32) * TOKENS + 1)[None, :],
        "c_steps": (np.arange(3)[None, :] + 3 * np.arange(P)[:, None]).astype(np.float32),
        "c_tokens": (np.arange(TILES)[None, :] * P + np.arange(P)[:, None]).astype(np.uint32),
    }


def bc(ap, axis, n):
    shape = list(ap.shape)
    shape[axis] = n
    return ap.broadcast_to(shape)


def phase2_weights(a, sb):
    loads = []

    def const(dst, src):
        loads.append((dst, src))

    def weights(name, rows, cols, p=P):
        w = sb(name, [p, rows // p, cols])
        const(w[:, :, :], a[name].rearrange("(c p) n -> p c n", p=p))
        return w

    def spread(name, n):
        w = sb(name, [P, n])
        const(w[:, :], bc(a[name].rearrange("(a n) -> a n", a=1), 0, P))
        return w

    def column(name, n):
        w = sb(name, [P, n])
        const(w[:, :], a[name])
        return w

    wf = weights("wf", DIM, DIM)
    wqd, wod = weights("wqd", DIM, DIM), weights("wod", DIM, DIM)
    wkd, wvd = weights("wkd", CDIM, DIM, CW), weights("wvd", CDIM, DIM, CW)
    bqd, bkd = column("bqd", 2), column("bkd", 2)
    bvd, bod = spread("bvd", DIM), spread("bod", DIM)
    lns, lnb = spread("lns", DIM), spread("lnb", DIM)
    wh, bh = weights("wh", DIM, 1024), spread("bh", 1024)
    wqk, bqk = weights("wqk", DIM, P), column("bqk", 1)
    osw, osb = column("osw", 2), column("osb", 2)
    wout, bout = weights("wout", 512, DIM), spread("bout", DIM)
    wgs, wds = weights("wgs", DIM, P), weights("wds", P, DIM)
    wr, be = weights("wr", DIM, EXPERTS), spread("be", EXPERTS)
    tri, ones = weights("c_tri", P, P), weights("c_ones", P, P)
    base = sb("base", [P, EXPERTS])
    const(base[:, :], bc(a["c_base"], 0, P))
    tokens = sb("tokens", [P, TILES], U32)
    const(tokens[:, :], a["c_tokens"])
    tern = sb("tern", [P, 2, DIM])
    return (tern, wf, wqd, wod, wkd, wvd, bqd, bkd, bvd, bod, lns, lnb, wh, bh, wqk, bqk, osw, osb, wout, bout, wgs, wds, wr, be,
            tri, ones, base, tokens), loads


def phase2(nc, a, plan, routes, sem, bank, X, XN, ident, head, small, idle, dchain, amax, pool_waits, carrier, resident, sc):
    slots, wts, shift, who, todo_row, slots_d, xf_d, todo_d = routes
    pe, dve, act, pool, sp = nc.tensor, nc.vector, nc.scalar, nc.gpsimd, nc.sync
    ph = ExitStack()
    with ph:
        def sb(name, shape, dt=F32):
            return ph.enter_context(nc.sbuf_tensor(name, shape, dt))

        (tern, wf, wqd, wod, wkd, wvd, bqd, bkd, bvd, bod, lns, lnb, wh, bh, wqk, bqk, osw, osb, wout, bout, wgs, wds, wr, be,
         tri, ones, base, tokens) = resident
        s_set = sem("s_set2")

        cT = sb("cT2", [CW, 2, 512])
        s_c = sem("s_c2")
        xq = sb("xq", [P, DIM])
        xqT = sb("xqT", [P, 2, P])
        x3 = sb("x3", [P, DIM])
        stC = sb("stC", [P, 16])
        xnC = sb("xnC", [P, DIM])
        xbC = sb("xbC", [P, DIM])
        xT = sb("xTC", [P, 2, P])
        qT = sb("qTC", [P, 2, P])
        qx = sb("qxC", [P, 2, 2, 2, 64])
        kT = sb("kTC", [P, 2, 512])
        vv = sb("vvC", [P, 4, DIM])
        ex = sb("ex", [P, 8, 512])
        nm = sb("nmC", [P, 8, 2])
        pT = sb("pTC", [P, 8, 512])
        dn = sb("dn", [P, 4, DIM])
        oT = sb("oTC", [P, 2, P])
        x4 = sb("x4", [P, DIM])

        x4r = sb("x4r", [P, DIM])
        xbE = sb("xbE", [P, DIM])
        stE = sb("stE", [P, 16])
        xnE = sb("xnE", [P, 2, DIM])
        xTE = sb("xTE", [P, 2, P])
        th = sb("th", [P, 1024])
        uu = sb("uu", [P, 1024])
        hid = sb("hid", [P, 1024])
        qk = sb("qk", [P, 4, P])
        qk2 = sb("qk2", [P, P])
        rel = sb("rel", [P, P])
        att = sb("att", [P, P])
        og = sb("og", [P, 512])
        ogT = sb("ogT", [P, 4, P])
        x5 = sb("x5", [P, DIM])
        xf = sb("xf", [P, DIM])
        xfT = sb("xfT", [P, 2, P])
        ths = sb("ths", [P, P])
        hs = sb("hs", [P, P])
        lg = sb("lg", [P, EXPERTS])
        ez = sb("ez", [P, EXPERTS])
        pr = sb("pr", [P, EXPERTS])
        sel = sb("sel", [P, EXPERTS])
        comb = sb("comb", [P, EXPERTS])
        before = sb("before", [P, EXPERTS])
        junk = sb("junk", [P, TOPK, EXPERTS])
        top = sb("top", [P, 4, 8])
        slot_id = sb("slot_id", [P, 8], U32)
        tok_id = sb("tok_id", [P, 1], U32)
        ones_e = sb("ones_e", [P, EXPERTS])
        s_mark, s_xf, s_sc = sem("s_mark"), sem("s_xf"), sem("s_sc")
        sp.sem_inc(s_xf, 16)

        pool.memset(rel[:, :], 0.0).then_inc(s_set, 1)
        pool.memset(before[:, :], 0.0).then_inc(s_set, 1)
        pool.memset(slot_id[:, :], NOBODY).then_inc(s_set, 1)
        pool.memset(tok_id[:, :], 0).then_inc(s_set, 1)
        last_slot = pool.to_reg(ROWS - 1)
        dve.memset(ones_e[:, :], 1.0).then_inc(s_set, 1)
        for e in (pe, dve, act, pool, sp):
            e.wait_ge(s_set, 5)
        pool.partition_all_reduce(sc[:, 2:3], amax[:, 0:1], P, bass.bass_isa.ReduceOp.max).then_inc(s_set, 1)
        dve.wait_ge(s_set, 6)
        link = dchain.link
        link(dve.reciprocal(sc[:, 3:4], sc[:, 2:3]))
        link(dve.tensor_scalar(sc[:, 3:4], sc[:, 3:4], 128.0, None, ALU.mult))
        dve.tensor_scalar(sc[:, 4:5], sc[:, 2:3], sc[:, 1:2], 1.0 / 128, ALU.mult, ALU.mult).then_inc(s_set, 1)
        for e in (pe, dve, act, pool):
            e.wait_ge(s_set, 7)
        dchain.reset()

        C, E, R = Stage(nc, sem, "C", plan), Stage(nc, sem, "E", plan), Stage(nc, sem, "R", plan)

        def moments(S, st, x, tag):
            link(dve.bn_stats(st[:, 0:6], x))
            link(dve.bn_aggr(st[:, 6:8], st[:, 0:6]))
            S.done("dve", dve.tensor_scalar(st[:, 8:9], st[:, 7:8], 1e-5, None, ALU.add), f"var{tag}")
            S.wait(pool, f"var{tag}")
            S.done("pool", pool.tensor_tensor(st[:, 9:10], st[:, 8:9], small[:, 0:1], ALU.pow), f"rstd{tag}")
            S.wait(dve, f"rstd{tag}")

        def halves(b):
            return b[:, 0:2 * P].rearrange("p (c n) -> p c n", c=2)

        def stage_c(i):
            C.begin(i)
            C.wait(sp, "v1", 1)
            sp.dma_start(cT[:, :, :], a["ctx"][bass.ds(i, 1)].rearrange("a p c n -> (a p) c n")).then_inc(s_c, 16)
            pe.wait_ge(s_c, (i + 1) * 16)
            for m in range(2):
                C.wait(pe, f"e{6 + m}", 1)
                for c in range(2):
                    last = pe.matmul(bank[2 + m][:, :], wkd[:, c, m * P:(m + 1) * P], cT[:, c, :], start=(c == 0), stop=(c == 1))
                C.done("pe", last, f"k{m}")
                C.wait(act, f"k{m}")
                C.wait(act, "s7", 1)
                C.done("act", act.activation(kT[:, m, :], bank[2 + m][:, :], ACT.Identity, bias=bkd[:, m:m + 1]), f"k{m}e")
            lim = float(np.float32(128.0 - 1e-5))
            C.wait(pool, "xqT", 1)
            pool_waits.link(pool.tensor_tensor(xq[:, :], XN[:, bass.ds(i, 1), :].rearrange("p a n -> p (a n)"), bc(sc[:, 3:4], 1, DIM), ALU.mult))
            C.done("pool", pool.tensor_scalar(xq[:, :], xq[:, :], lim, -lim, ALU.min, ALU.max), "xq")
            C.wait(pe, "xq")
            C.wait(pe, "pT6e", 1)
            for c in range(2):
                last = pe.transpose(bank[4][:, c * P:(c + 1) * P], xq[:, c * P:(c + 1) * P], ident[:, :])
            C.done("pe", last, "xqT")
            C.wait(act, "xqT")
            C.wait(act, "yc", 1)
            C.done("act", act.copy(xqT[:, :, :], halves(bank[4])), "xqTe")
            yield
            C.wait(pe, "xqTe")
            for c in range(2):
                last = pe.matmul(bank[4][:, DIM:512], xqT[:, c, :], tern[:, c, :], start=(c == 0), stop=(c == 1))
            C.done("pe", last, "yc")
            C.wait(dve, "yc")
            C.wait(dve, "xb", 1)
            C.done("dve", dve.scalar_tensor_tensor(out=x3[:, :], in0=bank[4][:, DIM:512], scalar=sc[:, 4:5],
                                                   in1=X[:, bass.ds(i, 1), :].rearrange("p a n -> p (a n)"),
                                                   op0=ALU.mult, op1=ALU.add), "x3")
            C.wait(dve, "x3")
            moments(C, stC, x3[:, :], "")
            C.wait(dve, "xnT", 1)
            C.done("dve", dve.tensor_scalar(xnC[:, :], x3[:, :], stC[:, 6:7], stC[:, 9:10], ALU.subtract, ALU.mult), "xn")
            E.wait(pool, "x4", idx=i - 1)
            C.wait(pool, "xn")
            C.done("pool", pool.tensor_tensor(xbC[:, :], x3[:, :], bod[:, :], ALU.add), "xb")
            yield
            for m in range(2):
                C.wait(pe, "own", 1)
                for t2 in range(2):
                    q = 2 * m + t2
                    for c in range(2):
                        last = pe.matmul(bank[m][:, t2 * DIM:(t2 + 1) * DIM], cT[:, c, q * P:(q + 1) * P], wvd[:, c, :],
                                         start=(c == 0), stop=(c == 1))
                C.done("pe", last, f"v{m}")
                C.wait(dve, f"v{m}")
                C.wait(dve, "pv", 1)
                C.done("dve", dve.tensor_tensor(vv[:, 2 * m:2 * m + 2, :], bank[m][:, :].rearrange("p (c n) -> p c n", c=2),
                                                bc(bvd[:, :].rearrange("p (o n) -> p o n", o=1), 1, 2), ALU.add), f"v{m}e")
            yield
            C.wait(pe, "xn")
            C.wait(pe, "xqTe")
            for c in range(2):
                last = pe.transpose(bank[4][:, c * P:(c + 1) * P], xnC[:, c * P:(c + 1) * P], ident[:, :])
            C.done("pe", last, "xnT")
            C.wait(act, "xnT")
            C.wait(act, "q", 1)
            C.done("act", act.copy(xT[:, :, :], halves(bank[4])), "xT")
            yield
            C.wait(pe, "xT")
            E.wait(pe, "x4", idx=i - 1)
            for m in range(2):
                for c in range(2):
                    last = pe.matmul(bank[5][:, m * P:(m + 1) * P], wqd[:, c, m * P:(m + 1) * P], xT[:, c, :],
                                     start=(c == 0), stop=(c == 1))
            C.done("pe", last, "q")
            C.wait(act, "q")
            C.wait(act, "qx", 1)
            for m in range(2):
                last = act.activation(qT[:, m, :], bank[5][:, m * P:(m + 1) * P], ACT.Identity, bias=bqd[:, m:m + 1], scale=0.25)
            C.done("act", last, "qe")
            C.wait(dve, "qe")
            C.wait(dve, "s7", 1)
            hm = head[:, :].rearrange("p (a h o) -> p a h o", a=1, o=1)
            for m in range(2):
                last = dve.tensor_tensor(qx[:, m, :, :, :], bc(qT[:, m, :].rearrange("p (b o t) -> p b o t", b=2, o=1), 2, 2),
                                         bc(bc(hm, 1, 2), 3, 64), ALU.mult)
            C.done("dve", last, "qx")
            yield
            for u in range(8):
                m, hp = divmod(u, 4)
                bk = bank[2 + u % 2]
                rows = slice(32 * hp, 32 * hp + 32)
                if u == 0:
                    C.wait(pe, "qx")
                if hp == 0:
                    C.wait(pe, f"k{m}e")
                if u == 1:
                    C.wait(pe, "k1e")
                C.wait(pe, f"e{(u - 2) % 8}", 0 if u >= 2 else 1)
                for b in range(2):
                    last = pe.matmul(bk[:, 256 * b:256 * b + 256], qx[rows, m, b, :, :].rearrange("p h t -> p (h t)"),
                                     kT[rows, m, 256 * b:256 * b + 256], start=True, stop=True)
                C.done("pe", last, f"s{u}")
                C.wait(dve, f"s{u}")
                C.wait(dve, f"e{u}", 1)
                C.done("dve", dve.tensor_reduce(nm[:, u, :], bk[:, :].rearrange("p (b n) -> p b n", b=2), AX.X, ALU.max, negate=True), f"m{u}")
                C.wait(act, f"m{u}")
                C.wait(act, f"pT{u}", 1)
                for b in range(2):
                    last = act.activation(ex[:, u, 256 * b:256 * b + 256], bk[:, 256 * b:256 * b + 256], ACT.Exp,
                                          bias=nm[:, u, b:b + 1])
                C.done("act", last, f"e{u}")
                if u % 2:
                    yield
            for u in range(8):
                bk = bank[4 + u % 2]
                C.wait(pe, f"e{u}")
                C.wait(pe, {0: "xT", 1: "qe"}.get(u, f"pT{u - 2}e"))
                for q in range(4):
                    last = pe.transpose(bk[:, q * P:(q + 1) * P], ex[:, u, q * P:(q + 1) * P], ident[:, :])
                C.done("pe", last, f"pT{u}")
                eng, en = (act, "act") if u % 2 else (dve, "dve")
                C.wait(eng, f"pT{u}")
                if u < 2:
                    C.wait(eng, "pv", 1)
                copy = act.copy if u % 2 else dve.tensor_copy
                C.done(en, copy(pT[:, u, :], bk[:, :]), f"pT{u}e")
                if u == 3:
                    yield
            yield
            C.wait(pe, "pT6e")
            C.wait(pe, "pT7e")
            C.wait(pe, "v1e")
            if not (isinstance(i, int) and i < 2):
                R.wait(pe, "before", idx=i - 2)
            for t, part in ((1, "den"), (0, "pv")):
                C.wait(pe, f"v{t}e")
                for m in range(2):
                    for b in range(2):
                        for kc in range(2):
                            q = 2 * b + kc
                            for hp in range(4):
                                u = 4 * m + hp
                                rows = slice(32 * hp, 32 * hp + 32)
                                dst = bank[t][rows, :].rearrange("p (h m b q) -> p m b h q", h=2, m=2, b=2)[:, m, b, :, :]
                                src = vv[:, q, 32 * u:32 * u + 32] if t == 0 else ones[:, 0, 0:32]
                                last = pe.matmul(dst, src, pT[:, u, q * P:(q + 1) * P].rearrange("p (h q) -> p h q", h=2),
                                                 start=(kc == 0), stop=(kc == 1))
                C.done("pe", last, part)
            C.wait(dve, "den")
            C.wait(dve, "ot", 1)
            link(dve.tensor_scalar(dn[:, 0, :], bank[1][:, 0:DIM], head[:, 0:1], None, ALU.mult))
            link(dve.scalar_tensor_tensor(out=dn[:, 1, :], in0=bank[1][:, DIM:512], scalar=head[:, 1:2], in1=dn[:, 0, :], op0=ALU.mult, op1=ALU.add))
            dve.reciprocal(dn[:, 0, :], dn[:, 1, :])
            C.wait(dve, "pv")
            link(dve.tensor_scalar(dn[:, 2, :], bank[0][:, 0:DIM], head[:, 0:1], None, ALU.mult))
            C.done("dve", dve.scalar_tensor_tensor(out=dn[:, 3, :], in0=bank[0][:, DIM:512], scalar=head[:, 1:2], in1=dn[:, 2, :],
                                                   op0=ALU.mult, op1=ALU.add), "own")
            C.wait(dve, "own")
            E.wait(dve, "yp", idx=i - 1)
            C.done("dve", dve.tensor_tensor(oT[:, :, :].rearrange("p c n -> p (c n)"), dn[:, 3, :], dn[:, 0, :], ALU.mult), "ot")
            C.end()

        def scatter():
            pool_waits.link(pool.tensor_tensor(carrier[:, 1:2], carrier[:, 0:1], carrier[:, 0:1], ALU.add))
            for k in range(TOPK):
                pool.indirect_dma_start(out=slots_d, out_offset=bass.IndirectOffsetOnAxis(ap=slot_id[:, k:k + 1], axis=0),
                                        in_=tok_id[:, 0:1], in_offset=None, bounds_check=last_slot, oob_is_err=False).then_inc(s_sc, 16)

        def stage_e(j):
            E.begin(j)
            C.wait(pe, "ot", idx=j)
            C.wait(pe, "pT7e", idx=j)
            for c in range(2):
                last = pe.matmul(bank[5][:, 0:DIM], oT[:, c, :], wod[:, c, :], start=(c == 0), stop=(c == 1))
            E.done("pe", last, "yp")
            E.wait(dve, "yp")
            C.wait(dve, "xb", idx=j)
            E.wait(dve, "x4r0", 1)
            E.done("dve", dve.tensor_tensor(x4[:, :], bank[5][:, 0:DIM], xbC[:, :], ALU.add), "x4")
            E.wait(dve, "x4")
            moments(E, stE, x4[:, :], "a")
            link(dve.tensor_scalar(stE[:, 10:11], stE[:, 7:8], stE[:, 9:10], stE[:, 9:10], ALU.mult, ALU.mult))
            E.done("dve", dve.tensor_scalar(stE[:, 11:12], stE[:, 10:11], 1e-5, None, ALU.add), "var2")
            E.wait(pool, "var2")
            E.done("pool", pool.tensor_tensor(stE[:, 12:13], stE[:, 11:12], small[:, 0:1], ALU.pow), "rstd2")
            E.wait(dve, "rstd2")
            E.wait(dve, "xnT", 1)
            E.done("dve", dve.tensor_scalar(xnE[:, 0, :], x4[:, :], stE[:, 6:7], stE[:, 9:10], ALU.subtract, ALU.mult), "xc")
            E.wait(act, "x4")
            E.wait(act, "xbE", 1)
            E.done("act", act.copy(x4r[:, :], x4[:, :]), "x4r0")
            E.wait(dve, "xc")
            link(dve.scalar_tensor_tensor(out=xnE[:, 1, :], in0=xnE[:, 0, :], scalar=stE[:, 12:13], in1=lns[:, :], op0=ALU.mult, op1=ALU.mult))
            E.wait(dve, "x4r0")
            E.done("dve", dve.tensor_tensor(xnE[:, 0, :], xnE[:, 1, :], lnb[:, :], ALU.add), "x4r")
            E.wait(pool, "x5", 1)
            E.wait(pool, "x4r0")
            E.done("pool", pool.tensor_tensor(xbE[:, :], x4r[:, :], bout[:, :], ALU.add), "xbE")
            yield
            E.wait(pe, "x4r")
            E.wait(pe, "lge", 1)
            for c in range(2):
                last = pe.transpose(bank[6][:, c * P:(c + 1) * P], xnE[:, 0, c * P:(c + 1) * P], ident[:, :])
            E.done("pe", last, "xnT")
            E.wait(act, "xnT")
            E.wait(act, "h1", 1)
            E.done("act", act.copy(xTE[:, :, :], halves(bank[6])), "xT")
            yield
            E.wait(pe, "xT")
            E.wait(pe, "x6", 1)
            for c in range(2):
                last = pe.matmul(bank[7][:, 0:P], wqk[:, c, :], xTE[:, c, :], start=(c == 0), stop=(c == 1))
            E.done("pe", last, "qk")
            E.wait(act, "qk")
            E.wait(act, "qke", 1)
            act.activation(qk[:, 1, :], bank[7][:, 0:P], ACT.Identity, bias=bqk[:, 0:1], scale=0.5)
            E.done("act", act.activation(qk[:, 0, :], bank[7][:, 0:P], ACT.Tanh, bias=bqk[:, 0:1], scale=0.5), "qku")
            E.wait(dve, "qku")
            E.wait(dve, "sim", 1)
            link(dve.scalar_tensor_tensor(out=qk2[:, :], in0=qk[:, 0, :], scalar=1.0, in1=qk[:, 1, :], op0=ALU.add, op1=ALU.mult))
            dve.tensor_scalar(qk[:, 2, :], qk2[:, :], osw[:, 0:1], osb[:, 0:1], ALU.mult, ALU.add)
            E.done("dve", dve.tensor_scalar(qk[:, 3, :], qk2[:, :], osw[:, 1:2], osb[:, 1:2], ALU.mult, ALU.add), "qke")
            yield
            for g in range(2):
                bk = bank[6 + g]
                E.wait(pe, "xT" if g == 0 else "qku")
                for c in range(2):
                    last = pe.matmul(bk[:, :], xTE[:, c, :], wh[:, c, 512 * g:512 * g + 512], start=(c == 0), stop=(c == 1))
                E.done("pe", last, f"h{g}")
                hs_ = slice(512 * g, 512 * g + 512)
                E.wait(dve, f"h{g}")
                E.wait(dve, f"hid{g}", 1)
                E.done("dve", dve.tensor_tensor(uu[:, hs_], bk[:, :], bh[:, hs_], ALU.add), f"u{g}")
                E.wait(act, f"u{g}")
                E.done("act", act.activation(th[:, hs_], uu[:, hs_], ACT.Tanh, scale=0.5), f"th{g}")
            for g in range(2):
                hs_ = slice(512 * g, 512 * g + 512)
                E.wait(dve, f"th{g}")
                E.wait(dve, "av" if g == 0 else "og", 1)
                E.done("dve", dve.scalar_tensor_tensor(out=hid[:, hs_], in0=th[:, hs_], scalar=1.0, in1=uu[:, hs_], op0=ALU.add, op1=ALU.mult), f"hid{g}")
            yield
            E.wait(pe, "qke")
            E.wait(pe, "u0")
            E.done("pe", pe.matmul(bank[6][:, 0:P], qk[:, 3, :], qk[:, 2, :], start=True, stop=True), "sim")
            E.wait(dve, "sim")
            for b in range(2):
                r = slice(64 * b, 64 * b + 64)
                last = dve.tensor_scalar(rel[r, r], bank[6][r, r], 1.0 / SEQ, 0.0, ALU.mult, ALU.max)
            E.done("dve", last, "rel")
            E.wait(dve, "rel")
            E.wait(dve, "av", 1)
            E.done("dve", dve.tensor_tensor(att[:, :], rel[:, :], rel[:, :], ALU.mult), "att")
            yield
            E.wait(pe, "att")
            E.wait(pe, "hid0")
            E.wait(pe, "u1")
            E.done("pe", pe.matmul(bank[7][:, :], att[:, :], hid[:, 0:512], start=True, stop=True), "av")
            E.wait(dve, "av")
            E.wait(dve, "hid1")
            E.wait(dve, "ogT", 1)
            E.done("dve", dve.scalar_tensor_tensor(out=og[:, :], in0=bank[7][:, :], scalar=0.25, in1=hid[:, 512:1024], op0=ALU.mult, op1=ALU.mult), "og")
            yield
            E.wait(pe, "og")
            E.wait(pe, "rel")
            for c in range(4):
                last = pe.transpose(bank[6][:, c * P:(c + 1) * P], og[:, c * P:(c + 1) * P], ident[:, :])
            E.done("pe", last, "ogT")
            E.wait(act, "ogT")
            E.wait(act, "yo", 1)
            E.done("act", act.copy(ogT[:, :, :], bank[6][:, :].rearrange("p (c n) -> p c n", c=4)), "ogTe")
            yield
            E.wait(pe, "ogTe")
            for c in range(4):
                last = pe.matmul(bank[7][:, 0:DIM], ogT[:, c, :], wout[:, c, :], start=(c == 0), stop=(c == 3))
            E.done("pe", last, "yo")
            E.wait(dve, "yo")
            E.wait(dve, "xbE")
            E.wait(dve, "x6", 1)
            E.done("dve", dve.tensor_tensor(x5[:, :], bank[7][:, 0:DIM], xbE[:, :], ALU.add), "x5")
            E.wait(dve, "x5")
            moments(E, stE, x5[:, :], "f")
            E.wait(dve, "xfT", 1)
            dve.wait_ge(s_xf, (j + 1) * 16)
            E.done("dve", dve.tensor_scalar(xf[:, :], x5[:, :], stE[:, 6:7], stE[:, 9:10], ALU.subtract, ALU.mult), "xf")
            yield
            E.wait(pe, "xf")
            E.wait(pe, "ogTe")
            for c in range(2):
                last = pe.transpose(bank[6][:, c * P:(c + 1) * P], xf[:, c * P:(c + 1) * P], ident[:, :])
            E.done("pe", last, "xfT")
            E.wait(act, "xfT")
            E.wait(act, "sh", 1)
            E.done("act", act.copy(xfT[:, :, :], halves(bank[6])), "xfTe")
            yield
            E.wait(pe, "xfTe")
            for c in range(2):
                last = pe.matmul(bank[6][:, DIM:DIM + EXPERTS], xfT[:, c, :], wr[:, c, :], start=(c == 0), stop=(c == 1))
            E.done("pe", last, "lg")
            E.wait(dve, "lg")
            E.done("dve", dve.tensor_tensor(lg[:, :], bank[6][:, DIM:DIM + EXPERTS], be[:, :], ALU.add), "lge")
            E.wait(act, "lge")
            E.done("act", act.activation(ez[:, :], lg[:, :], ACT.Exp, scale=-1.0), "ez")
            E.wait(dve, "ez")
            E.done("dve", dve.tensor_scalar(ez[:, :], ez[:, :], 1.0, None, ALU.add), "ez1")
            E.wait(dve, "ez1")
            link(dve.reciprocal(pr[:, :], ez[:, :]))
            link(dve.max(top[:, 0, :], pr[:, :]))
            link(dve.match_replace(out=ez[:, :], in_to_replace=top[:, 0, :], in_values=pr[:, :], imm_value=-1.0))
            R.wait(dve, "before", idx=j - 1)
            E.done("dve", dve.tensor_scalar(sel[:, :], ez[:, :], 0.0, None, ALU.is_lt), "sel")
            link(dve.tensor_reduce(top[:, 3, 0:1], top[:, 0, :], AX.X, ALU.add))
            link(dve.tensor_scalar(top[:, 3, 0:1], top[:, 3, 0:1], 1e-9, None, ALU.add))
            link(dve.reciprocal(top[:, 3, 1:2], top[:, 3, 0:1]))
            link(dve.tensor_scalar(top[:, 3, 1:2], top[:, 3, 1:2], 2.5, None, ALU.mult))
            E.wait(dve, "sel")
            link(dve.scalar_tensor_tensor(out=comb[:, :], in0=pr[:, :], scalar=top[:, 3, 1:2], in1=sel[:, :], op0=ALU.mult, op1=ALU.mult))
            yield
            E.wait(pe, "xfTe")
            E.wait(pe, "x5")
            for c in range(2):
                last = pe.matmul(bank[7][:, 0:P], wgs[:, c, :], xfT[:, c, :], start=(c == 0), stop=(c == 1))
            E.done("pe", last, "sh")
            E.wait(act, "sh")
            E.wait(act, "hs", 1)
            E.done("act", act.activation(ths[:, :], bank[7][:, 0:P], ACT.Tanh, scale=0.5), "ths")
            E.wait(dve, "ths")
            E.wait(dve, "ys", 1)
            E.done("dve", dve.scalar_tensor_tensor(out=hs[:, :], in0=ths[:, :], scalar=1.0, in1=bank[7][:, 0:P], op0=ALU.add, op1=ALU.mult), "hs")
            yield
            E.wait(pe, "hs")
            E.done("pe", pe.matmul(bank[7][:, 0:DIM], hs[:, :], wds[:, 0, :], start=True, stop=True), "ys")
            E.wait(dve, "ys")
            E.done("dve", dve.scalar_tensor_tensor(out=X[:, bass.ds(j, 1), :].rearrange("p a n -> p (a n)"), in0=bank[7][:, 0:DIM],
                                                   scalar=0.5, in1=x5[:, :], op0=ALU.mult, op1=ALU.add), "x6")
            E.wait(sp, "xf")
            sp.dma_start(xf_d[bass.ds(j, 1)].rearrange("a p n -> (a p) n"), xf[:, :]).then_inc(s_xf, 16)
            E.end()

        def stage_r(j, with_c):
            R.begin(j)
            R.wait(pool, "ids", 1)
            scatter()
            E.wait(pe, "sel", idx=j)
            if with_c:
                C.wait(pe, "v1e", idx=j + 2)
            else:
                C.wait(pe, "own", idx=TILES - 1)
            R.wait(pe, "before", 1)
            pe.matmul(bank[1][:, 0:EXPERTS], tri[:, 0, :], sel[:, :], start=True, stop=False)
            R.done("pe", pe.matmul(bank[1][:, 0:EXPERTS], ones[:, 0, :], before[:, :], start=False, stop=True), "rank")
            R.wait(dve, "rank")
            link(dve.tensor_tensor(lg[:, :], bank[1][:, 0:EXPERTS], base[:, :], ALU.add))
            R.done("dve", dve.tensor_tensor(before[:, :], before[:, :], sel[:, :], ALU.add), "before")
            link(dve.tensor_tensor(lg[:, :], lg[:, :], sel[:, :], ALU.mult))
            link(dve.max(top[:, 1, :], lg[:, :]))
            for k in range(TOPK):
                last = dve.scalar_tensor_tensor(out=junk[:, k, :], in0=lg[:, :], scalar=top[:, 1, k:k + 1], in1=comb[:, :],
                                                op0=ALU.is_equal, op1=ALU.mult, accum_out=top[:, 2, k:k + 1])
            link(last)
            dve.wait_ge(s_sc, (j + 1) * 16 * TOPK)
            dve.tensor_scalar(slot_id[:, :], top[:, 1, :], 1.0, None, ALU.subtract).then_inc(dchain.sem, 1)
            dchain.n += 1
            R.done("dve", dve.tensor_copy(tok_id[:, :], tokens[:, bass.ds(j, 1)]), "tok")
            dve.wait_ge(dchain.sem, dchain.n)
            R.done("dve", dve.tensor_copy(slots[:, bass.ds(j, 1), :].rearrange("p a n -> p (a n)"), lg[:, :]), "ids")
            R.done("dve", dve.tensor_copy(wts[:, bass.ds(j, 1), :].rearrange("p a n -> p (a n)"), top[:, 2, :]), "wts")
            R.wait(dve, "wts")
            link(dve.memset(idle[:, 0:1], 0.0))
            R.end()
            yield

        def step(s, do_c, do_e, do_r):
            parts = {"C": stage_c(s) if do_c else iter(()), "E": stage_e(s - 1) if do_e else iter(()),
                     "R": stage_r(s - 2, do_c) if do_r else iter(())}
            for which in "CECCEECEECRECCECECECCEECE":
                next(parts[which], None)
            for part in parts.values():
                for _ in part:
                    pass
            dchain.reset()
            pool_waits.reset()

        step(0, True, False, False)
        step(1, True, True, False)
        with nc.Fori(2, TILES, 1) as s:
            step(s, True, True, True)
        step(TILES, False, True, True)
        step(TILES + 1, False, False, True)
        R.wait(pool, "ids", idx=TILES - 1)
        scatter()
        pool_waits.reset()
        R.wait(pe, "before", idx=TILES - 1)
        s_pl = sem("s_plan")
        pe.matmul(bank[0][:, 0:EXPERTS], ones[:, 0, :], before[:, :], start=True, stop=True).then_inc(s_pl, 1)
        dve.wait_ge(s_pl, 1)
        blocks = sb("blocks", [P, EXPERTS], I32)
        bf = sb("bf", [P, EXPERTS])
        ends = sb("ends", [P, EXPERTS])
        steps = sb("steps", [P, 3])
        done = sb("done", [P, 3, EXPERTS])
        st = sb("st", [P, 3, 4])
        blk = sb("blk", [P, 3], U32)
        expert = sb("expert", [P, 3], U32)
        taken = sb("taken", [P, 3, P], U32)
        takenf = sb("takenf", [P, 3, P])
        sp.dma_start(steps[:, :], a["c_steps"]).then_inc(s_mark, 16)
        link(dve.tensor_scalar(blocks[:, :], bank[0][:, 0:EXPERTS], P - 1.0, None, ALU.add))
        link(dve.tensor_scalar(blocks[:, :], blocks[:, :], 7, None, ALU.logical_shift_right))
        link(dve.tensor_copy(bf[:, :], blocks[:, :]))
        link(dve.tensor_tensor_scan(ends[:, :], ones_e[:, :], bf[:, :], 0.0, ALU.mult, ALU.add))
        link(dve.tensor_tensor(bf[:, :], ends[:, :], bf[:, :], ALU.subtract))
        link(dve.scalar_tensor_tensor(out=bf[:, :], in0=bf[:, :], scalar=float(P), in1=base[:, :], op0=ALU.mult, op1=ALU.subtract))
        link(dve.tensor_scalar(shift[:, :], bf[:, :], 1.0, None, ALU.add))
        dve.wait_ge(s_mark, 16)
        for g in range(3):
            link(dve.tensor_scalar(done[:, g, :], ends[:, :], steps[:, g:g + 1], None, ALU.is_le))
            link(dve.tensor_reduce(st[:, g, 0:1], done[:, g, :], AX.X, ALU.add))
            link(dve.tensor_tensor(done[:, g, :], done[:, g, :], ends[:, :], ALU.mult))
            link(dve.tensor_reduce(st[:, g, 1:2], done[:, g, :], AX.X, ALU.max))
            link(dve.tensor_tensor(st[:, g, 2:3], steps[:, g:g + 1], st[:, g, 1:2], ALU.subtract))
            link(dve.scalar_tensor_tensor(out=blk[:, g:g + 1], in0=st[:, g, 0:1], scalar=float(REGION), in1=st[:, g, 2:3], op0=ALU.mult, op1=ALU.add))
            link(dve.tensor_scalar(expert[:, g:g + 1], st[:, g, 0:1], EXPERTS - 1.0, None, ALU.min))
        dve.memset(idle[:, 0:1], 0.0).then_inc(s_pl, 1)
        dchain.reset()
        sp.wait_ge(s_pl, 2)
        sp.dma_start(todo_d.rearrange("(p g) n -> p (g n)", p=P), expert[:, :]).then_inc(s_mark, 16)
        sp.wait_ge(s_mark, 32)
        sp.dma_start(todo_row[:, :], todo_d.rearrange("(o t) n -> o (t n)", o=1)).then_inc(s_mark, 16)
        pool.wait_ge(s_pl, 2)
        pool.wait_ge(s_sc, 16 * TOPK * (TILES + 1))
        s_t = [sem(f"s_taken{g}") for g in range(3)]
        for g in range(3):
            pool.indirect_dma_start(out=taken[:, g, :], out_offset=None, in_=slots_d.rearrange("(q p) o -> q (p o)", p=P),
                                    in_offset=bass.IndirectOffsetOnAxis(ap=blk[:, g:g + 1], axis=0)).then_inc(s_t[g], 16)
        for g in range(3):
            dve.wait_ge(s_t[g], 16)
            dve.tensor_copy(takenf[:, g, :], taken[:, g, :]).then_inc(s_pl, 1)
            pe.wait_ge(s_pl, 3 + g)
            pe.transpose(bank[1][:, g * P:(g + 1) * P], takenf[:, g, :], ident[:, :]).then_inc(s_set, 1)
        dve.wait_ge(s_set, 10)
        dve.tensor_copy(who[:, :].rearrange("s (p g) -> s g p", g=3), bank[1][:, 0:3 * P].rearrange("s (g p) -> s g p", g=3)).then_inc(s_pl, 1)
        dve.wait_ge(s_pl, 6)
        sp.wait_ge(s_mark, 48)
        sp.wait_ge(s_xf, 16 * (TILES + 1))
        E.wait(sp, "x6", idx=TILES - 1)
        R.wait(sp, "wts", idx=TILES - 1)
    nc.all_engine_barrier()


def experts(nc, a, plan, sem, bank, ident, who, todo_row, xf_d, y_d, pool_waits, carrier):
    pe, dve, act, pool, sp = nc.tensor, nc.vector, nc.scalar, nc.gpsimd, nc.sync
    DEEP = 8
    UP, DOWN = 2, 4
    HALF = DEEP // 2
    ph = ExitStack()
    with ph:
        def ring(name, shape, dt=F32):
            return [ph.enter_context(nc.sbuf_tensor(f"{name}{z}", shape, dt)) for z in range(DEEP)]

        mine = [ph.enter_context(nc.sbuf_tensor(f"mine{f}", [P, HALF], U32)) for f in range(2)]
        w = ring("w", [P, DIM + DIM])
        xg = ring("xg", [P, DIM])
        xgT = ring("xgT", [P, 2, P])
        h = ring("h", [P, P])
        y = ring("y", [P, DIM])
        s_w = [sem(f"s_w{z}") for z in range(DEEP)]
        s_g = [sem(f"s_g{z}") for z in range(DEEP)]
        s_y = [sem(f"s_y{z}") for z in range(DEEP)]
        s_z = sem("s_zero")
        for z in range(DEEP):
            dve.memset(xg[z][:, :], 0.0).then_inc(s_z, 1)
        pool.wait_ge(s_z, DEEP)
        last_token = pool.to_reg(TOKENS - 1)
        rows = xf_d.rearrange("t p n -> (t p) n")
        y_blocks = y_d.rearrange("(q p) n -> q p n", p=P)
        T, U, D = (Steps(nc, sem, n) for n in ("T", "U", "D"))
        s_mine = [sem(f"s_mine{f}") for f in range(2)]

        def indices(s, f):
            for z in range(HALF * f, HALF * f + HALF):
                dve.wait_ge(s_g[z], s * 16)
            dve.tensor_copy(mine[f][:, :], who[:, bass.ds(s * DEEP + HALF * f, HALF)]).then_inc(s_mine[f], 1)

        def load(s, z):
            b = s * DEEP + z
            e = sp.value_load(todo_row[0:1, bass.ds(b, 1)])
            D.wait(sp, "pe", b - DEEP)
            sp.dma_start(w[z][:, :], a["wexp"][bass.ds(e, 1)].rearrange("a p n -> (a p) n")).then_inc(s_w[z], 16)
            if z % 2 == 0:
                T.wait(pool, "pe", b + 1 - DEEP)
                pool.wait_ge(s_mine[z // HALF], s + 1)
                pool_waits.link(pool.tensor_tensor(carrier[:, 1:2], carrier[:, 0:1], carrier[:, 0:1], ALU.add))
                for g in (z, z + 1):
                    pool.indirect_dma_start(out=xg[g][:, :], out_offset=None, in_=rows,
                                            in_offset=bass.IndirectOffsetOnAxis(ap=mine[g // HALF][:, g % HALF:g % HALF + 1], axis=0),
                                            bounds_check=last_token, oob_is_err=False).then_inc(s_g[g], 16)

        def turn(s, z):
            b, bk = s * DEEP + z, bank[z % 4]
            pe.wait_ge(s_g[z], (s + 1) * 16)
            T.wait(pe, "dve", b - 4)
            for c in range(2):
                last = pe.transpose(bk[:, c * P:(c + 1) * P], xg[z][:, c * P:(c + 1) * P], ident[:, :])
            T.done("pe", last)
            T.wait(dve, "pe", b)
            U.wait(dve, "pe", b - DEEP)
            T.done("dve", dve.tensor_copy(xgT[z][:, :, :], bk[:, 0:2 * P].rearrange("p (c n) -> p c n", c=2)))

        def up(s, z):
            b, bk = s * DEEP + z, bank[4 + z % 2]
            pe.wait_ge(s_w[z], (s + 1) * 16)
            T.wait(pe, "dve", b)
            U.wait(pe, "act", b - 2)
            for c in range(2):
                last = pe.matmul(bk[:, 0:P], w[z][:, c * P:(c + 1) * P], xgT[z][:, c, :], start=(c == 0), stop=(c == 1))
            U.done("pe", last)
            U.wait(act, "pe", b)
            D.wait(act, "pe", b - DEEP)
            U.done("act", act.activation(h[z][:, :], bk[:, 0:P], ACT.Silu))

        def down(s, z):
            b, bk = s * DEEP + z, bank[6 + z % 2]
            U.wait(pe, "act", b)
            D.wait(pe, "dve", b - 2)
            D.done("pe", pe.matmul(bk[:, 0:DIM], h[z][:, :], w[z][:, DIM:2 * DIM], start=True, stop=True))
            D.wait(dve, "pe", b)
            dve.wait_ge(s_y[z], s * 16)
            D.done("dve", dve.tensor_copy(y[z][:, :], bk[:, 0:DIM]))

        def store(s, z):
            b = s * DEEP + z
            D.wait(act, "dve", b)
            act.dma_start(y_blocks[bass.ds(b, 1)].rearrange("a p n -> (a p) n"), y[z][:, :]).then_inc(s_y[z], 16)

        def run(s, first=False, last=False):
            for z in range(DEEP):
                if not last:
                    if z == HALF:
                        indices(s + 1, 0)
                    if z == 0:
                        indices(s, 1)
                    load(s, z)
                for part, lag in ((down, DOWN), (up, UP)):
                    if z >= lag and not last:
                        part(s, z - lag)
                    elif z < lag and not first:
                        part(s - 1, z - lag + DEEP)
                if not last:
                    turn(s, z)
                if z >= DOWN and not last:
                    store(s, z - DOWN)
                elif z < DOWN and not first:
                    store(s - 1, z - DOWN + DEEP)
            pool_waits.reset()

        indices(0, 0)
        run(0, first=True)
        with nc.Fori(1, BLOCKS // DEEP, 1) as s:
            run(s)
        run(BLOCKS // DEEP, last=True)
        for z in range(DEEP):
            sp.wait_ge(s_y[z], 16 * (BLOCKS // DEEP))
    nc.all_engine_barrier()


def combine(nc, plan, sem, X, slots, shift, wts, y_d, out, dchain, pool_waits, carrier):
    dve, pool, sp = nc.vector, nc.gpsimd, nc.sync
    ph = ExitStack()
    with ph:
        def pair(name, shape, dt=F32):
            return [ph.enter_context(nc.sbuf_tensor(f"{name}{z}", shape, dt)) for z in range(2)]

        ids, wt = pair("ids", [P, TOPK], U32), pair("wt", [P, TOPK])
        g, acc = pair("g", [P, TOPK, DIM]), pair("acc", [P, 2, DIM])
        moved = ph.enter_context(nc.sbuf_tensor("moved", [P, 2, EXPERTS], F32))
        top = ph.enter_context(nc.sbuf_tensor("top_rows", [P, 8], F32))
        s_row = [[sem(f"s_row{z}{k}") for k in range(TOPK)] for z in range(2)]
        s_o = [sem(f"s_o{z}") for z in range(2)]
        for z in range(2):
            sp.sem_inc(s_o[z], 16)
        T = Stage(nc, sem, "S", plan)
        I = Stage(nc, sem, "I", plan)

        def rows_of(s, z):
            mine = slots[:, bass.ds(s * 2 + z, 1), :].rearrange("p a n -> p (a n)")
            dchain.link(dve.tensor_tensor(moved[:, 0, :], mine, shift[:, :], ALU.add))
            dchain.link(dve.scalar_tensor_tensor(out=moved[:, 1, :], in0=mine, scalar=0.0, in1=moved[:, 0, :], op0=ALU.is_gt, op1=ALU.mult))
            dchain.link(dve.max(top[:, :], moved[:, 1, :]))
            I.done("dve", dve.tensor_scalar(ids[z][:, :], top[:, :], 1.0, None, ALU.subtract), f"ids{z}")

        def run(s, last):
            T.begin(s)
            for z in range(2):
                I.wait(pool, f"ids{z}", idx=s)
                T.wait(pool, f"acc{z}", 1)
                pool_waits.link(pool.tensor_tensor(carrier[:, 1:2], carrier[:, 0:1], carrier[:, 0:1], ALU.add))
                for k in range(TOPK):
                    pool.indirect_dma_start(out=g[z][:, k, :], out_offset=None, in_=y_d,
                                            in_offset=bass.IndirectOffsetOnAxis(ap=ids[z][:, k:k + 1], axis=0)).then_inc(s_row[z][k], 16)
            if not last:
                I.begin(s + 1)
            for z in range(2):
                i = s * 2 + z
                T.wait(dve, f"acc{z}", 1)
                T.done("dve", dve.tensor_copy(wt[z][:, :], wts[:, bass.ds(i, 1), :].rearrange("p a n -> p (a n)")), f"wt{z}")
                T.wait(dve, f"wt{z}")
                dve.wait_ge(s_o[z], (s + 1) * 16)
                for k in range(TOPK):
                    dve.wait_ge(s_row[z][k], (s + 1) * 16)
                    prev = X[:, bass.ds(i, 1), :].rearrange("p a n -> p (a n)") if k == 0 else acc[z][:, (k - 1) % 2, :]
                    ins = dve.scalar_tensor_tensor(out=acc[z][:, k % 2, :], in0=g[z][:, k, :], scalar=wt[z][:, k:k + 1], in1=prev,
                                                   op0=ALU.mult, op1=ALU.add)
                    if k < TOPK - 1:
                        dchain.link(ins)
                T.done("dve", ins, f"acc{z}")
                T.wait(sp, f"acc{z}")
                sp.dma_start(out.rearrange("(t p) n -> t p n", p=P)[bass.ds(i, 1)].rearrange("a p n -> (a p) n"),
                             acc[z][:, (TOPK - 1) % 2, :]).then_inc(s_o[z], 16)
                if not last:
                    rows_of(s + 1, z)
            if not last:
                I.end()
            T.end()
            dchain.reset()
            pool_waits.reset()

        I.begin(0)
        for z in range(2):
            rows_of(0, z)
        I.end()
        dchain.reset()
        with nc.Fori(0, TILES // 2 - 1, 1) as s:
            run(s, False)
        run(TILES // 2 - 1, True)
        for z in range(2):
            sp.wait_ge(s_o[z], 16 * (TILES // 2 + 1))


def program(nc, a, out, plan):
    ctx = ExitStack()
    with ctx:
        pe, dve, act, pool, sp = nc.tensor, nc.vector, nc.scalar, nc.gpsimd, nc.sync

        def sb(name, shape, dt=F32):
            return ctx.enter_context(nc.sbuf_tensor(name, shape, dt))

        bank = [ctx.enter_context(nc.psum_tensor(f"bank{k}", [P, 512], F32)) for k in range(8)]

        def sem(name):
            return ctx.enter_context(nc.semaphore(name))

        X = sb("X", [P, TILES, DIM])
        XN = sb("XN", [P, TILES, DIM])
        amax = sb("amax", [P, 2])
        ident = sb("ident", [P, P])
        head = sb("head", [P, 2])
        small = sb("small", [P, 16])
        idle = sb("idle", [1, 1])
        s_const, s_w0, s_setup = sem("s_const"), sem("s_rope"), sem("s_setup")
        dchain = Chain(nc, ctx, dve, "dve_chain")
        pool_waits = Chain(nc, ctx, pool, "pool_waits")
        carrier = sb("carrier", [1, 2])

        slots, wts, shift = sb("slots", [P, TILES, EXPERTS]), sb("wts", [P, TILES, TOPK]), sb("shift", [P, EXPERTS])
        who = sb("who", [P, 3 * P], U32)
        todo_row = sb("todo_row", [1, 3 * P], U32)
        slots_d = nc.dram_tensor("slots_d", (ROWS, 1), U32, kind="Internal").ap()
        xf_d = nc.dram_tensor("xf_d", (TILES, P, DIM), F32, kind="Internal").ap()
        todo_d = nc.dram_tensor("todo_d", (3 * P, 1), U32, kind="Internal").ap()
        y_d = nc.dram_tensor("y_d", (BLOCKS * P, DIM), F32, kind="Internal").ap()
        resident, loads = phase2_weights(a, sb)
        tern, wf = resident[:2]
        bqd, bqk = resident[6], resident[15]
        sc = sb("sc", [P, 8])
        s_load, s_prep = sem("s_load"), sem("s_prep")
        n_const = 0

        def const(dst, src):
            nonlocal n_const
            sp.dma_start(dst, src).then_inc(s_const, 16)
            n_const += 1

        const(ident[:, :], a["c_ident"])
        const(head[:, :], a["c_head"])

        ph1 = ExitStack()
        with ph1:
            def sb1(name, shape, dt=F32):
                return ph1.enter_context(nc.sbuf_tensor(name, shape, dt))

            wq0 = sb1("wq0", [P, 2, 512])
            wk0 = sb1("wk0", [CW, 2, 512])
            wv0 = sb1("wv0", [CW, 2, 512])
            wo0 = sb1("wo0", [P, 4, DIM])
            bo0 = sb1("bo0", [P, DIM])
            const(wq0[:, :, :], a["wq0"].rearrange("(c p) n -> p c n", p=P))
            const(wk0[:, :, :], a["wk0"].rearrange("(c p) n -> p c n", p=CW))
            const(wv0[:, :, :], a["wv0"].rearrange("(c p) n -> p c n", p=CW))
            const(wo0[:, :, :], a["wo0"].rearrange("(c p) n -> p c n", p=P))
            const(bo0[:, :], bc(a["bo0"].rearrange("(a n) -> a n", a=1), 0, P))
            wqs = sb1("wqs", [P, 2, DIM])
            wla = sb1("wla", [P, 2, P])
            wlb = sb1("wlb", [P, DIM])
            wos = sb1("wos", [P, 2, DIM])
            gam = sb1("gam", [P, DIM])
            bet = sb1("bet", [P, DIM])
            rope = sb1("rope", [P, 2 * P])
            wraw = sb1("wraw", [P, 3, DIM])
            const(wraw[:, 0:2, :], a["wqs"].rearrange("(c p) n -> p c n", p=P))
            const(wraw[0:64, 2, :], a["wkb"])
            const(wlb[64:128, :], a["wvb"])
            const(wla[:, :, 0:64], a["wka"].rearrange("(c p) n -> p c n", p=P))
            const(wla[:, :, 64:128], a["wva"].rearrange("(c p) n -> p c n", p=P))
            const(wos[:, :, :], a["wos"].rearrange("(c p) n -> p c n", p=P))
            const(gam[:, :], bc(a["gam"].rearrange("(a n) -> a n", a=1), 0, P))
            const(bet[:, :], bc(a["bet"].rearrange("(a n) -> a n", a=1), 0, P))
            const(rope[:, :], bc(a["c_rope"], 0, P))

            xin = sb1("xin", [P, DIM])
            cT = sb1("cT", [CW, 2, 512])
            mk = sb1("mk", [P, 512], U8)
            s_x, s_c, s_m = sem("s_x"), sem("s_c"), sem("s_m")
            stA = sb1("stA", [P, 16])
            xnA = sb1("xnA", [P, DIM])
            xb = sb1("xb", [P, DIM])
            xT = sb1("xT", [P, 2, P])
            qx = sb1("qx", [P, 2, 4, P])
            kT = sb1("kT", [P, 4, 512])
            vv = sb1("vv", [P, 4, 512])
            mb = sb1("mb", [P, 512])
            sm = sb1("sm", [P, 4, 512])
            nm = sb1("nm", [P, 8])
            sums = sb1("sums", [P, 8])
            rec = sb1("rec", [P, 8])
            pT = sb1("pT", [P, 4, 512])
            oA = sb1("oA", [P, 4, 2, 64])
            oT = sb1("oT", [P, 4, P])
            xB = sb1("xB", [P, DIM])

            xr = sb1("xr", [P, DIM])
            stB = sb1("stB", [P, 16])
            xnB = sb1("xnB", [P, DIM])
            xTB = sb1("xTB", [P, 2, P])
            lat = sb1("lat", [P, P])
            qTB = sb1("qTB", [P, 2, P])
            kx = sb1("kx", [P, 2, 2, P])
            vB = sb1("vB", [P, DIM])
            negm = sb1("negm", [P, H1])
            pB = sb1("pB", [P, H1, P])
            pTB = sb1("pTB", [P, H1, P])
            dn = sb1("dn1", [P, 4, DIM])
            ones = sb1("ones1", [P, 32])
            oTB = sb1("oTB", [P, 2, P])
            x2 = sb1("x2", [P, DIM])
            t3 = sb1("t3", [P, 2, DIM])
            wtmp = sb1("wtmp", [P, 2, DIM])
            mark = sb1("mark", [P, ROWS // P // 4], U32)

            pool.memset(small[:, 0:1], -0.5).then_inc(s_setup, 1)
            pool.memset(carrier[:, :], 0.0).then_inc(s_setup, 1)
            pool.memset(qx[:, :, :, :], 0.0).then_inc(s_setup, 1)
            pool.memset(pB[:, :, :], 0.0).then_inc(s_setup, 1)
            pool.memset(amax[:, :], 0.0).then_inc(s_setup, 1)
            pool.memset(ones[:, :], 1.0).then_inc(s_setup, 1)
            for e in (pe, dve, act, pool):
                e.wait_ge(s_const, 16 * n_const)
                e.wait_ge(s_setup, 6)

            A, B = Stage(nc, sem, "A", plan), Stage(nc, sem, "B", plan)

            def stage_a(i):
                A.begin(i)
                A.wait(sp, "xb", 1)
                sp.dma_start(xin[:, :], a["x"][bass.ds(i, 1)].rearrange("a p n -> (a p) n")).then_inc(s_x, 16)
                A.wait(sp, "v3", 1)
                sp.dma_start(cT[:, :, :], a["ctx"][bass.ds(i, 1)].rearrange("a p c n -> (a p) c n")).then_inc(s_c, 16)
                A.wait(act, "mb", 1)
                act.dma_start(mk[:, :], bc(a["mask"][bass.ds(i, 1)], 0, P)).then_inc(s_m, 16)
                pe.wait_ge(s_c, (i + 1) * 16)
                for m in range(4):
                    bk = bank[2 + m % 2]
                    A.wait(pe, f"k{m - 2}e" if m >= 2 else f"t{m + 2}", 0 if m >= 2 else 1)
                    for c in range(2):
                        last = pe.matmul(bk[:, :], wk0[:, c, m * P:(m + 1) * P], cT[:, c, :], start=(c == 0), stop=(c == 1))
                    A.done("pe", last, f"k{m}")
                    A.wait(act, f"k{m}")
                    if m == 0:
                        A.wait(act, "s3", 1)
                    A.done("act", act.copy(kT[:, m, :], bk[:, :]), f"k{m}e")
                    if m % 2:
                        yield
                dve.wait_ge(s_x, (i + 1) * 16)
                dchain.link(dve.bn_stats(stA[:, 0:6], xin[:, :]))
                dchain.link(dve.bn_aggr(stA[:, 6:8], stA[:, 0:6]))
                A.done("dve", dve.tensor_scalar(stA[:, 8:9], stA[:, 7:8], 1e-5, None, ALU.add), "var")
                A.wait(pool, "var")
                A.done("pool", pool.tensor_tensor(stA[:, 9:10], stA[:, 8:9], small[:, 0:1], ALU.pow), "rstd")
                A.wait(dve, "rstd")
                A.wait(dve, "xnT", 1)
                A.done("dve", dve.tensor_scalar(xnA[:, :], xin[:, :], stA[:, 6:7], stA[:, 9:10], ALU.subtract, ALU.mult), "xn")
                B.wait(pool, "y", idx=i - 1)
                A.wait(pool, "xn")
                A.done("pool", pool.tensor_tensor(xb[:, :], xin[:, :], bo0[:, :], ALU.add), "xb")
                yield
                A.wait(pe, "xn")
                A.wait(pe, "oTe", 1)
                pe.transpose(bank[4][:, 0:P], xnA[:, 0:P], ident[:, :])
                A.done("pe", pe.transpose(bank[4][:, P:2 * P], xnA[:, P:2 * P], ident[:, :]), "xnT")
                A.wait(act, "xnT")
                A.wait(act, "q", 1)
                A.done("act", act.copy(xT[:, :, :], bank[4][:, 0:2 * P].rearrange("p (c n) -> p c n", c=2)), "xT")
                A.wait(pe, "xT")
                B.wait(pe, "y", idx=i - 1)
                for m in range(4):
                    for c in range(2):
                        last = pe.matmul(bank[5][:, m * P:(m + 1) * P], wq0[:, c, m * P:(m + 1) * P], xT[:, c, :],
                                         start=(c == 0), stop=(c == 1))
                A.done("pe", last, "q")
                A.wait(act, "q")
                A.wait(act, "s3", 1)
                for h2 in range(2):
                    src = bank[5][64 * h2:64 * h2 + 64, :].rearrange("p (m b t) -> p b m t", m=4, b=2)
                    last = act.copy(qx[64 * h2:64 * h2 + 64, :, :, 64 * h2:64 * h2 + 64], src)
                A.done("act", last, "qx")
                yield
                dve.wait_ge(s_m, (i + 1) * 16)
                A.done("dve", dve.tensor_scalar(mb[:, :], mk[:, :], 1.0, -NEG, ALU.subtract, ALU.mult), "mb")
                A.wait(pe, "qx")
                for hp in range(4):
                    bk = bank[2 + hp % 2]
                    A.wait(pe, f"k{hp}e")
                    A.wait(pe, f"t{hp - 2}" if hp >= 2 else f"k{hp + 2}e")
                    for b in range(2):
                        last = pe.matmul(bk[:, 256 * b:256 * b + 256], qx[:, b, hp, :], kT[:, hp, 256 * b:256 * b + 256],
                                         start=True, stop=True)
                    A.done("pe", last, f"s{hp}")
                    A.wait(dve, f"s{hp}")
                    if hp == 0:
                        A.wait(dve, "mb")
                        A.wait(dve, "e3", 1)
                    A.wait(dve, f"pT{hp}", 1)
                    dchain.link(dve.memset(idle[:, 0:1], 0.0))
                    for b in range(2):
                        last = dve.tensor_tensor_reduce(sm[:, hp, 256 * b:256 * b + 256], bk[:, 256 * b:256 * b + 256],
                                                        mb[:, 256 * b:256 * b + 256], -0.125, -NEG, ALU.add, ALU.min,
                                                        nm[:, 2 * hp + b:2 * hp + b + 1])
                    A.done("dve", last, f"t{hp}")
                    A.wait(act, f"t{hp}")
                    if hp == 0:
                        A.wait(act, "rec", 1)
                    for b in range(2):
                        blk = sm[:, hp, 256 * b:256 * b + 256]
                        last = act.activation(blk, blk, ACT.Exp, bias=nm[:, 2 * hp + b:2 * hp + b + 1], scale=-1.0,
                                              accum_out=sums[:, 2 * hp + b:2 * hp + b + 1])
                    A.done("act", last, f"e{hp}")
                    if hp % 2:
                        yield
                for c4 in range(4):
                    bk = bank[c4 % 2]
                    A.wait(pe, f"v{c4 - 2}e" if c4 >= 2 else f"o{c4}", 0 if c4 >= 2 else 1)
                    for c in range(2):
                        last = pe.matmul(bk[:, :], cT[:, c, c4 * P:(c4 + 1) * P], wv0[:, c, :], start=(c == 0), stop=(c == 1))
                    A.done("pe", last, f"v{c4}")
                    A.wait(dve, f"v{c4}")
                    if c4 == 0:
                        A.wait(dve, "pv1", 1)
                    A.done("dve", dve.tensor_copy(vv[:, c4, :], bk[:, :]), f"v{c4}e")
                    if c4 % 2:
                        yield
                for hp in range(4):
                    bk = bank[4 + hp % 2]
                    A.wait(pe, f"e{hp}")
                    A.wait(pe, {0: "xT", 1: "qx", 2: "pT0e", 3: "pT1e"}[hp])
                    for q in range(4):
                        last = pe.transpose(bk[:, q * P:(q + 1) * P], sm[:, hp, q * P:(q + 1) * P], ident[:, :])
                    A.done("pe", last, f"pT{hp}")
                    eng, en = (act, "act") if hp % 2 else (dve, "dve")
                    A.wait(eng, f"pT{hp}")
                    if hp < 2:
                        A.wait(eng, "pv1", 1)
                    copy = act.copy if hp % 2 else dve.tensor_copy
                    A.done(en, copy(pT[:, hp, :], bk[:, :]), f"pT{hp}e")
                    if hp % 2:
                        yield
                A.wait(dve, "e3")
                A.wait(dve, "o1", 1)
                A.done("dve", dve.reciprocal(rec[:, :], sums[:, :]), "rec")
                A.wait(pe, "pT3e")
                A.wait(pe, "pT2e")
                for b in range(2):
                    A.wait(pe, f"v{b + 2}e")
                    for hp in range(4):
                        for kc in range(2):
                            q = 2 * b + kc
                            last = pe.matmul(bank[b][:, hp * P:(hp + 1) * P], pT[:, hp, q * P:(q + 1) * P],
                                             vv[:, q, hp * P:(hp + 1) * P], start=(kc == 0), stop=(kc == 1))
                    A.done("pe", last, f"pv{b}")
                    A.wait(dve, f"pv{b}")
                    if b == 0:
                        A.wait(dve, "rec")
                        A.wait(dve, "oT", 1)
                    for h2 in range(2):
                        r = slice(64 * h2, 64 * h2 + 64)
                        src = bank[b][r, :].rearrange("p (m n) -> p m n", m=4)[:, :, 64 * h2:64 * h2 + 64]
                        w = bc(rec[r, b:8:2].rearrange("p (m o) -> p m o", o=1), 2, 64)
                        last = dve.tensor_tensor(oA[64 * b:64 * b + 64, :, h2, :], src, w, ALU.mult)
                    A.done("dve", last, f"o{b}")
                yield
                A.wait(pe, "o1")
                A.wait(pe, "pT2e")
                for m in range(4):
                    last = pe.transpose(bank[4][:, m * P:(m + 1) * P], oA[:, m, :, :].rearrange("p a n -> p (a n)"), ident[:, :])
                A.done("pe", last, "oT")
                A.wait(act, "oT")
                B.wait(act, "yp0", idx=i - 1)
                A.done("act", act.copy(oT[:, :, :], bank[4][:, :].rearrange("p (m n) -> p m n", m=4)), "oTe")
                A.end()

            def stage_b(j):
                B.begin(j)
                A.wait(pe, "oTe", idx=j)
                A.wait(pe, "pT3e", idx=j)
                for m in range(4):
                    last = pe.matmul(bank[5][:, 0:DIM], oT[:, m, :], wo0[:, m, :], start=(m == 0), stop=(m == 3))
                B.done("pe", last, "yp0")
                B.wait(dve, "yp0")
                A.wait(dve, "xb", idx=j)
                B.wait(dve, "xr", 1)
                B.done("dve", dve.tensor_tensor(xB[:, :], bank[5][:, 0:DIM], xb[:, :], ALU.add), "y")
                B.wait(dve, "y")
                dchain.link(dve.bn_stats(stB[:, 0:6], xB[:, :]))
                dchain.link(dve.bn_aggr(stB[:, 6:8], stB[:, 0:6]))
                B.done("dve", dve.tensor_scalar(stB[:, 8:9], stB[:, 7:8], 1e-5, None, ALU.add), "var")
                B.wait(pool, "var")
                B.done("pool", pool.tensor_tensor(stB[:, 9:10], stB[:, 8:9], small[:, 0:1], ALU.pow), "rstd")
                B.wait(act, "y")
                B.wait(act, "x2", 1)
                B.done("act", act.copy(xr[:, :], xB[:, :]), "xr")
                B.wait(dve, "rstd")
                B.wait(dve, "xnT", 1)
                B.done("dve", dve.tensor_scalar(xnB[:, :], xB[:, :], stB[:, 6:7], stB[:, 9:10], ALU.subtract, ALU.mult), "xnB")
                yield
                B.wait(pe, "xnB")
                B.wait(pe, "x2", 1)
                pe.transpose(bank[6][:, 0:P], xnB[:, 0:P], ident[:, :])
                B.done("pe", pe.transpose(bank[6][:, P:2 * P], xnB[:, P:2 * P], ident[:, :]), "xnT")
                B.wait(act, "xnT")
                B.wait(act, "qk", 1)
                B.done("act", act.copy(xTB[:, :, :], bank[6][:, 0:2 * P].rearrange("p (c n) -> p c n", c=2)), "xT")
                yield
                B.wait(pe, "xT")
                B.wait(pe, "own", 1)
                for c in range(2):
                    last = pe.matmul(bank[7][:, 0:P], wla[:, c, :], xTB[:, c, :], start=(c == 0), stop=(c == 1))
                B.done("pe", last, "lat")
                B.wait(act, "lat")
                B.wait(act, "v", 1)
                B.done("act", act.copy(lat[:, :], bank[7][:, 0:P]), "late")
                for m in range(2):
                    for c in range(2):
                        pe.matmul(bank[6][:, m * P:(m + 1) * P], wqs[:, c, m * P:(m + 1) * P], xTB[:, c, :],
                                  start=(c == 0), stop=(c == 1))
                B.wait(pe, "late")
                for m in range(2):
                    last = pe.matmul(bank[6][:, 256 + m * P:256 + (m + 1) * P], wlb[0:64, m * P:(m + 1) * P], lat[0:64, :],
                                     start=True, stop=True)
                B.done("pe", last, "qk")
                last = pe.matmul(bank[7][:, 0:DIM], lat[64:128, :], wlb[64:128, :], start=True, stop=True)
                B.done("pe", last, "v")
                B.wait(act, "v")
                B.wait(act, "pv", 1)
                B.done("act", act.copy(vB[:, :], bank[7][:, 0:DIM]), "ve")
                B.wait(dve, "qk")
                B.wait(dve, "s3", 1)
                dve.tensor_copy(qTB[:, :, :], bank[6][:, 0:2 * P].rearrange("p (c n) -> p c n", c=2))
                for m in range(2):
                    src = bc(bank[6][:, 256 + m * P:256 + (m + 1) * P].rearrange("p (o n) -> p o n", o=1), 1, 2)
                    last = dve.tensor_tensor(kx[:, m, :, :], src, bc(head[:, :].rearrange("p (h o) -> p h o", o=1), 2, P), ALU.mult)
                B.done("dve", last, "kx")
                yield
                for c in range(4):
                    bk = bank[6 + c % 2]
                    rows = slice(32 * c, 32 * c + 32)
                    B.wait(pe, {0: "kx", 1: "ve", 2: "d0", 3: "d1"}[c])
                    if c == 1:
                        B.wait(pe, "kx")
                    for m in range(2):
                        last = pe.matmul(bk[:, 256 * m:256 * m + 256], qTB[rows, m, :], kx[rows, m, :, :].rearrange("p h n -> p (h n)"),
                                         start=True, stop=True)
                    B.done("pe", last, f"s{c}")
                    B.wait(dve, f"s{c}")
                    hs = slice(4 * c, 4 * c + 4)
                    if c == 0:
                        B.wait(dve, "pT3", 1)
                    for b in range(2):
                        r = slice(64 * b, 64 * b + 64)
                        blk = bk[r, :].rearrange("p (h n) -> p h n", h=4)[:, :, 64 * b:64 * b + 64]
                        last = dve.tensor_reduce(negm[r, hs], blk, AX.X, ALU.max, negate=True)
                    dchain.link(last)
                    for b in range(2):
                        r = slice(64 * b, 64 * b + 64)
                        blk = bk[r, :].rearrange("p (h n) -> p h n", h=4)[:, :, 64 * b:64 * b + 64]
                        last = dve.tensor_tensor(pB[r, hs, 64 * b:64 * b + 64], blk,
                                                 bc(negm[r, hs].rearrange("p (h o) -> p h o", o=1), 2, 64), ALU.add)
                    B.done("dve", last, f"d{c}")
                    B.wait(act, f"d{c}")
                    for b in range(2):
                        r = slice(64 * b, 64 * b + 64)
                        blk = pB[r, hs, 64 * b:64 * b + 64]
                        last = act.activation(blk, blk, ACT.Exp, scale=0.25)
                    B.done("act", last, f"e{c}")
                    if c % 2:
                        yield
                for c in range(4):
                    hs = slice(4 * c, 4 * c + 4)
                    bk = bank[6 + c % 2]
                    B.wait(pe, f"e{c}")
                    B.wait(pe, {0: "d2", 1: "d3", 2: "pT0e", 3: "pT1e"}[c])
                    for h in range(4):
                        last = pe.transpose(bk[:, h * P:(h + 1) * P], pB[:, 4 * c + h, :], ident[:, :])
                    B.done("pe", last, f"pT{c}")
                    B.wait(act, f"pT{c}")
                    if c == 0:
                        B.wait(act, "pv", 1)
                    B.done("act", act.copy(pTB[:, hs, :], bk[:, :].rearrange("p (h n) -> p h n", h=4)), f"pT{c}e")
                    if c % 2:
                        yield
                B.wait(pe, "pT3e")
                B.wait(pe, "ve")
                for t, part in ((1, "den"), (0, "pv")):
                    for m in range(2):
                        for c in range(4):
                            rows = slice(32 * c, 32 * c + 32)
                            dst = bank[6 + t][rows, :].rearrange("p (h m n) -> p m h n", h=2, m=2)[:, m, :, :]
                            src = vB[:, P * m + 32 * c:P * m + 32 * c + 32] if t == 0 else ones[:, :]
                            last = pe.matmul(dst, src, pTB[:, 4 * c + 2 * m:4 * c + 2 * m + 2, :], start=True, stop=True)
                    B.done("pe", last, part)
                B.wait(dve, "den")
                B.wait(dve, "ot", 1)
                dchain.link(dve.tensor_scalar(dn[:, 0, :], bank[7][:, 0:DIM], head[:, 0:1], None, ALU.mult))
                dchain.link(dve.scalar_tensor_tensor(out=dn[:, 1, :], in0=bank[7][:, DIM:512], scalar=head[:, 1:2], in1=dn[:, 0, :],
                                                     op0=ALU.mult, op1=ALU.add))
                dve.reciprocal(dn[:, 0, :], dn[:, 1, :])
                B.wait(dve, "pv")
                dchain.link(dve.tensor_scalar(dn[:, 2, :], bank[6][:, 0:DIM], head[:, 0:1], None, ALU.mult))
                B.done("dve", dve.scalar_tensor_tensor(out=dn[:, 3, :], in0=bank[6][:, DIM:512], scalar=head[:, 1:2], in1=dn[:, 2, :],
                                                       op0=ALU.mult, op1=ALU.add), "own")
                B.wait(dve, "own")
                B.wait(dve, "yp", 1)
                B.done("dve", dve.tensor_tensor(oTB[:, :, :].rearrange("p c n -> p (c n)"), dn[:, 3, :], dn[:, 0, :], ALU.mult), "ot")
                yield
                B.wait(pe, "ot")
                for c in range(2):
                    last = pe.matmul(bank[6][:, 0:DIM], oTB[:, c, :], wos[:, c, :], start=(c == 0), stop=(c == 1))
                B.done("pe", last, "yp")
                B.wait(dve, "yp")
                B.wait(dve, "xr")
                B.wait(dve, "keep", 1)
                B.done("dve", dve.tensor_tensor(x2[:, :], bank[6][:, 0:DIM], xr[:, :], ALU.add), "x2")
                B.wait(dve, "x2")
                dchain.link(dve.bn_stats(stB[:, 0:6], x2[:, :]))
                dchain.link(dve.bn_aggr(stB[:, 6:8], stB[:, 0:6]))
                B.done("dve", dve.tensor_scalar(stB[:, 8:9], stB[:, 7:8], 1e-5, None, ALU.add), "var2")
                B.wait(pool, "var2")
                B.done("pool", pool.tensor_tensor(stB[:, 9:10], stB[:, 8:9], small[:, 0:1], ALU.pow), "rstd2")
                B.wait(dve, "rstd2")
                dchain.link(dve.tensor_scalar(stB[:, 10:11], stB[:, 7:8], stB[:, 9:10], stB[:, 9:10], ALU.mult, ALU.mult))
                B.done("dve", dve.tensor_scalar(stB[:, 11:12], stB[:, 10:11], 1e-3, None, ALU.add), "var3")
                B.wait(pool, "var3")
                B.done("pool", pool.tensor_tensor(stB[:, 12:13], stB[:, 11:12], small[:, 0:1], ALU.pow), "rstd3")
                B.wait(dve, "rstd3")
                dchain.link(dve.tensor_scalar(t3[:, 0, :], x2[:, :], stB[:, 6:7], stB[:, 9:10], ALU.subtract, ALU.mult))
                dchain.link(dve.scalar_tensor_tensor(out=t3[:, 1, :], in0=t3[:, 0, :], scalar=stB[:, 12:13], in1=gam[:, :],
                                                     op0=ALU.mult, op1=ALU.mult))
                dchain.link(dve.tensor_tensor(t3[:, 0, :], t3[:, 1, :], bet[:, :], ALU.add))
                dchain.link(dve.tensor_reduce(amax[:, 1:2], t3[:, 0, :], AX.X, ALU.max, apply_absolute_value=True))
                dchain.link(dve.tensor_tensor(amax[:, 0:1], amax[:, 0:1], amax[:, 1:2], ALU.max))
                B.done("dve", dve.tensor_copy(XN[:, bass.ds(j, 1), :].rearrange("p a n -> p (a n)"), t3[:, 0, :]), "xn3")
                B.wait(act, "x2")
                B.done("act", act.copy(X[:, bass.ds(j, 1), :].rearrange("p a n -> p (a n)"), x2[:, :]), "keep")
                B.wait(dve, "xn3")
                dchain.link(dve.memset(idle[:, 0:1], 0.0))
                B.end()

            def rotate():
                cos, sin = rope[:, 0:P], rope[:, P:2 * P]
                for c, (dst, src, np_) in enumerate([(wqs[:, 0, :], wraw[:, 0, :], P), (wqs[:, 1, :], wraw[:, 1, :], P),
                                                     (wlb[0:64, :], wraw[0:64, 2, :], 64)]):
                    s4 = src.rearrange("p (n t) -> p t n", t=2)
                    d4 = dst.rearrange("p (n t) -> p t n", t=2)
                    tmp = t3[0:np_, 0, 0:P]
                    tmp2 = t3[0:np_, 0, P:2 * P]
                    dchain.link(dve.tensor_tensor(tmp, s4[:, 1, :], sin[0:np_], ALU.mult))
                    dchain.link(dve.tensor_tensor(tmp2, s4[:, 0, :], cos[0:np_], ALU.mult))
                    dchain.link(dve.tensor_tensor(d4[:, 0, :], tmp2, tmp, ALU.subtract))
                    dchain.link(dve.tensor_tensor(tmp, s4[:, 0, :], sin[0:np_], ALU.mult))
                    dchain.link(dve.tensor_tensor(tmp2, s4[:, 1, :], cos[0:np_], ALU.mult))
                    last = dve.tensor_tensor(d4[:, 1, :], tmp2, tmp, ALU.add)
                    dchain.link(last)
                    yield

            def step(s, do_a, do_b):
                ga = stage_a(s) if do_a else iter(())
                gb = stage_b(s - 1) if do_b else rotate()
                for which in "ABAABABABAABABABABABA":
                    next(gb if which == "B" else ga, None)
                for g in (ga, gb):
                    for _ in g:
                        pass
                dchain.reset()

            step(0, True, False)
            dve.memset(idle[:, 0:1], 0.0).then_inc(s_w0, 1)
            pe.wait_ge(s_w0, 1)
            for dst, src in loads:
                sp.dma_start(dst, src).then_inc(s_load, 16)
            pool.memset(mark[:, :], NOBODY).then_inc(s_prep, 1)
            sp.wait_ge(s_prep, 1)
            for f in range(4):
                sp.dma_start(slots_d.rearrange("(f p n) o -> f p (n o)", f=4, p=P)[f], mark[:, :]).then_inc(s_load, 16)
            with nc.Fori(1, TILES, 1) as s:
                step(s, True, True)
            link = dchain.link
            for e in (pe, dve, act, pool, sp):
                e.wait_ge(s_load, 16 * (len(loads) + 4))
            dve.tensor_reduce(sc[:, 0:1], wf[:, :, :], AX.XY, ALU.add, apply_absolute_value=True).then_inc(s_prep, 1)
            pool.wait_ge(s_prep, 2)
            pool.partition_all_reduce(sc[:, 1:2], sc[:, 0:1], P, bass.bass_isa.ReduceOp.add).then_inc(s_prep, 1)
            dve.wait_ge(s_prep, 3)
            link(dve.tensor_scalar(sc[:, 1:2], sc[:, 1:2], 1.0 / (DIM * DIM), None, ALU.mult))
            link(dve.tensor_scalar(sc[:, 5:6], sc[:, 1:2], 1e-5, None, ALU.add))
            link(dve.reciprocal(sc[:, 6:7], sc[:, 5:6]))
            link(dve.tensor_scalar(wtmp[:, :, :], wf[:, :, :], sc[:, 6:7], None, ALU.mult))
            link(dve.tensor_scalar(tern[:, :, :], wtmp[:, :, :], 0.5, None, ALU.is_gt))
            link(dve.tensor_scalar(wtmp[:, :, :], wtmp[:, :, :], -0.5, None, ALU.is_lt))
            link(dve.tensor_tensor(tern[:, :, :], tern[:, :, :], wtmp[:, :, :], ALU.subtract))
            link(dve.tensor_scalar(bqd[:, :], bqd[:, :], 0.25, None, ALU.mult))
            link(dve.tensor_scalar(bqk[:, :], bqk[:, :], 0.5, None, ALU.mult))
            dchain.reset()
            step(TILES, False, True)
            B.wait(dve, "keep", idx=TILES - 1)
            B.wait(pool, "xn3", idx=TILES - 1)
            B.wait(pool, "keep", idx=TILES - 1)
        nc.all_engine_barrier()
        phase2(nc, a, plan, (slots, wts, shift, who, todo_row, slots_d, xf_d, todo_d), sem, bank, X, XN, ident, head, small, idle,
               dchain, amax, pool_waits, carrier, resident, sc)
        experts(nc, a, plan, sem, bank, ident, who, todo_row, xf_d, y_d, pool_waits, carrier)
        combine(nc, plan, sem, X, slots, shift, wts, y_d, out, dchain, pool_waits, carrier)


def lay_out(i):
    c = np.ascontiguousarray
    t = lambda k: c(np.asarray(i[k]).T)
    ctx = np.asarray(i["ctx_768"]).reshape(TILES, 512, 2, CW)
    d = {
        "x": np.asarray(i["x"]).reshape(TILES, P, DIM),
        "ctx": c(ctx.transpose(0, 3, 2, 1)),
        "mask": np.asarray(i["mask_BxS2_bk0"]).reshape(TILES, 512),
        "wq0": np.asarray(i["L0_xattn_W_q"]), "wk0": np.asarray(i["L0_xattn_W_k"]), "wv0": np.asarray(i["L0_xattn_W_v"]),
        "wo0": np.asarray(i["L0_xattn_W_o"]), "bo0": np.asarray(i["L0_xattn_b_o"]),
        "wqs": t("L0_attn_wq"), "wka": t("L0_attn_wk_a"), "wkb": t("L0_attn_wk_b"), "wva": t("L0_attn_wv_a"),
        "wvb": t("L0_attn_wv_b"), "wos": t("L0_attn_wo"),
        "gam": np.asarray(i["L0_ffn_ln_gamma"]), "bet": np.asarray(i["L0_ffn_ln_beta"]),
    }
    for k, v in {"wf": "L0_ffn_weight", "bqd": "L1_xattn_bq", "bkd": "L1_xattn_bk", "bvd": "L1_xattn_bv", "bod": "L1_xattn_bo",
                 "lns": "L1_attn_ln_scale", "lnb": "L1_attn_ln_bias", "wh": "L1_attn_W_hidden", "bh": "L1_attn_b_hidden",
                 "wqk": "L1_attn_W_qk", "bqk": "L1_attn_b_qk", "wout": "L1_attn_W_out", "bout": "L1_attn_b_out"}.items():
        d[k] = np.asarray(i[v])
    for k, v in {"wqd": "L1_xattn_Wq", "wkd": "L1_xattn_Wk", "wvd": "L1_xattn_Wv", "wod": "L1_xattn_Wo",
                 "wgs": "L1_ffn_w_gate_shared", "wds": "L1_ffn_w_down_shared"}.items():
        d[k] = t(v)
    d["osw"], d["osb"] = np.asarray(i["L1_attn_os_weight"]), np.asarray(i["L1_attn_os_bias"])
    for k in ("bqd", "bkd", "bqk", "osw", "osb"):
        d[k] = c(d[k].reshape(-1, P).T)
    d["wr"], d["be"] = t("L1_ffn_router_w"), np.asarray(i["L1_ffn_expert_bias"])
    gate = np.asarray(i["L1_ffn_w_gate"]).reshape(EXPERTS, INTER, 2, P).transpose(0, 3, 2, 1).reshape(EXPERTS, P, 2 * INTER)
    down = np.asarray(i["L1_ffn_w_down"]).transpose(0, 2, 1)
    d["wexp"] = np.concatenate([gate, down], axis=2)
    d.update(constants())
    return d


def kernel(**inputs):
    import concourse.bacc as bacc
    from concourse.bass_utils import run_bass_kernel_spmd

    arrays = lay_out(inputs)
    plan = {}
    for _ in range(2):
        nc = bacc.Bacc("TRN2", target_bir_lowering=False, num_devices=1)
        a = {n: nc.dram_tensor(f"in_{n}", v.shape, mybir.dt.from_np(v.dtype), kind="ExternalInput").ap() for n, v in arrays.items()}
        out = nc.dram_tensor("out", (TOKENS, DIM), F32, kind="ExternalOutput").ap()
        program(nc, a, out, plan)
    r = run_bass_kernel_spmd(nc, [{f"in_{n}": v for n, v in arrays.items()}], core_ids=[0])
    return r.results[0]["out"].reshape(BATCHES, SEQ, DIM)
```
